# Optimizing a Trainium2 kernel written in Bass

```python
import numpy as np
import jax
import jax.numpy as jnp

def _softmax(x, axis=-1):
    return jax.nn.softmax(x, axis=axis)

def _gelu(x):
    return jax.nn.gelu(x, approximate=True)

def _silu(x):
    return jax.nn.silu(x)

def _sigmoid(x):
    return jax.nn.sigmoid(x)

def _layernorm(x, axis=-1, eps=1e-05):
    m = jnp.mean(x, axis=axis, keepdims=True)
    v = jnp.var(x, axis=axis, keepdims=True)
    return (x - m) / jnp.sqrt(v + eps)

def _scatter_add(tgt, idx, src, axis=0):
    return tgt.at[idx].add(src)

def _segment_sum(src, seg, n):
    return jax.ops.segment_sum(src, seg, n)
kernel_name = 'mk_adaln_d2_jaxref_r8_ab4df4'

def setup_inputs(seed: int=0):
    np.random.seed(seed)
    _w = jnp.asarray

    def _L0_attn_setup():
        import jax, jax.numpy as jnp
        import numpy as np
        CHUNK = 16

        def _ssm(xp, Wx, Wdt, bdt, A_log, Dp):
            B, L, D = xp.shape
            N = A_log.shape[1]
            dt_rank = Wdt.shape[1]
            x_dbl = xp @ Wx.T
            dlt, Bp, Cp = jnp.split(x_dbl, [dt_rank, dt_rank + N], axis=-1)
            delta = jax.nn.softplus(dlt @ Wdt.T + bdt)
            A = -jnp.exp(A_log)
            nc = L // CHUNK
            rs = lambda t: t.reshape(B, nc, CHUNK, t.shape[-1]).transpose(1, 0, 2, 3)
            d_c, B_c, C_c, x_c = (rs(delta), rs(Bp), rs(Cp), rs(xp))
            h0 = jnp.zeros((B, D, N), xp.dtype)

            def step(h, inp):
                dck, Bck, Cck, xck = inp
                dA = jnp.exp(dck[..., None] * A)
                b = dck[..., None] * Bck[:, :, None, :] * xck[..., None]
                cp = jnp.cumprod(dA, axis=1)
                free = jnp.cumsum(b / cp, axis=1)
                y = jnp.einsum('bkn,bkdn,bkdn->bkd', Cck, cp, h[:, None] + free)
                h_new = cp[:, -1] * (h + free[:, -1])
                return (h_new, y)
            _, ys = jax.lax.scan(step, h0, (d_c, B_c, C_c, x_c))
            y = ys.transpose(1, 0, 2, 3).reshape(B, L, D)
            return y + xp * Dp
        key = jax.random.key(seed)
        ks = jax.random.split(key, 8)
        B, L, d_model = (2, 512, 128)
        d_state, d_conv, expand = (16, 4, 2)
        d_inner = expand * d_model
        dt_rank = 64
        s = lambda fan: 1.0 / np.sqrt(fan)
        x = jax.random.normal(ks[0], (B, L, d_model), jnp.float32)
        Wi = jax.random.normal(ks[1], (2 * d_inner, d_model), jnp.float32) * s(d_model)
        conv_w = jax.random.normal(ks[2], (d_inner, 1, d_conv), jnp.float32) * s(d_conv)
        conv_b = jax.random.normal(ks[3], (d_inner,), jnp.float32) * 0.01
        Wx = jax.random.normal(ks[4], (dt_rank + 2 * d_state, d_inner), jnp.float32) * s(d_inner)
        Wdt = jax.random.normal(ks[5], (d_inner, dt_rank), jnp.float32) * 0.01
        dt = jnp.exp(jax.random.uniform(ks[6], (d_inner,), jnp.float32) * (np.log(0.1) - np.log(0.001)) + np.log(0.001))
        dt = jnp.clip(dt, 0.0001)
        bdt = dt + jnp.log(-jnp.expm1(-dt))
        A_log = jnp.log(jnp.tile(jnp.arange(1, d_state + 1, dtype=jnp.float32), (d_inner, 1)))
        Dp = jnp.ones((d_inner,), jnp.float32)
        Wo = jax.random.normal(ks[7], (d_model, d_inner), jnp.float32) * s(d_inner)
        return dict(x=x, Wi=Wi, conv_w=conv_w, conv_b=conv_b, Wx=Wx, Wdt=Wdt, bdt=bdt, A_log=A_log, Dp=Dp, Wo=Wo)
    _L0_attn_in = _L0_attn_setup()

    def _L0_ffn_setup():
        import jax, jax.numpy as jnp
        import numpy as np
        JITTER_EPS = 0.01
        NEG_INF = -jnp.inf

        def sparsemixer_eval(scores, jitter_eps):
            m1 = jnp.max(scores, axis=-1, keepdims=True)
            ind1 = jnp.argmax(scores, axis=-1)
            factor1 = jnp.maximum(jnp.abs(scores), m1)
            mask1 = jax.lax.stop_gradient((m1 - scores) / factor1 > 2.0 * jitter_eps)
            gates1 = jax.nn.softmax(jnp.where(mask1, NEG_INF, scores), axis=-1)
            mult1 = jnp.take_along_axis(gates1, ind1[:, None], axis=-1)[:, 0]
            E = scores.shape[-1]
            onehot1 = ind1[:, None] == jnp.arange(E)[None, :]
            masked_scores = jnp.where(onehot1, NEG_INF, scores)
            m2 = jnp.max(masked_scores, axis=-1, keepdims=True)
            ind2 = jnp.argmax(masked_scores, axis=-1)
            factor2 = jnp.maximum(jnp.abs(scores), m2)
            mask2 = jax.lax.stop_gradient((m2 - scores) / factor2 > 2.0 * jitter_eps)
            gates2 = jax.nn.softmax(jnp.where(mask2, NEG_INF, masked_scores), axis=-1)
            mult2 = jnp.take_along_axis(gates2, ind2[:, None], axis=-1)[:, 0]
            multiplier = jnp.stack([mult1, mult2], axis=-1)
            selected = jnp.stack([ind1, ind2], axis=-1)
            return (multiplier, selected)
        key = jax.random.key(seed)
        k0, k1, k2, k3, k4 = jax.random.split(key, 5)
        B, S, H, F, E = (2, 128, 128, 256, 8)
        scale = 0.02
        return {'hidden_states': jax.random.normal(k0, (B, S, H), dtype=jnp.float32), 'router_w': jax.random.normal(k1, (E, H), dtype=jnp.float32) * scale, 'w_gate': jax.random.normal(k2, (E, F, H), dtype=jnp.float32) * scale, 'w_up': jax.random.normal(k3, (E, F, H), dtype=jnp.float32) * scale, 'w_down': jax.random.normal(k4, (E, H, F), dtype=jnp.float32) * scale}
    _L0_ffn_in = _L0_ffn_setup()
    _L0_c = _w((lambda *s: np.random.randn(*s).astype(np.float32) * 0.05)(4, 128))
    _L0_wmod = _w((lambda *s: np.random.randn(*s).astype(np.float32) * 0.05)(128, 6 * 128) * 128 ** (-0.5))

    def _L1_attn_setup():
        import jax, jax.numpy as jnp
        import numpy as np
        D_MODEL = 128
        D_STATE = 128
        D_CONV = 4
        EXPAND = 2
        HEADDIM = 64
        D_INNER = EXPAND * D_MODEL
        NHEADS = D_INNER // HEADDIM
        NGROUPS = 1
        CONV_DIM = D_INNER + 2 * NGROUPS * D_STATE
        D_IN_PROJ = 2 * D_INNER + 2 * NGROUPS * D_STATE + NHEADS
        CHUNK = 64
        BATCH, SEQLEN = (4, 256)
        EPS = 1e-05

        def _segsum_exp(x):
            T = x.shape[-1]
            cs = jnp.cumsum(x, axis=-1)
            seg = cs[..., :, None] - cs[..., None, :]
            mask = jnp.tril(jnp.ones((T, T), dtype=bool))
            return jnp.where(mask, jnp.exp(jnp.where(mask, seg, 0.0)), 0.0)

        def _causal_conv(x, w, b):
            xt = jnp.transpose(x, (0, 2, 1))
            out = jax.lax.conv_general_dilated(xt, w[:, None, :], (1,), [(w.shape[-1] - 1, 0)], dimension_numbers=('NCH', 'OIH', 'NCH'), feature_group_count=w.shape[0])
            return jnp.transpose(out, (0, 2, 1)) + b

        def _ssd(X, A, B, C):
            b, l, h, p = X.shape
            c, Q = (l // CHUNK, CHUNK)
            X = X.reshape(b, c, Q, h, p)
            A = jnp.transpose(A.reshape(b, c, Q, h), (0, 3, 1, 2))
            B = B.reshape(b, c, Q, -1)
            C = C.reshape(b, c, Q, -1)
            A_cum = jnp.cumsum(A, axis=-1)
            L = _segsum_exp(A)
            Y_diag = jnp.einsum('bcln,bcsn,bhcls,bcshp->bclhp', C, B, L, X)
            decay_states = jnp.exp(A_cum[..., -1:] - A_cum)
            states = jnp.einsum('bcln,bhcl,bclhp->bchpn', B, decay_states, X)
            A_sum = jnp.pad(A_cum[..., -1], ((0, 0), (0, 0), (1, 0)))
            decay_chunk = _segsum_exp(A_sum)
            states = jnp.concatenate([jnp.zeros_like(states[:, :1]), states], axis=1)
            prev = jnp.einsum('bhzc,bchpn->bzhpn', decay_chunk, states)[:, :-1]
            Y_off = jnp.einsum('bcln,bchpn,bhcl->bclhp', C, prev, jnp.exp(A_cum))
            return (Y_diag + Y_off).reshape(b, l, h, p)
        key = jax.random.key(seed)
        ks = jax.random.split(key, 8)
        return {'hidden_states': jax.random.normal(ks[0], (BATCH, SEQLEN, D_MODEL), jnp.float32), 'W_in': jax.random.normal(ks[1], (D_MODEL, D_IN_PROJ), jnp.float32) * D_MODEL ** (-0.5), 'conv_w': jax.random.normal(ks[2], (CONV_DIM, D_CONV), jnp.float32) * 0.2, 'conv_b': jnp.zeros((CONV_DIM,), jnp.float32), 'dt_bias': jax.random.normal(ks[3], (NHEADS,), jnp.float32) * 0.1, 'A_log': jnp.log(jnp.arange(1, NHEADS + 1, dtype=jnp.float32)), 'D': jnp.ones((NHEADS,), jnp.float32), 'rms_w': jnp.ones((D_INNER,), jnp.float32), 'W_out': jax.random.normal(ks[4], (D_INNER, D_MODEL), jnp.float32) * D_INNER ** (-0.5), 'ln_g': jnp.ones((D_MODEL,), jnp.float32), 'ln_b': jnp.zeros((D_MODEL,), jnp.float32)}
    _L1_attn_in = _L1_attn_setup()

    def _L1_ffn_setup():
        import jax, jax.numpy as jnp
        import numpy as np
        D_MODEL = 128
        D_FF = 512
        NUM_EXPERTS = 8
        key = jax.random.key(seed)
        ks = jax.random.split(key, 8)
        scale_in = 1.0 / np.sqrt(D_MODEL)
        scale_ff = 1.0 / np.sqrt(D_FF)
        x = jax.random.normal(ks[0], (4, 256, D_MODEL), dtype=jnp.float32)
        gate_w = jax.random.uniform(ks[1], (NUM_EXPERTS, D_MODEL), jnp.float32, -scale_in, scale_in)
        gate_b = jax.random.uniform(ks[2], (NUM_EXPERTS,), jnp.float32, -scale_in, scale_in)
        expert_bias = jnp.zeros((NUM_EXPERTS,), dtype=jnp.float32)
        w1 = jax.random.uniform(ks[3], (NUM_EXPERTS, D_MODEL, D_FF), jnp.float32, -scale_in, scale_in)
        b1 = jax.random.uniform(ks[4], (NUM_EXPERTS, D_FF), jnp.float32, -scale_in, scale_in)
        w2 = jax.random.uniform(ks[5], (NUM_EXPERTS, D_FF, D_MODEL), jnp.float32, -scale_ff, scale_ff)
        b2 = jax.random.uniform(ks[6], (NUM_EXPERTS, D_MODEL), jnp.float32, -scale_ff, scale_ff)
        return {'x': x, 'gate_w': gate_w, 'gate_b': gate_b, 'expert_bias': expert_bias, 'w1': w1, 'b1': b1, 'w2': w2, 'b2': b2}
    _L1_ffn_in = _L1_ffn_setup()
    _L1_c = _w((lambda *s: np.random.randn(*s).astype(np.float32) * 0.05)(4, 128))
    _L1_wmod = _w((lambda *s: np.random.randn(*s).astype(np.float32) * 0.05)(128, 6 * 128) * 128 ** (-0.5))
    _d = {'L0_attn_x': _L0_attn_in['x'], 'L0_attn_Wi': _L0_attn_in['Wi'], 'L0_attn_conv_w': _L0_attn_in['conv_w'], 'L0_attn_conv_b': _L0_attn_in['conv_b'], 'L0_attn_Wx': _L0_attn_in['Wx'], 'L0_attn_Wdt': _L0_attn_in['Wdt'], 'L0_attn_bdt': _L0_attn_in['bdt'], 'L0_attn_A_log': _L0_attn_in['A_log'], 'L0_attn_Dp': _L0_attn_in['Dp'], 'L0_attn_Wo': _L0_attn_in['Wo'], 'L0_ffn_router_w': _L0_ffn_in['router_w'], 'L0_ffn_w_gate': _L0_ffn_in['w_gate'], 'L0_ffn_w_up': _L0_ffn_in['w_up'], 'L0_ffn_w_down': _L0_ffn_in['w_down'], 'L0_c': _L0_c, 'L0_wmod': _L0_wmod, 'L1_attn_W_in': _L1_attn_in['W_in'], 'L1_attn_conv_w': _L1_attn_in['conv_w'], 'L1_attn_conv_b': _L1_attn_in['conv_b'], 'L1_attn_dt_bias': _L1_attn_in['dt_bias'], 'L1_attn_A_log': _L1_attn_in['A_log'], 'L1_attn_D': _L1_attn_in['D'], 'L1_attn_rms_w': _L1_attn_in['rms_w'], 'L1_attn_W_out': _L1_attn_in['W_out'], 'L1_attn_ln_g': _L1_attn_in['ln_g'], 'L1_attn_ln_b': _L1_attn_in['ln_b'], 'L1_ffn_gate_w': _L1_ffn_in['gate_w'], 'L1_ffn_gate_b': _L1_ffn_in['gate_b'], 'L1_ffn_expert_bias': _L1_ffn_in['expert_bias'], 'L1_ffn_w1': _L1_ffn_in['w1'], 'L1_ffn_b1': _L1_ffn_in['b1'], 'L1_ffn_w2': _L1_ffn_in['w2'], 'L1_ffn_b2': _L1_ffn_in['b2'], 'L1_c': _L1_c, 'L1_wmod': _L1_wmod}
    _x0 = _d['L0_attn_x']
    _d['L0_attn_x'] = jax.random.normal(jax.random.fold_in(jax.random.key(seed), 1), (4, 1024, 128), dtype=_x0.dtype)
    del _x0
    return _d

def reference(L0_attn_x, L0_attn_Wi, L0_attn_conv_w, L0_attn_conv_b, L0_attn_Wx, L0_attn_Wdt, L0_attn_bdt, L0_attn_A_log, L0_attn_Dp, L0_attn_Wo, L0_ffn_router_w, L0_ffn_w_gate, L0_ffn_w_up, L0_ffn_w_down, L0_c, L0_wmod, L1_attn_W_in, L1_attn_conv_w, L1_attn_conv_b, L1_attn_dt_bias, L1_attn_A_log, L1_attn_D, L1_attn_rms_w, L1_attn_W_out, L1_attn_ln_g, L1_attn_ln_b, L1_ffn_gate_w, L1_ffn_gate_b, L1_ffn_expert_bias, L1_ffn_w1, L1_ffn_b1, L1_ffn_w2, L1_ffn_b2, L1_c, L1_wmod):

    def _L0_attn_ref(x, Wi, conv_w, conv_b, Wx, Wdt, bdt, A_log, Dp, Wo):
        import jax, jax.numpy as jnp
        import numpy as np
        CHUNK = 16

        def _ssm(xp, Wx, Wdt, bdt, A_log, Dp):
            B, L, D = xp.shape
            N = A_log.shape[1]
            dt_rank = Wdt.shape[1]
            x_dbl = xp @ Wx.T
            dlt, Bp, Cp = jnp.split(x_dbl, [dt_rank, dt_rank + N], axis=-1)
            delta = jax.nn.softplus(dlt @ Wdt.T + bdt)
            A = -jnp.exp(A_log)
            nc = L // CHUNK
            rs = lambda t: t.reshape(B, nc, CHUNK, t.shape[-1]).transpose(1, 0, 2, 3)
            d_c, B_c, C_c, x_c = (rs(delta), rs(Bp), rs(Cp), rs(xp))
            h0 = jnp.zeros((B, D, N), xp.dtype)

            def step(h, inp):
                dck, Bck, Cck, xck = inp
                dA = jnp.exp(dck[..., None] * A)
                b = dck[..., None] * Bck[:, :, None, :] * xck[..., None]
                cp = jnp.cumprod(dA, axis=1)
                free = jnp.cumsum(b / cp, axis=1)
                y = jnp.einsum('bkn,bkdn,bkdn->bkd', Cck, cp, h[:, None] + free)
                h_new = cp[:, -1] * (h + free[:, -1])
                return (h_new, y)
            _, ys = jax.lax.scan(step, h0, (d_c, B_c, C_c, x_c))
            y = ys.transpose(1, 0, 2, 3).reshape(B, L, D)
            return y + xp * Dp
        B, L, _ = x.shape
        d_inner = Wdt.shape[0]
        xz = x @ Wi.T
        xp, z = (xz[..., :d_inner], xz[..., d_inner:])
        k = conv_w.shape[-1]
        xc = xp.transpose(0, 2, 1)
        xc = jax.lax.conv_general_dilated(xc, conv_w, (1,), [(k - 1, 0)], feature_group_count=d_inner, dimension_numbers=('NCH', 'OIH', 'NCH')) + conv_b[None, :, None]
        xp = jax.nn.silu(xc.transpose(0, 2, 1))
        y = _ssm(xp, Wx, Wdt, bdt, A_log, Dp)
        return y * jax.nn.silu(z) @ Wo.T

    def _L0_ffn_ref(hidden_states, router_w, w_gate, w_up, w_down):
        import jax, jax.numpy as jnp
        import numpy as np
        JITTER_EPS = 0.01
        NEG_INF = -jnp.inf

        def sparsemixer_eval(scores, jitter_eps):
            m1 = jnp.max(scores, axis=-1, keepdims=True)
            ind1 = jnp.argmax(scores, axis=-1)
            factor1 = jnp.maximum(jnp.abs(scores), m1)
            mask1 = jax.lax.stop_gradient((m1 - scores) / factor1 > 2.0 * jitter_eps)
            gates1 = jax.nn.softmax(jnp.where(mask1, NEG_INF, scores), axis=-1)
            mult1 = jnp.take_along_axis(gates1, ind1[:, None], axis=-1)[:, 0]
            E = scores.shape[-1]
            onehot1 = ind1[:, None] == jnp.arange(E)[None, :]
            masked_scores = jnp.where(onehot1, NEG_INF, scores)
            m2 = jnp.max(masked_scores, axis=-1, keepdims=True)
            ind2 = jnp.argmax(masked_scores, axis=-1)
            factor2 = jnp.maximum(jnp.abs(scores), m2)
            mask2 = jax.lax.stop_gradient((m2 - scores) / factor2 > 2.0 * jitter_eps)
            gates2 = jax.nn.softmax(jnp.where(mask2, NEG_INF, masked_scores), axis=-1)
            mult2 = jnp.take_along_axis(gates2, ind2[:, None], axis=-1)[:, 0]
            multiplier = jnp.stack([mult1, mult2], axis=-1)
            selected = jnp.stack([ind1, ind2], axis=-1)
            return (multiplier, selected)
        B, S, H = hidden_states.shape
        E = router_w.shape[0]
        x = hidden_states.reshape(-1, H)
        T = x.shape[0]
        logits = x @ router_w.T
        routing_weights, selected = sparsemixer_eval(logits, JITTER_EPS)
        tok = jnp.arange(T)
        dense_w = jnp.zeros((T, E), dtype=x.dtype)
        dense_w = dense_w.at[tok, selected[:, 0]].add(routing_weights[:, 0])
        dense_w = dense_w.at[tok, selected[:, 1]].add(routing_weights[:, 1])
        out = jnp.zeros_like(x)
        for e in range(E):
            h = jax.nn.silu(x @ w_gate[e].T) * (x @ w_up[e].T)
            out = out + dense_w[:, e:e + 1] * (h @ w_down[e].T)
        return out.reshape(B, S, H)

    def _L1_attn_ref(hidden_states, W_in, conv_w, conv_b, dt_bias, A_log, D, rms_w, W_out, ln_g, ln_b):
        import jax, jax.numpy as jnp
        import numpy as np
        D_MODEL = 128
        D_STATE = 128
        D_CONV = 4
        EXPAND = 2
        HEADDIM = 64
        D_INNER = EXPAND * D_MODEL
        NHEADS = D_INNER // HEADDIM
        NGROUPS = 1
        CONV_DIM = D_INNER + 2 * NGROUPS * D_STATE
        D_IN_PROJ = 2 * D_INNER + 2 * NGROUPS * D_STATE + NHEADS
        CHUNK = 64
        BATCH, SEQLEN = (4, 256)
        EPS = 1e-05

        def _segsum_exp(x):
            T = x.shape[-1]
            cs = jnp.cumsum(x, axis=-1)
            seg = cs[..., :, None] - cs[..., None, :]
            mask = jnp.tril(jnp.ones((T, T), dtype=bool))
            return jnp.where(mask, jnp.exp(jnp.where(mask, seg, 0.0)), 0.0)

        def _causal_conv(x, w, b):
            xt = jnp.transpose(x, (0, 2, 1))
            out = jax.lax.conv_general_dilated(xt, w[:, None, :], (1,), [(w.shape[-1] - 1, 0)], dimension_numbers=('NCH', 'OIH', 'NCH'), feature_group_count=w.shape[0])
            return jnp.transpose(out, (0, 2, 1)) + b

        def _ssd(X, A, B, C):
            b, l, h, p = X.shape
            c, Q = (l // CHUNK, CHUNK)
            X = X.reshape(b, c, Q, h, p)
            A = jnp.transpose(A.reshape(b, c, Q, h), (0, 3, 1, 2))
            B = B.reshape(b, c, Q, -1)
            C = C.reshape(b, c, Q, -1)
            A_cum = jnp.cumsum(A, axis=-1)
            L = _segsum_exp(A)
            Y_diag = jnp.einsum('bcln,bcsn,bhcls,bcshp->bclhp', C, B, L, X)
            decay_states = jnp.exp(A_cum[..., -1:] - A_cum)
            states = jnp.einsum('bcln,bhcl,bclhp->bchpn', B, decay_states, X)
            A_sum = jnp.pad(A_cum[..., -1], ((0, 0), (0, 0), (1, 0)))
            decay_chunk = _segsum_exp(A_sum)
            states = jnp.concatenate([jnp.zeros_like(states[:, :1]), states], axis=1)
            prev = jnp.einsum('bhzc,bchpn->bzhpn', decay_chunk, states)[:, :-1]
            Y_off = jnp.einsum('bcln,bchpn,bhcl->bclhp', C, prev, jnp.exp(A_cum))
            return (Y_diag + Y_off).reshape(b, l, h, p)
        residual = hidden_states
        zxbcdt = hidden_states @ W_in
        z, xBC, dt = jnp.split(zxbcdt, [D_INNER, D_INNER + CONV_DIM], axis=-1)
        dt = jax.nn.softplus(dt + dt_bias)
        xBC = jax.nn.silu(_causal_conv(xBC, conv_w, conv_b))
        x, B, C = jnp.split(xBC, [D_INNER, D_INNER + NGROUPS * D_STATE], axis=-1)
        b, l, _ = x.shape
        x = x.reshape(b, l, NHEADS, HEADDIM)
        a = -jnp.exp(A_log)
        y = _ssd(x * dt[..., None], dt * a, B, C)
        y = y + x * D[None, None, :, None]
        y = y.reshape(b, l, D_INNER)
        y = y * jax.nn.silu(z)
        y = y * jax.lax.rsqrt(jnp.mean(y * y, axis=-1, keepdims=True) + EPS) * rms_w
        out = y @ W_out
        h = residual + out
        mu = jnp.mean(h, axis=-1, keepdims=True)
        var = jnp.mean((h - mu) ** 2, axis=-1, keepdims=True)
        return (h - mu) * jax.lax.rsqrt(var + EPS) * ln_g + ln_b

    def _L1_ffn_ref(x, gate_w, gate_b, expert_bias, w1, b1, w2, b2):
        import jax, jax.numpy as jnp
        import numpy as np
        D_MODEL = 128
        D_FF = 512
        NUM_EXPERTS = 8
        gate_logits = jnp.einsum('bsd,ed->bse', x, gate_w) + gate_b + expert_bias
        top_idx = jnp.argmax(gate_logits, axis=-1)
        out = jnp.zeros_like(x)
        for e in range(NUM_EXPERTS):
            mask = (top_idx == e)[..., None].astype(x.dtype)
            h = jax.nn.relu(jnp.einsum('bsd,df->bsf', x, w1[e]) + b1[e])
            y = jnp.einsum('bsf,fd->bsd', h, w2[e]) + b2[e]
            out = out + mask * y
        return out
    x = L0_attn_x
    mod = (_silu(L0_c) @ L0_wmod).reshape(L0_c.shape[0], 6, 1, -1)
    sa, ca, ga, sb, cb, gb = (mod[:, 0], mod[:, 1], mod[:, 2], mod[:, 3], mod[:, 4], mod[:, 5])
    ga = (2 * (ga >= 0) - 1) * jnp.maximum(jnp.abs(ga), 0.25)
    gb = (2 * (gb >= 0) - 1) * jnp.maximum(jnp.abs(gb), 0.25)
    h = _layernorm(x, axis=-1) * (1 + ca) + sa
    x = x + ga * _L0_attn_ref(h, L0_attn_Wi, L0_attn_conv_w, L0_attn_conv_b, L0_attn_Wx, L0_attn_Wdt, L0_attn_bdt, L0_attn_A_log, L0_attn_Dp, L0_attn_Wo)
    h = _layernorm(x, axis=-1) * (1 + cb) + sb
    x = x + gb * _L0_ffn_ref(h, L0_ffn_router_w, L0_ffn_w_gate, L0_ffn_w_up, L0_ffn_w_down)
    mod = (_silu(L1_c) @ L1_wmod).reshape(L1_c.shape[0], 6, 1, -1)
    sa, ca, ga, sb, cb, gb = (mod[:, 0], mod[:, 1], mod[:, 2], mod[:, 3], mod[:, 4], mod[:, 5])
    ga = (2 * (ga >= 0) - 1) * jnp.maximum(jnp.abs(ga), 0.25)
    gb = (2 * (gb >= 0) - 1) * jnp.maximum(jnp.abs(gb), 0.25)
    h = _layernorm(x, axis=-1) * (1 + ca) + sa
    x = x + ga * _L1_attn_ref(h, L1_attn_W_in, L1_attn_conv_w, L1_attn_conv_b, L1_attn_dt_bias, L1_attn_A_log, L1_attn_D, L1_attn_rms_w, L1_attn_W_out, L1_attn_ln_g, L1_attn_ln_b)
    h = _layernorm(x, axis=-1) * (1 + cb) + sb
    x = x + gb * _L1_ffn_ref(h, L1_ffn_gate_w, L1_ffn_gate_b, L1_ffn_expert_bias, L1_ffn_w1, L1_ffn_b1, L1_ffn_w2, L1_ffn_b2)
    return x

_drawn_inputs = setup_inputs


def setup_inputs(seed=0):
    import zlib

    import numpy as np

    out = dict(_drawn_inputs(seed))
    spreads = {'L0_attn_Dp': (1.0, 0.2),
     'L1_attn_conv_b': (0.0, 0.1),
     'L1_attn_D': (1.0, 0.2),
     'L1_attn_rms_w': (1.0, 0.2),
     'L1_attn_ln_g': (1.0, 0.2),
     'L1_attn_ln_b': (0.0, 0.1),
     'L1_ffn_expert_bias': (0.0, 0.1)}
    factors = {}
    for name, (base, spread) in spreads.items():
        noise = np.random.default_rng([zlib.crc32(name.encode()), seed]).standard_normal(out[name].shape)
        drawn = base * np.exp(spread * noise) if base else spread * noise
        out[name] = jnp.asarray(drawn.astype(out[name].dtype))
    for name, factor in factors.items():
        out[name] = (out[name] * factor).astype(out[name].dtype)
    return out
```

```python
from contextlib import ExitStack

import concourse.bass as bass
from concourse import mybir

ALU = mybir.AluOpType
ACT = mybir.ActivationFunctionType
F32 = mybir.dt.float32
BF16 = mybir.dt.bfloat16
AX = mybir.AxisListType.X

P = 128
NBATCH = 4
SEQ = 1024
TOKENS = NBATCH * SEQ
TILES = TOKENS // P
BT = SEQ // P
COL = 512
NCOL = SEQ // COL
TAPS = 4
PAD = TAPS - 1
EPS = 1e-5

D_IN = 256
HALVES = D_IN // P
N0 = 16
RANK = 64
F0 = 256
NE = 8
D_STATE = 128
HEADS = 4
HD = D_IN // HEADS
F1 = 512


class Memory:
    pass


ONE = 1
NORM_SEMS = "s_stats s_chain s_std s_xn s_tr s_h"
MAMBA_SEMS = ("pre_done pre_read low_done low_read split_done split_step parts_done dmm_done sp_step ln_done "
              "relu_done delta_done u_done bc_done bc_read bu_done decay_done scan_done ch_done acc_done "
              "yg_done out_done gated x_done")
EXPERT_SEMS = "lg_done route_step exp_done act_done mul_done down_done acc_done x_done routed up_done"
SSD_SEMS = ("proj_done proj_read dt_done dt_step dt_ready dtt_done dtt_read dA_done cs_done tr_done "
                 "csc_done seg_done dec_done cdec_done lastx_done gm_done m_done cts_done xdt_done xdd_done bt_done "
                 "y_done st_done s_done s_step yd_done yg_done yq_done o_done o_read h_done dtl_done last_done oc_done fin "
                 "sq_done zero_done tail_step h_step")


def setup(nc, a, m):
    with ExitStack() as ctx:
        sb = lambda name, shape, dt=F32: ctx.enter_context(nc.sbuf_tensor("su_" + name, shape, dt))
        sem = lambda name: m.kept.enter_context(nc.semaphore("su_" + name))
        ps = ctx.enter_context(nc.psum_tensor("ps_setup", [P, 8, COL], F32))
        cw0 = sb("cw0", [P, TAPS, D_IN])
        cw1 = sb("cw1", [P, TAPS, COL])
        wmod = sb("wmod", [P, 2, 6 * P])
        win0 = sb("win0", [P, D_IN])
        win1 = sb("win1", [P, COL])
        wout_raw = sb("wout_raw", [P, HALVES, P])
        cT = sb("cT", [P, 2, NBATCH])
        scT = sb("scT", [P, 2, NBATCH])
        sig = sb("sig", [P, 2, NBATCH])
        alog0 = sb("alog0", [P, HALVES, N0])
        alog1 = sb("alog1", [P, HEADS])
        dp0 = sb("dp0", [P, HALVES])
        rms = sb("rms", [P, HALVES])
        gsign = sb("gsign", [P, 2, 2, NBATCH, P])
        gate_raw = sb("gate_raw", [P, 2, 2, NBATCH, P])
        small, big, s_silu, s_modT, s_modB, s_v, s_exp = (
            sem(n) for n in ("small", "big", "s_silu", "s_modT", "s_modB", "s_v", "s_exp"))
        s_abs = sem("s_abs")
        block = ctx.enter_context(nc.Block())
        n_small, n_big = [0], [0]

        @block.sync
        def _(sp):
            def load(dst, src, s=small, n=n_small):
                sp.dma_start(dst, src).then_inc(s, 16)
                n[0] += 1
            for l, name in ((0, "L0"), (1, "L1")):
                load(cT[:, l, :], a[name + "_cT"])
                load(wmod[:, l, :], a[name + "_wmod"])
            load(m.ident[:], a["ident"])
            load(m.tri[:], a["tri"])
            load(m.pick[:], a["pick"])
            load(m.expert_no[:], a["expert_no"][0].partition_broadcast(P))
            load(m.onesrow[:], a["onesrow"])
            load(cw0[:], a["L0_conv_row"].partition_broadcast(P))
            load(cw1[:], a["L1_conv_row"].partition_broadcast(P))
            load(win0[:], a["L0_WiT"][:, 0:D_IN])
            load(m.wz0[:], a["L0_WiT"][:, D_IN:2 * D_IN])
            load(win1[:], a["L1_attn_W_in"][:, D_IN:D_IN + COL])
            load(m.wz1[:], a["L1_attn_W_in"][:, 0:D_IN])
            load(m.wdt1[:], a["L1_attn_W_in"][:, D_IN + COL:D_IN + COL + HEADS])
            load(m.wx[:], a["L0_WxT"].rearrange("(j p) n -> p j n", p=P))
            load(m.wdt0[:], a["L0_WdtT"])
            load(m.wo0[:], a["L0_WoT"].rearrange("(j p) n -> p j n", p=P))
            load(wout_raw[:], a["L1_attn_W_out"].rearrange("(j p) n -> p j n", p=P))
            load(m.cb0[:], a["cb0"])
            load(m.cb1[:], a["cb1"])
            load(m.bdt0[:], a["bdt0"])
            load(dp0[:], a["dp0"])
            load(rms[:], a["rms"])
            load(alog0[:], a["L0_attn_A_log"].rearrange("(j p) n -> p j n", p=P))
            load(alog1[:], a["L1_attn_A_log"].partition_broadcast(P))
            load(m.dtb1[:], a["L1_attn_dt_bias"].rearrange("(h o) -> h o", o=1))
            for j in range(HALVES):
                for q in range(P // HD):
                    load(m.d1[q * HD:(q + 1) * HD, j:j + 1],
                         a["L1_attn_D"][2 * j + q:2 * j + q + 1].partition_broadcast(HD))
            load(m.lng[:], a["L1_attn_ln_g"].partition_broadcast(P))
            load(m.lnb[:], a["L1_attn_ln_b"].partition_broadcast(P))
            load(m.gb1[:, 0, :], a["L1_ffn_gate_b"].partition_broadcast(P))
            load(m.gb1[:, 1, :], a["L1_ffn_expert_bias"].partition_broadcast(P))
            load(m.X[:], a["L0_attn_x"].rearrange("b (j p) d -> p (b j) d", p=P), big, n_big)
            load(m.router[:], a["router_T"], big, n_big)
            load(m.wgate[:], a["w_gate_T"].rearrange("e k f -> k e f"), big, n_big)
            load(m.wup[:], a["w_up_T"].rearrange("e k f -> k e f"), big, n_big)
            load(m.wdown[:], a["w_down_T"].rearrange("e (j p) d -> p e j d", p=P), big, n_big)
            load(m.gate1[:], a["gate_T"], big, n_big)
            load(m.b1[:], a["b1"], big, n_big)
            load(m.b2[:], a["L1_ffn_b2"], big, n_big)
            for semaphore in m.sems.values():
                sp.sem_inc(semaphore, ONE)
            sp.wait_ge(big, 16 * n_big[0])

        @block.scalar
        def _(act):
            act.wait_ge(small, 16 * n_small[0])
            act.activation(scT[:], cT[:], ACT.Silu).then_inc(s_silu, 1)
            act.activation(m.negA0[:], alog0[:], ACT.Exp).then_inc(s_exp, 1)
            act.activation(m.negA1[:], alog1[:], ACT.Exp).then_inc(s_exp, 1)
            act.wait_ge(s_modB, 16)
            for l in range(2):
                for g in range(2):
                    src = ps[:, 2 * (2 * l + g), 0:NBATCH * P].rearrange("p (b d) -> p b d", b=NBATCH)
                    act.activation(gate_raw[:, l, g], src, ACT.Abs).then_inc(s_abs, 1)

        @block.tensor
        def _(pe):
            pe.wait_ge(s_silu, 1)
            for l in range(2):
                for j in range(6):
                    mm = pe.matmul(ps[:, 1, (6 * l + j) * NBATCH:(6 * l + j + 1) * NBATCH],
                                   wmod[:, l, j * P:(j + 1) * P], scT[:, l, :], start=True, stop=True)
            mm.then_inc(s_modT, 1)
            for l in range(2):
                for g in range(2):
                    for b in range(NBATCH):
                        pe.matmul(ps[:, 2 * (2 * l + g), b * P:(b + 1) * P],
                                  scT[:, l, b:b + 1].broadcast_to([P, P]),
                                  wmod[:, l, (3 * g + 2) * P:(3 * g + 3) * P], start=True, stop=True
                                  ).then_inc(s_modB, 1)

        @block.vector
        def _(dve):
            steps = [0]

            def step(ins):
                steps[0] += 1
                ins.then_inc(s_v, 1)

            dve.wait_ge(small, 16 * n_small[0])
            for k in range(TAPS):
                step(dve.tensor_tensor(m.wc0[:, k, :], win0[:], cw0[:, k, :], ALU.mult))
                step(dve.tensor_tensor(m.wc1[:, k, :], win1[:], cw1[:, k, :], ALU.mult))
            for j in range(HALVES):
                step(dve.tensor_scalar(m.wout1[:, j, :], wout_raw[:, j, :], rms[:, j:j + 1], None, ALU.mult))
                step(dve.tensor_scalar(m.diagD0[:, j, :], m.ident[:], dp0[:, j:j + 1], None, ALU.mult))
            step(dve.memset(m.hT[:, :, 0:PAD], 0.0))
            step(dve.memset(m.ones[:], 1.0))
            step(dve.tensor_tensor(m.gb1[:, 0, :], m.gb1[:, 0, :], m.gb1[:, 1, :], ALU.add))
            dve.wait_ge(s_exp, 2)
            step(dve.tensor_scalar(m.negA0[:], m.negA0[:], -1.0, None, ALU.mult))
            step(dve.tensor_scalar(m.negA1[:], m.negA1[:], -1.0, None, ALU.mult))
            dve.wait_ge(s_modT, 1)
            modT = ps[:, 1, 0:12 * NBATCH].rearrange("p (l j b) -> p l j b", l=2, j=6)
            for l in range(2):
                for g in range(2):
                    step(dve.tensor_copy(m.shift[:, l, g, :], modT[:, l, 3 * g, :]))
                    step(dve.tensor_scalar(m.scale[:, l, g, :], modT[:, l, 3 * g + 1, :], 1.0, None, ALU.add))
            dve.wait_ge(s_modB, 16)
            dve.wait_ge(s_abs, 4)
            for l in range(2):
                for g in range(2):
                    src = ps[:, 2 * (2 * l + g), 0:NBATCH * P].rearrange("p (b d) -> p b d", b=NBATCH)
                    step(dve.tensor_scalar(gsign[:, l, g], src, 0.0, 2.0, ALU.is_ge, ALU.mult))
            for l in range(2):
                for g in range(2):
                    step(dve.tensor_scalar(gate_raw[:, l, g], gate_raw[:, l, g], 0.25, None, ALU.max))
            dve.wait_ge(s_v, steps[0])
            step(dve.scalar_tensor_tensor(m.gate[:], gsign[:], -1.0, gate_raw[:], ALU.add, ALU.mult))
            dve.wait_ge(s_v, steps[0])


def norm(nc, m, layer, sub):
    GROUP = 4
    GROUPS = TILES // GROUP
    with ExitStack() as ctx:
        sb = lambda name, shape, dt=F32: ctx.enter_context(nc.sbuf_tensor(f"n{layer}{sub}_" + name, shape, dt))
        sem = lambda name: m.sems[f"n{layer}{sub}_" + name]
        banks = [ctx.enter_context(nc.psum_tensor(f"n{layer}{sub}_ps{i}", [P, COL], F32)) for i in range(2)]
        stats = sb("stats", [P, TILES, 6])
        mean = sb("mean", [P, TILES])
        var = sb("var", [P, TILES])
        rstd = sb("rstd", [P, TILES])
        tmp = sb("tmp", [P, TILES])
        xn = [sb(f"xn{i}", [P, GROUP, P]) for i in range(2)]
        s_stats, s_chain, s_std, s_xn, s_tr, s_h = (
            sem(n) for n in NORM_SEMS.split())
        block = ctx.enter_context(nc.Block())

        @block.vector
        def _(dve):
            with dve.Fori(0, TILES) as t:
                dve.bn_stats(stats[:, bass.ds(t, 1), :], m.X[:, bass.ds(t, 1), :]).then_inc(s_stats, 1)
            dve.wait_ge(s_stats, ONE + TILES)
            half_e, half_o = stats[:, :, 1], stats[:, :, 4]
            dve.tensor_tensor(tmp[:], half_e, half_o, ALU.subtract).then_inc(s_chain, 1)
            dve.tensor_tensor(mean[:], half_e, half_o, ALU.add).then_inc(s_chain, 1)
            dve.tensor_tensor(var[:], stats[:, :, 2], stats[:, :, 5], ALU.add).then_inc(s_chain, 1)
            dve.wait_ge(s_chain, ONE + 3)
            dve.tensor_scalar(mean[:], mean[:], 0.5, None, ALU.mult).then_inc(s_chain, 1)
            dve.scalar_tensor_tensor(tmp[:], tmp[:], 0.25, tmp[:], ALU.mult, ALU.mult).then_inc(s_chain, 1)
            dve.wait_ge(s_chain, ONE + 5)
            dve.scalar_tensor_tensor(var[:], var[:], 1.0 / P, tmp[:], ALU.mult, ALU.add).then_inc(s_chain, 1)
            dve.wait_ge(s_chain, ONE + 6)
            dve.tensor_scalar(var[:], var[:], EPS, None, ALU.add).then_inc(s_chain, 1)
            dve.wait_ge(s_std, ONE + 1)
            dve.reciprocal(rstd[:], rstd[:]).then_inc(s_chain, 1)
            dve.wait_ge(s_chain, ONE + 8)
            with dve.Fori(0, GROUPS // 2) as i:
                for r in range(2):
                    dve.wait_ge(s_tr, ONE + i * 2 + r + 1)
                    for j in range(GROUP):
                        t = (i * 2 + r) * GROUP + j
                        dve.tensor_scalar(xn[r][:, j, :], m.X[:, bass.ds(t, 1), :], mean[:, bass.ds(t, 1)],
                                          rstd[:, bass.ds(t, 1)], ALU.subtract, ALU.mult).then_inc(s_xn, 1)

        @block.tensor
        def _(pe):
            pe.sem_inc(s_tr, 2)
            pe.wait_ge(s_h, ONE + 2)
            with pe.Fori(0, GROUPS // 2) as i:
                for r in range(2):
                    pe.wait_ge(s_xn, ONE + (i * 2 + r + 1) * GROUP)
                    pe.wait_ge(s_h, ONE + i * 2 + r + 1)
                    for j in range(GROUP):
                        tr = pe.transpose(banks[r][:, j * P:(j + 1) * P], xn[r][:, j, :], m.ident[:])
                    tr.then_inc(s_tr, 1)

        @block.scalar
        def _(act):
            act.sem_inc(s_h, 2)
            act.wait_ge(s_chain, ONE + 7)
            act.activation(rstd[:], var[:], ACT.Sqrt).then_inc(s_std, 1)
            with act.Fori(0, NBATCH) as b:
                for r in range(2):
                    act.wait_ge(s_tr, ONE + 2 + b * 2 + r + 1)
                    act.sem_inc(m.passed, 1)
                    act.activation(m.hT[:, bass.ds(b, 1), PAD + r * COL:PAD + (r + 1) * COL],
                                   banks[r][:].rearrange("p (o c) -> p o c", o=1), ACT.Identity,
                                   bias=m.shift[:, layer, sub, bass.ds(b, 1)],
                                   scale=m.scale[:, layer, sub, bass.ds(b, 1)]).then_inc(s_h, 1)
            act.wait_ge(s_h, ONE + 2 + GROUPS)


def mamba(nc, m):
    with ExitStack() as ctx:
        sb = lambda name, shape, dt=F32: ctx.enter_context(nc.sbuf_tensor("ma_" + name, shape, dt))
        sem = lambda name: m.sems["ma_" + name]
        bank = [ctx.enter_context(nc.psum_tensor(f"mps{i}", [P, COL], F32)) for i in range(2)]
        bc_ps = ctx.enter_context(nc.psum_tensor("bc_ps", [P, SEQ], F32))
        y_ps = [ctx.enter_context(nc.psum_tensor(f"y_ps{i}", [P, SEQ], F32)) for i in range(HALVES)]
        xp = [sb(f"xp{i}", [P, SEQ]) for i in range(HALVES)]
        sz = [sb(f"sz{i}", [P, SEQ]) for i in range(HALVES)]
        delta = [sb(f"delta{i}", [P, SEQ]) for i in range(HALVES)]
        u = [sb(f"u{i}", [P, SEQ]) for i in range(HALVES)]
        low = sb("low", [RANK, SEQ])
        G = 2 * N0
        parts = sb("parts", [3 * G, SEQ], BF16)
        hi = sb("hi", [3 * G, COL], BF16)
        mid = sb("mid", [3 * G, COL], BF16)
        rest = sb("rest", [3 * G, COL])
        bsb = [sb(f"bsb{i}", [P, SEQ]) for i in range(2)]
        csb = [sb(f"csb{i}", [P, SEQ]) for i in range(2)]
        SLOTS = 4
        bu = [sb(f"bu{i}", [P, SEQ]) for i in range(SLOTS)]
        h = [sb(f"h{i}", [P, SEQ]) for i in range(HALVES)]
        ch = [sb(f"ch{i}", [P, SEQ]) for i in range(SLOTS)]
        yg, ab, lt = bu, ch, h
        (pre_done, pre_read, low_done, low_read, split_done, split_step, parts_done, dmm_done, sp_step, ln_done,
         relu_done, delta_done, u_done, bc_done, bc_read, bu_done, decay_done, scan_done, ch_done, acc_done,
         yg_done, out_done, gated, x_done) = (sem(n) for n in MAMBA_SEMS.split())
        RING = 2
        SCANS = 6
        block = ctx.enter_context(nc.Block())
        NPRE = 2 * HALVES * NCOL
        col = lambda c: slice(c * COL, (c + 1) * COL)

        @block.tensor
        def _(pe):
            pe.sem_inc(acc_done, SLOTS)
            with pe.Fori(0, NBATCH) as b:
                pe.wait_ge(x_done, ONE + b * 2)
                for i in range(NPRE):
                    what, j, c = i // (HALVES * NCOL), i // NCOL % HALVES, i % NCOL
                    pe.wait_ge(pre_read, ONE + b * NPRE + i + 1)
                    if what == 0:
                        for k in range(TAPS):
                            mm = pe.matmul(bank[i % 2][:], m.wc0[:, k, j * P:(j + 1) * P],
                                           m.hT[:, bass.ds(b, 1), c * COL + k:c * COL + k + COL],
                                           start=(k == 0), stop=(k == TAPS - 1))
                    else:
                        mm = pe.matmul(bank[i % 2][:], m.wz0[:, j * P:(j + 1) * P],
                                       m.hT[:, bass.ds(b, 1), c * COL + PAD:c * COL + PAD + COL],
                                       start=True, stop=True)
                    mm.then_inc(pre_done, 1)
                pe.wait_ge(pre_read, ONE + b * NPRE + NPRE + RING)
                for c in range(NCOL):
                    for j in range(HALVES):
                        mm = pe.matmul(bank[c][0:RANK, :], m.wx[:, j, 0:RANK], xp[j][:, col(c)],
                                       start=(j == 0), stop=(j == 1))
                    mm.then_inc(low_done, 1)
                for c in range(NCOL):
                    for j in range(HALVES):
                        mm = pe.matmul(bc_ps[0:3 * G, col(c)], m.wx[:, j, RANK:RANK + 3 * G], xp[j][:, col(c)],
                                       start=(j == 0), stop=(j == 1))
                    mm.then_inc(split_done, 1)
                pe.wait_ge(low_read, ONE + b * NCOL + NCOL)
                for j in range(HALVES):
                    for c in range(NCOL):
                        mm = pe.matmul(y_ps[j][:, col(c)], m.wdt0[:, j * P:(j + 1) * P], low[:, col(c)],
                                       start=True, stop=True)
                    mm.then_inc(dmm_done, 1)
                for j in range(HALVES):
                    pe.wait_ge(sp_step, ONE + b * 4 + j + 1)
                    pe.wait_ge(relu_done, ONE + b * 2 + j + 1)
                    for c in range(NCOL):
                        pe.matmul(y_ps[j][:, col(c)], m.diagD0[:, j, :], xp[j][:, col(c)], start=True, stop=True)
                pe.wait_ge(parts_done, ONE + b * 6 + 6)

                def row(n, w):
                    for c in range(NCOL):
                        q = (b * N0 + n) * 4 + 2 * w + c
                        pe.wait_ge(bc_read, ONE + q + 1)
                        pe.matmul(bc_ps[:, col(c)], m.pick[:, bass.ds((n + w * N0) * P, P)], parts[:, col(c)],
                                  start=True, stop=True).then_inc(bc_done, 1)

                def add_state(n, r, j):
                    pe.wait_ge(ch_done, ONE + (b * N0 + n) * 2 + j + 1 + SLOTS)
                    for c in range(NCOL):
                        mm = pe.matmul(y_ps[j][:, col(c)], m.ident[:], ch[2 * r + j][:, col(c)], start=False,
                                       stop=True, skip_group_check=True)
                    mm.then_inc(acc_done, 1)

                for n in range(2):
                    for w in range(2):
                        row(n, w)
                with pe.Fori(0, N0 // 2 - 1) as i:
                    for r in range(2):
                        for w in range(2):
                            row(i * 2 + r + 2, w)
                            add_state(i * 2 + r, r, w)
                for r in range(2):
                    for j in range(HALVES):
                        add_state(N0 - 2 + r, r, j)
                pe.wait_ge(yg_done, ONE + b * 2 + 2)
                for q in range(NCOL):
                    for t in range(COL // P):
                        tok = slice(q * COL + t * P, q * COL + (t + 1) * P)
                        for j in range(HALVES):
                            mm = pe.matmul(bc_ps[:, tok], yg[j][:, tok], m.wo0[:, j, :], start=(j == 0), stop=(j == 1))
                    mm.then_inc(out_done, 1)

        @block.scalar
        def _(act):
            act.sem_inc(pre_read, RING)
            act.sem_inc(bc_read, RING)
            with act.Fori(0, NBATCH) as b:
                act.wait_ge(x_done, ONE + b * 2)
                for i in range(NPRE):
                    what, j, c = i // (HALVES * NCOL), i // NCOL % HALVES, i % NCOL
                    act.wait_ge(pre_done, ONE + b * NPRE + i + 1)
                    act.activation((xp, sz)[what][j][:, col(c)], bank[i % 2][:], ACT.Silu,
                                   bias=m.cb0[:, j:j + 1] if what == 0 else 0.0).then_inc(pre_read, 1)
                for j in range(HALVES):
                    act.wait_ge(dmm_done, ONE + b * 2 + j + 1)
                    act.activation(ab[j][:], y_ps[j][:], ACT.Abs, bias=m.bdt0[:, j:j + 1]).then_inc(sp_step, 1)
                for j in range(HALVES):
                    act.wait_ge(sp_step, ONE + b * 4 + j + 1)
                    act.activation(lt[j][:], ab[j][:], ACT.Exp, scale=-1.0).then_inc(sp_step, 1)
                for j in range(HALVES):
                    act.wait_ge(sp_step, ONE + b * 4 + j + 3)
                    act.activation(lt[j][:], lt[j][:], ACT.Ln, bias=1.0).then_inc(ln_done, 1)
                act.wait_ge(delta_done, ONE + b * 2 + 2)

                def read_row(n, r, w):
                    act.wait_ge((bu_done, ch_done)[w], ONE + (b * N0 + n) * 2 + 2)
                    for c in range(NCOL):
                        act.wait_ge(bc_done, ONE + (b * N0 + n) * 4 + 2 * w + c + 1)
                        act.activation((bsb, csb)[w][r][:, col(c)], bc_ps[:, col(c)], ACT.Copy
                                       ).then_inc(bc_read, 1)

                def decays(n, j):
                    for c in range(NCOL):
                        act.wait_ge(scan_done, ONE + (b * N0 + n) * 4 + 2 * j + c - 1 + SCANS)
                        act.sem_inc(m.passed, 1)
                        act.activation(bank[c][:], delta[j][:, col(c)], ACT.Exp,
                                       scale=m.negA0[:, j, bass.ds(n, 1)]).then_inc(decay_done, 1)

                def ahead(n, r):
                    for w in range(2):
                        read_row(n, r, w)
                        decays(n - 1, w)

                read_row(0, 0, 0)
                read_row(0, 0, 1)
                ahead(1, 1)
                with act.Fori(0, N0 // 2 - 1) as i:
                    for r in range(2):
                        ahead(i * 2 + r + 2, r)
                decays(N0 - 1, 0)
                decays(N0 - 1, 1)

        @block.gpsimd
        def _(pool):
            pool.sem_inc(bu_done, SLOTS)
            with pool.Fori(0, NBATCH) as b:
                for j in range(HALVES):
                    pool.wait_ge(ln_done, ONE + b * 2 + j + 1)
                    pool.wait_ge(relu_done, ONE + b * 2 + j + 1)
                    pool.tensor_tensor(delta[j][:], delta[j][:], lt[j][:], ALU.add).then_inc(delta_done, 1)
                    pool.wait_ge(delta_done, ONE + b * 2 + j + 1)
                    pool.tensor_tensor(u[j][:], delta[j][:], xp[j][:], ALU.mult).then_inc(u_done, 1)
                with pool.Fori(0, N0 // 2) as i:
                    pool.wait_ge(u_done, ONE + b * 2 + 2)
                    for r in range(2):
                        n = b * N0 + i * 2 + r
                        pool.wait_ge(bc_read, ONE + n * 4 + 2 + RING)
                        for j in range(HALVES):
                            pool.wait_ge(scan_done, ONE + n * 4 + 2 * j - 6 + SCANS)
                            pool.tensor_tensor(bu[2 * r + j][:], u[j][:], bsb[r][:], ALU.mult).then_inc(bu_done, 1)

        @block.vector
        def _(dve):
            dve.sem_inc(scan_done, SCANS)
            dve.sem_inc(ch_done, SLOTS)
            with dve.Fori(0, NBATCH) as b:
                for c in range(NCOL):
                    dve.wait_ge(low_done, ONE + b * 2 + c + 1)
                    dve.tensor_copy(low[:, col(c)], bank[c][0:RANK, :]).then_inc(low_read, 1)
                for j in range(HALVES):
                    dve.wait_ge(sp_step, ONE + b * 4 + j + 1)
                    dve.tensor_scalar(delta[j][:], y_ps[j][:], m.bdt0[:, j:j + 1], 0.0, ALU.add,
                                      ALU.max).then_inc(relu_done, 1)
                for c in range(NCOL):
                    k = b * 6 + 3 * c
                    dve.wait_ge(split_done, ONE + b * 2 + c + 1)
                    dve.tensor_copy(hi[:], bc_ps[0:3 * G, col(c)]).then_inc(split_step, 1)
                    dve.wait_ge(split_step, ONE + k + 1)
                    dve.tensor_tensor(rest[:], bc_ps[0:3 * G, col(c)], hi[:], ALU.subtract).then_inc(split_step, 1)
                    dve.tensor_copy(parts[0:G, col(c)], hi[0:G, :]).then_inc(parts_done, 1)
                    dve.wait_ge(split_step, ONE + k + 2)
                    dve.tensor_copy(mid[:], rest[:]).then_inc(split_step, 1)
                    dve.wait_ge(split_step, ONE + k + 3)
                    dve.tensor_copy(parts[G:2 * G, col(c)], mid[G:2 * G, :]).then_inc(parts_done, 1)
                    dve.tensor_tensor(parts[2 * G:3 * G, col(c)], rest[2 * G:3 * G, :], mid[2 * G:3 * G, :],
                                      ALU.subtract).then_inc(parts_done, 1)
                with dve.Fori(0, N0 // 2) as i:
                    for r in range(2):
                        n = b * N0 + i * 2 + r
                        for j in range(HALVES):
                            dve.wait_ge(bu_done, ONE + n * 2 + j + 1 + SLOTS)
                            for c in range(NCOL):
                                dve.wait_ge(decay_done, ONE + n * 4 + 2 * j + c + 1)
                                if c:
                                    dve.wait_ge(scan_done, ONE + n * 4 + 2 * j + c + SCANS)
                                dve.tensor_tensor_scan(h[j][:, col(c)], bank[c][:], bu[2 * r + j][:, col(c)],
                                                       h[j][:, c * COL - 1:c * COL] if c else 0.0,
                                                       ALU.mult, ALU.add).then_inc(scan_done, 1)
                            dve.wait_ge(scan_done, ONE + n * 4 + 2 * j + 2 + SCANS)
                            dve.wait_ge(bc_read, ONE + n * 4 + 4 + RING)
                            dve.wait_ge(acc_done, ONE + n * 2 + j - 3 + SLOTS)
                            dve.tensor_tensor(ch[2 * r + j][:], h[j][:], csb[r][:], ALU.mult).then_inc(ch_done, 1)
                dve.wait_ge(acc_done, ONE + b * (N0 * 2) + N0 * 2 + SLOTS)
                for j in range(HALVES):
                    dve.tensor_tensor(yg[j][:], y_ps[j][:], sz[j][:], ALU.mult).then_inc(yg_done, 1)
                for q in range(NCOL):
                    dve.wait_ge(out_done, ONE + b * 2 + q + 1)
                    src = bc_ps[:, col(q)].rearrange("p (t d) -> p t d", t=4)
                    tmp = ch[0][:, col(q)].rearrange("p (t d) -> p t d", t=4)
                    dve.tensor_tensor(tmp, src, m.gate[:, 0, 0, bass.ds(b, 1), :].broadcast_to([P, 4, P]),
                                      ALU.mult).then_inc(gated, 1)
                    dve.wait_ge(gated, ONE + b * 2 + q + 1)
                    xs = m.X[:, bass.ds(b * BT + 4 * q, 4), :]
                    dve.tensor_tensor(xs, xs, tmp, ALU.add).then_inc(x_done, 1)
            dve.wait_ge(x_done, ONE + 2 * NBATCH)


def experts(nc, a, m, layer):
    FB = (F0 if layer == 0 else F1) // P
    NA = 2 if layer == 0 else 4
    with ExitStack() as ctx:
        sb = lambda name, shape, dt=F32: ctx.enter_context(nc.sbuf_tensor(f"e{layer}_" + name, shape, dt))
        sem = lambda name: m.sems[f"e{layer}_" + name]
        up = [ctx.enter_context(nc.psum_tensor(f"e{layer}_up{i}", [P, COL], F32)) for i in range(4)]
        down = [ctx.enter_context(nc.psum_tensor(f"e{layer}_dn{i}", [P, COL], F32)) for i in range(2)]
        lg_ps = ctx.enter_context(nc.psum_tensor(f"e{layer}_lg_ps", [P, TILES * NE], F32))
        hb = [[sb(f"hb{i}_{j}", [P, COL]) for j in range(FB)] for i in range(2)]
        sg = [[sb(f"sg{i}_{j}", [P, COL]) for j in range(2)] for i in range(2)]
        acc = sb("acc", [P, 4, P])
        R = [P, TILES, NE]
        lg, w, onehot, keep, val, ex = (sb(n, R) for n in ("lg", "w", "onehot", "keep", "val", "ex"))
        mx, first, sm = (sb(n, [P, TILES]) for n in ("mx", "first", "sm"))
        (lg_done, route_step, exp_done, act_done, mul_done, down_done, acc_done, x_done, routed, up_done) = (
            sem(n) for n in EXPERT_SEMS.split())
        loaded = m.kept.enter_context(nc.semaphore(f"e{layer}_loaded"))
        sel1 = sb("sel1", R)
        RING = 2
        block = ctx.enter_context(nc.Block())
        router = m.router if layer == 0 else m.gate1
        over = lambda t: t[:].unsqueeze(2).broadcast_to(R)
        numbers = m.expert_no[:].unsqueeze(1).broadcast_to(R)

        @block.tensor
        def _(pe):
            for t in range(TILES):
                c0 = PAD + t % BT * P
                mm = pe.matmul(lg_ps[:, t * NE:(t + 1) * NE], m.hT[:, t // BT, c0:c0 + P], router[:],
                               start=True, stop=True)
            mm.then_inc(lg_done, 1)

            with pe.Fori(0, NBATCH) as b:
                for c in range(NCOL):
                    def widen(e):
                        v = (b * NCOL + c) * NE + e
                        for k in range(4):
                            if k < NA:
                                pe.wait_ge(act_done, ONE + v * NA + k + 1)
                            else:
                                pe.wait_ge(mul_done, ONE + v * 2 + k - NA + 1)
                            if layer == 0:
                                wt = (m.wgate if k < 2 else m.wup)[:, e, k % 2 * P:(k % 2 + 1) * P]
                            else:
                                wt = m.w1[:, e, k * P:(k + 1) * P]
                            mm = pe.matmul(up[k][:], wt, m.hT[:, bass.ds(b, 1), PAD + c * COL:PAD + (c + 1) * COL],
                                           start=True, stop=True)
                            mm.then_inc(up_done, 1)

                    def narrow(e):
                        v = (b * NCOL + c) * NE + e
                        if layer == 0:
                            pe.wait_ge(mul_done, ONE + v * 2 + 2 + RING)
                        else:
                            pe.wait_ge(act_done, ONE + v * 4 + 4 + 4)
                        pe.wait_ge(acc_done, ONE + v + 1)
                        for t in range(4):
                            tok = slice(t * P, (t + 1) * P)
                            if layer == 1:
                                pe.matmul(down[e % 2][:, tok], m.onesrow[:], m.b2[:, e * P:(e + 1) * P], start=True,
                                          stop=False)
                            for j in range(FB):
                                wt = (m.wdown if layer == 0 else m.w2)[:, e, j, :]
                                mm = pe.matmul(down[e % 2][:, tok], hb[e % 2][j][:, tok], wt,
                                               start=(layer == 0 and j == 0), stop=(j == FB - 1))
                        mm.then_inc(down_done, 1)

                    widen(0)
                    for e in range(1, NE):
                        widen(e)
                        narrow(e - 1)
                    narrow(NE - 1)

        @block.scalar
        def _(act):
            act.sem_inc(act_done, NA)
            if layer == 0:
                for k in range(2):
                    act.wait_ge(routed, ONE + k + 1)
                    act.activation(ex[:], val[:], ACT.Exp).then_inc(exp_done, 1)
            with act.Fori(0, NBATCH) as b:
                for c in range(NCOL):
                    for e in range(NE):
                        v = (b * NCOL + c) * NE + e
                        if layer == 0:
                            act.wait_ge(mul_done, ONE + v * 2)
                        else:
                            act.wait_ge(down_done, ONE + v + 1)
                        for k in range(NA):
                            act.wait_ge(up_done, ONE + v * 4 + k + 1)
                            if layer == 0:
                                act.activation(sg[e % 2][k][:], up[k][:], ACT.Silu).then_inc(act_done, 1)
                            else:
                                act.activation(hb[e % 2][k][:], up[k][:], ACT.Relu,
                                               bias=m.b1[:, e, k:k + 1]).then_inc(act_done, 1)

        @block.vector
        def _(dve):
            dve.sem_inc(mul_done, RING)
            dve.sem_inc(acc_done, RING)
            dve.sem_inc(down_done, RING)
            steps = [0]

            def then(ins):
                steps[0] += 1
                ins.then_inc(route_step, 1)
                dve.wait_ge(route_step, ONE + steps[0])

            def first_of_max(scores):
                then(dve.tensor_reduce(mx[:], scores[:], AX, ALU.max))
                then(dve.tensor_tensor(val[:], scores[:], over(mx), ALU.is_lt))
                then(dve.scalar_tensor_tensor(val[:], val[:], float(NE), numbers, ALU.mult, ALU.add))
                then(dve.tensor_reduce(first[:], val[:], AX, ALU.min))
                then(dve.tensor_tensor(onehot[:], numbers, over(first), ALU.is_equal))

            dve.wait_ge(lg_done, ONE + 1)
            lgv = lg_ps[:].rearrange("p (t e) -> p t e", t=TILES)
            if layer == 1:
                then(dve.tensor_tensor(lg[:], lgv, m.gb1[:, 0, :].unsqueeze(1).broadcast_to(R), ALU.add))
                first_of_max(lg)
                then(dve.tensor_copy(w[:], onehot[:]))
            else:
                then(dve.tensor_copy(lg[:], lgv))
                first_of_max(lg)
                masked = keep
                for k in range(2):
                    if k == 1:
                        then(dve.scalar_tensor_tensor(ex[:], onehot[:], -3.0e38, lg[:], ALU.mult, ALU.add))
                        then(dve.tensor_copy(sel1[:], onehot[:]))
                        first_of_max(ex)
                    then(dve.scalar_tensor_tensor(keep[:], lg[:], -1.0, lg[:], ALU.mult, ALU.max))
                    then(dve.tensor_tensor(keep[:], keep[:], over(mx), ALU.max))
                    then(dve.tensor_tensor(val[:], over(mx), lg[:], ALU.subtract))
                    then(dve.scalar_tensor_tensor(keep[:], keep[:], 0.02, val[:], ALU.mult, ALU.is_ge))
                    if k == 1:
                        then(dve.scalar_tensor_tensor(keep[:], sel1[:], 0.0, keep[:], ALU.is_equal, ALU.mult))
                    then(dve.tensor_scalar(val[:], val[:], -1.0, 0.0, ALU.mult, ALU.min))
                    dve.sem_inc(routed, 1)
                    dve.wait_ge(exp_done, ONE + k + 1)
                    then(dve.tensor_tensor(ex[:], ex[:], keep[:], ALU.mult))
                    then(dve.tensor_reduce(sm[:], ex[:], AX, ALU.add))
                    then(dve.reciprocal(sm[:], sm[:]))
                    if k == 0:
                        then(dve.tensor_tensor(w[:], onehot[:], over(sm), ALU.mult))
                    else:
                        then(dve.tensor_tensor(onehot[:], onehot[:], over(sm), ALU.mult))
                        then(dve.tensor_tensor(w[:], w[:], onehot[:], ALU.add))
            with dve.Fori(0, NBATCH) as b:
                for c in range(NCOL):
                    def products(e):
                        v = (b * NCOL + c) * NE + e
                        dve.wait_ge(act_done, ONE + v * 2 + 2 + NA)
                        dve.wait_ge(down_done, ONE + v + 1)
                        dve.wait_ge(up_done, ONE + v * 4 + 4)
                        for k in range(2):
                            dve.tensor_tensor(hb[e % 2][k][:], up[2 + k][:], sg[e % 2][k][:],
                                              ALU.mult).then_inc(mul_done, 1)

                    def gather(e):
                        v = (b * NCOL + c) * NE + e
                        dve.wait_ge(down_done, ONE + v + 1 + RING)
                        dve.wait_ge(acc_done, ONE + v + RING)
                        if e == 0:
                            dve.wait_ge(x_done, ONE + (b * NCOL + c) * 2)
                        for t in range(4):
                            tok = slice(t * P, (t + 1) * P)
                            we = w[:, bass.ds((b * NCOL + c) * 4 + t, 1), e]
                            if e == 0:
                                ins = dve.tensor_scalar(acc[:, t, :], down[e % 2][:, tok], we, None, ALU.mult)
                            else:
                                ins = dve.scalar_tensor_tensor(acc[:, t, :], down[e % 2][:, tok], we, acc[:, t, :],
                                                               ALU.mult, ALU.add)
                        ins.then_inc(acc_done, 1)

                    for e in range(NE):
                        if layer == 0:
                            products(e)
                        if e:
                            gather(e - 1)
                    gather(NE - 1)
                    g = b * NCOL + c
                    dve.wait_ge(acc_done, ONE + g * NE + NE + RING)
                    dve.tensor_tensor(acc[:], acc[:], m.gate[:, layer, 1, bass.ds(b, 1), :].broadcast_to([P, 4, P]),
                                      ALU.mult).then_inc(x_done, 1)
                    dve.wait_ge(x_done, ONE + g * 2 + 1)
                    xs = m.X[:, bass.ds(g * 4, 4), :]
                    dve.tensor_tensor(xs, xs, acc[:], ALU.add).then_inc(x_done, 1)

        @block.sync
        def _(sp):
            if layer == 0:
                sp.dma_start(m.w1[:], a["L1_ffn_w1"].rearrange("e k f -> k e f")).then_inc(loaded, 16)
                sp.dma_start(m.w2[:], a["L1_ffn_w2"].rearrange("e (j p) d -> p e j d", p=P)).then_inc(loaded, 16)
                sp.wait_ge(loaded, 32)
            else:
                for g in range(2 * NBATCH):
                    sp.wait_ge(x_done, ONE + g * 2 + 2)
                    sp.dma_start(m.out[g // 2, g % 2 * COL:(g % 2 + 1) * COL, :].rearrange("(t p) d -> p t d", p=P),
                                 m.X[:, g * 4:(g + 1) * 4, :]).then_inc(m.stored, 16)
                sp.wait_ge(m.stored, 16 * 2 * NBATCH)


def ssd(nc, m):
    with ExitStack() as ctx:
        sb = lambda name, shape, dt=F32: ctx.enter_context(nc.sbuf_tensor("ss_" + name, shape, dt))
        sem = lambda name: m.sems["ss_" + name]
        psum = lambda name: ctx.enter_context(nc.psum_tensor("ss_" + name, [P, COL], F32))
        pre = [psum("spre0"), psum("spre1")]
        cs_ps, tr_ps, st_ps, y_ps, o_ps, g_ps = (psum(n) for n in "cs_ps tr_ps st_ps y_ps o_ps g_ps".split())
        NB = COL // P
        xbc = [sb(f"xbc{i}", [P, SEQ]) for i in range(NB)]
        sz = [sb(f"ssz{i}", [P, SEQ]) for i in range(HALVES)]
        dtT, dte, dtl = (sb(n, [HEADS, SEQ]) for n in ("dtT", "dte", "dtl"))
        dt = sb("dt", [P, BT, HEADS])
        dA = sb("dA", [P, BT, HEADS])
        outs = sb("outs", [P, TILES, P])
        resid = sb("resid", [P, TILES, P])
        ss = sb("ss", [P, TILES])
        H4 = [P, HEADS, P]
        csc = sb("csc", [P, HEADS])
        seg, dec, cdec, mm_sb, cts = (sb(n, H4) for n in ("seg", "dec", "cdec", "mm_sb", "cts"))
        last, lastx = sb("last", [P, HEADS]), sb("lastx", [P, HEADS])
        gm, bt = sb("gm", [P, P]), sb("bt", [P, P])
        xdt, xdd = sb("xdt", [P, HEADS, HD]), sb("xdd", [P, HEADS, HD])
        S = [sb(f"S{i}", [P, HEADS, HD]) for i in range(2)]
        hcur = sb("hcur", [P, SEQ])
        stats = sb("stats", [P, TILES, 6])
        mean, var, tmp = (sb(n, [P, TILES]) for n in ("mean", "var", "tmp"))
        yv, yq = sb("yv", [P, HALVES, P]), sb("yq", [P, HALVES, P])
        (proj_done, proj_read, dt_done, dt_step, dt_ready, dtt_done, dtt_read, dA_done, cs_done, tr_done,
         csc_done, seg_done, dec_done, cdec_done, lastx_done, gm_done, m_done, cts_done, xdt_done, xdd_done,
         bt_done, y_done, st_done, s_done, s_step, yd_done, yg_done, yq_done, o_done, o_read, h_done,
         dtl_done, last_done, oc_done, fin, sq_done, zero_done, tail_step, h_step) = (sem(n) for n in SSD_SEMS.split())
        block = ctx.enter_context(nc.Block())
        NPRE = (NB + HALVES) * NCOL
        col = lambda c: slice(c * COL, (c + 1) * COL)
        tok = lambda t: slice(t * P, (t + 1) * P)
        four = lambda t: t.unsqueeze(1).broadcast_to(H4)

        @block.tensor
        def _(pe):
            with pe.Fori(0, NBATCH) as b:
                for i in range(NPRE):
                    j, c = i // NCOL, i % NCOL
                    if i < 2:
                        pe.wait_ge(dtt_read, ONE + b)
                    pe.wait_ge(proj_read, ONE + b * NPRE + i + 1)
                    if j < NB:
                        for k in range(TAPS):
                            mm = pe.matmul(pre[i % 2][:], m.wc1[:, k, j * P:(j + 1) * P],
                                           m.hT[:, bass.ds(b, 1), c * COL + k:c * COL + k + COL],
                                           start=(k == 0), stop=(k == TAPS - 1))
                    else:
                        mm = pe.matmul(pre[i % 2][:], m.wz1[:, (j - NB) * P:(j - NB + 1) * P],
                                       m.hT[:, bass.ds(b, 1), c * COL + PAD:c * COL + PAD + COL],
                                       start=True, stop=True)
                    mm.then_inc(proj_done, 1)
                pe.wait_ge(proj_read, ONE + b * NPRE + NPRE + 2)
                pe.sem_inc(m.passed, 1)
                for c in range(NCOL):
                    mm = pe.matmul(pre[c][0:HEADS, :], m.wdt1[:],
                                   m.hT[:, bass.ds(b, 1), c * COL + PAD:c * COL + PAD + COL], start=True, stop=True)
                mm.then_inc(dt_done, 1)
                pe.wait_ge(dt_ready, ONE + b + 1)
                pe.sem_inc(m.passed, 1)
                for t in range(BT):
                    tr = pe.transpose(pre[0][:, t * HEADS:(t + 1) * HEADS], dtT[:, tok(t)], m.ident[0:HEADS, 0:HEADS])
                tr.then_inc(dtt_done, 1)
                pe.wait_ge(dA_done, ONE + b + 1)
                for t in range(BT):
                    T = b * BT + t
                    pe.wait_ge(cdec_done, ONE + T)
                    pe.wait_ge(seg_done, ONE + T)
                    pe.wait_ge(lastx_done, ONE + T)
                    for h in range(HEADS):
                        pe.matmul(cs_ps[:, h * P:(h + 1) * P], dA[:, t, h:h + 1].broadcast_to([P, P]), m.tri[:],
                                  start=True, stop=True)
                    pe.wait_ge(csc_done, ONE + T)
                    pe.wait_ge(gm_done, ONE + T)
                    pe.matmul(g_ps[:, P:P + HEADS], m.tri[:], dA[:, t, :], start=True, stop=True)
                    pe.matmul(g_ps[:, 0:P], xbc[2][:, tok(t)], xbc[3][:, tok(t)], start=True,
                              stop=True).then_inc(cs_done, 1)
                    pe.wait_ge(xdt_done, ONE + T)
                    pe.wait_ge(bt_done, ONE + T * 2)
                    pe.wait_ge(h_done, ONE + b + 1)
                    for j in range(3):
                        pe.transpose(tr_ps[:, j * P:(j + 1) * P], xbc[j][:, tok(t)], m.ident[:])
                    pe.transpose(tr_ps[:, 3 * P:4 * P], hcur[:, tok(t)], m.ident[:]).then_inc(tr_done, 1)
                    pe.wait_ge(bt_done, ONE + T * 2 + 1)
                    pe.wait_ge(xdd_done, ONE + T + 1)
                    pe.wait_ge(s_done, ONE + T)
                    pe.matmul(st_ps[:, 0:D_IN], bt[:], xdd[:].rearrange("p h d -> p (h d)"), start=True,
                              stop=True).then_inc(st_done, 1)
                    pe.wait_ge(m_done, ONE + T + 1)
                    pe.wait_ge(cts_done, ONE + T + 1)
                    pe.wait_ge(yd_done, ONE + T * 2)
                    for h in range(HEADS):
                        dst = y_ps[h % 2 * HD:(h % 2 + 1) * HD, h // 2 * P:(h // 2 + 1) * P]
                        pe.matmul(dst, xdt[:, h, :], mm_sb[:, h, :], start=True, stop=False)
                        mm = pe.matmul(dst, S[t % 2][:, h, :], cts[:, h, :], start=False, stop=True)
                    mm.then_inc(y_done, 1)
                    pe.wait_ge(yg_done, ONE + T * 2 + 2)
                    pe.wait_ge(o_read, ONE + T)
                    pe.wait_ge(oc_done, ONE + T)
                    for j in range(HALVES):
                        pe.matmul(o_ps[:, 0:P], yv[:, j, :], m.wout1[:, j, :], start=(j == 0), stop=(j == 1))
                    pe.wait_ge(yq_done, ONE + T + 1)
                    for j in range(HALVES):
                        mm = pe.matmul(o_ps[:, P:P + 1], yq[:, j, :], m.ones[:, 0:1], start=(j == 0), stop=(j == 1))
                    mm.then_inc(o_done, 1)

        @block.scalar
        def _(act):
            act.sem_inc(proj_read, 2)
            with act.Fori(0, NBATCH) as b:
                act.wait_ge(o_done, ONE + b * BT)
                act.wait_ge(yg_done, ONE + b * BT * 2)
                act.sem_inc(m.passed, 1)
                act.activation(hcur[:], m.hT[:, bass.ds(b, 1), PAD:PAD + SEQ], ACT.Copy).then_inc(h_done, 1)
                for i in range(NPRE):
                    j, c = i // NCOL, i % NCOL
                    act.wait_ge(proj_done, ONE + b * NPRE + i + 1)
                    dst = (xbc + sz)[j][:, col(c)]
                    act.activation(dst, pre[i % 2][:], ACT.Silu,
                                   bias=m.cb1[:, j:j + 1] if j < NB else 0.0).then_inc(proj_read, 1)
                act.wait_ge(dt_done, ONE + b + 1)
                for c in range(NCOL):
                    act.activation(dtT[:, col(c)], pre[c][0:HEADS, :], ACT.Identity, bias=m.dtb1[:]).then_inc(dt_step, 1)
                act.wait_ge(dt_step, ONE + b * 4 + 2)
                act.activation(dte[:], dtT[:], ACT.Abs).then_inc(dt_step, 1)
                act.wait_ge(dt_step, ONE + b * 4 + 3)
                act.activation(dte[:], dte[:], ACT.Exp, scale=-1.0).then_inc(dt_step, 1)
                act.wait_ge(dt_step, ONE + b * 4 + 4)
                act.activation(dtl[:], dte[:], ACT.Ln, bias=1.0).then_inc(dtl_done, 1)
                for t in range(BT):
                    T = b * BT + t
                    act.wait_ge(seg_done, ONE + T + 1)
                    act.wait_ge(cts_done, ONE + T)
                    act.wait_ge(s_done, ONE + T)
                    act.activation(cdec[:].rearrange("p h l -> p (h l)"), cs_ps[:], ACT.Exp).then_inc(cdec_done, 1)
                    act.wait_ge(last_done, ONE + T + 1)
                    act.wait_ge(xdd_done, ONE + T)
                    act.activation(lastx[:], last[:], ACT.Exp).then_inc(lastx_done, 1)
                    act.wait_ge(seg_done, ONE + T + 1)
                    act.wait_ge(m_done, ONE + T)
                    act.activation(dec[:], seg[:], ACT.Exp).then_inc(dec_done, 1)
                    act.wait_ge(xdt_done, ONE + T + 1)
                    act.wait_ge(st_done, ONE + T)
                    act.activation(bt[:], tr_ps[:, 2 * P:3 * P], ACT.Copy).then_inc(bt_done, 1)
                    act.sem_inc(m.passed, 1)
                    act.activation(resid[:, bass.ds(T, 1), :], tr_ps[:, 3 * P:4 * P], ACT.Copy).then_inc(bt_done, 1)
                    act.wait_ge(yg_done, ONE + T * 2 + 2)
                    act.wait_ge(o_done, ONE + T)
                    act.activation(yq[:], yv[:], ACT.Square).then_inc(yq_done, 1)
                    act.wait_ge(o_read, ONE + T + 1)
                    act.sem_inc(m.passed, 1)
                    act.activation(outs[:, bass.ds(T, 1), :], o_ps[:, 0:P], ACT.Copy).then_inc(oc_done, 1)
            act.wait_ge(fin, ONE + 1)
            act.activation(ss[:], ss[:], ACT.Sqrt).then_inc(sq_done, 1)
            act.wait_ge(fin, ONE + 2)
            act.activation(var[:], var[:], ACT.Sqrt).then_inc(sq_done, 1)

        @block.gpsimd
        def _(pool):
            with pool.Fori(0, NBATCH) as b:
                for t in range(BT):
                    T = b * BT + t
                    pool.wait_ge(gm_done, ONE + T + 1)
                    pool.wait_ge(dec_done, ONE + T + 1)
                    pool.wait_ge(y_done, ONE + T)
                    pool.tensor_tensor(mm_sb[:], dec[:], four(gm[:]), ALU.mult).then_inc(m_done, 1)
                    pool.wait_ge(cdec_done, ONE + T + 1)
                    pool.tensor_tensor(cts[:], cdec[:], four(xbc[3][:, tok(t)]), ALU.mult).then_inc(cts_done, 1)

        @block.vector
        def _(dve):
            with dve.Fori(0, NBATCH) as b:
                dve.wait_ge(dt_step, ONE + b * 4 + 4)
                dve.wait_ge(dtl_done, ONE + b + 1)
                dve.scalar_tensor_tensor(dtT[:], dtT[:], 0.0, dtl[:], ALU.max, ALU.add).then_inc(dt_ready, 1)
                dve.wait_ge(dtt_done, ONE + b + 1)
                dve.tensor_copy(dt[:], pre[0][:, 0:BT * HEADS].rearrange("p (t h) -> p t h", h=HEADS)
                                ).then_inc(dtt_read, 1)
                dve.wait_ge(dtt_read, ONE + b + 1)
                dve.tensor_tensor(dA[:], dt[:], m.negA1[:].unsqueeze(1).broadcast_to([P, BT, HEADS]),
                                  ALU.mult).then_inc(dA_done, 1)
                dve.wait_ge(y_done, ONE + b * BT)
                dve.memset(S[0][:], 0.0).then_inc(zero_done, 1)
                for t in range(BT):
                    T = b * BT + t
                    cs = cs_ps[:].rearrange("p (h l) -> p h l", h=HEADS)
                    dve.wait_ge(cs_done, ONE + T + 1)
                    dve.tensor_copy(csc[:], g_ps[:, P:P + HEADS]).then_inc(csc_done, 1)
                    dve.wait_ge(csc_done, ONE + T + 1)
                    dve.wait_ge(lastx_done, ONE + T)
                    dve.tensor_tensor(last[:], cs[:, :, P - 1], csc[:], ALU.subtract).then_inc(last_done, 1)
                    dve.wait_ge(dec_done, ONE + T)
                    for h in range(HEADS):
                        ins = dve.tensor_scalar(seg[:, h, :], cs[:, h, :], csc[:, h:h + 1], 0.0, ALU.subtract, ALU.min)
                    ins.then_inc(seg_done, 1)
                    dve.wait_ge(m_done, ONE + T)
                    dve.tensor_tensor(gm[:], g_ps[:, 0:P], m.tri[:], ALU.mult).then_inc(gm_done, 1)
                    dve.wait_ge(tr_done, ONE + T + 1)
                    dve.wait_ge(y_done, ONE + T)
                    xv = tr_ps[:, 0:D_IN].rearrange("p (h d) -> p h d", h=HEADS)
                    spread = lambda v: v.unsqueeze(2).broadcast_to([P, HEADS, HD])
                    dve.tensor_tensor(xdt[:], xv, spread(dt[:, t, :]), ALU.mult).then_inc(xdt_done, 1)
                    dve.wait_ge(xdt_done, ONE + T + 1)
                    dve.wait_ge(lastx_done, ONE + T + 1)
                    dve.wait_ge(st_done, ONE + T)
                    dve.tensor_tensor(xdd[:], xdt[:], spread(lastx[:]), ALU.mult).then_inc(xdd_done, 1)
                    dve.wait_ge(cdec_done, ONE + T + 1)
                    if t == 0:
                        dve.wait_ge(zero_done, ONE + b + 1)
                    else:
                        dve.wait_ge(s_done, ONE + T)
                    dve.tensor_tensor(S[1 - t % 2][:], S[t % 2][:], spread(cdec[:, :, P - 1]), ALU.mult
                                      ).then_inc(s_step, 1)
                    dve.wait_ge(s_step, ONE + T + 1)
                    dve.wait_ge(st_done, ONE + T + 1)
                    dve.tensor_tensor(S[1 - t % 2][:], S[1 - t % 2][:],
                                      st_ps[:, 0:D_IN].rearrange("p (h d) -> p h d", h=HEADS), ALU.add
                                      ).then_inc(s_done, 1)
                    dve.wait_ge(y_done, ONE + T + 1)
                    dve.wait_ge(o_done, ONE + T)
                    dve.wait_ge(yq_done, ONE + T)
                    for j in range(HALVES):
                        dve.scalar_tensor_tensor(yv[:, j, :], xbc[j][:, tok(t)], m.d1[:, j:j + 1],
                                                 y_ps[:, j * P:(j + 1) * P], ALU.mult, ALU.add).then_inc(yd_done, 1)
                    for j in range(HALVES):
                        dve.wait_ge(yd_done, ONE + T * 2 + j + 1)
                        dve.tensor_tensor(yv[:, j, :], yv[:, j, :], sz[j][:, tok(t)], ALU.mult).then_inc(yg_done, 1)
                    dve.wait_ge(o_done, ONE + T + 1)
                    dve.tensor_scalar(ss[:, bass.ds(T, 1)], o_ps[:, P:P + 1], 1.0 / D_IN, EPS, ALU.mult, ALU.add
                                      ).then_inc(o_read, 1)
            chain = [0]

            def then(ins):
                chain[0] += 1
                ins.then_inc(tail_step, 1)
                dve.wait_ge(tail_step, ONE + chain[0])

            dve.wait_ge(o_read, ONE + TILES)
            dve.sem_inc(fin, 1)
            dve.wait_ge(sq_done, ONE + 1)
            then(dve.reciprocal(ss[:], ss[:]))
            dve.wait_ge(oc_done, ONE + TILES)
            dve.wait_ge(bt_done, ONE + 2 * TILES)
            with dve.Fori(0, TILES) as t:
                one = bass.ds(t, 1)
                dve.scalar_tensor_tensor(outs[:, one, :], outs[:, one, :], ss[:, one], resid[:, one, :],
                                         ALU.mult, ALU.add).then_inc(h_step, 1)
            dve.wait_ge(h_step, ONE + TILES)
            with dve.Fori(0, TILES) as t:
                dve.bn_stats(stats[:, bass.ds(t, 1), :], outs[:, bass.ds(t, 1), :]).then_inc(h_step, 1)
            dve.wait_ge(h_step, ONE + 2 * TILES)
            then(dve.tensor_tensor(tmp[:], stats[:, :, 1], stats[:, :, 4], ALU.subtract))
            then(dve.tensor_tensor(mean[:], stats[:, :, 1], stats[:, :, 4], ALU.add))
            then(dve.tensor_scalar(mean[:], mean[:], 0.5, None, ALU.mult))
            then(dve.tensor_tensor(var[:], stats[:, :, 2], stats[:, :, 5], ALU.add))
            then(dve.scalar_tensor_tensor(tmp[:], tmp[:], 0.25, tmp[:], ALU.mult, ALU.mult))
            then(dve.scalar_tensor_tensor(var[:], var[:], 1.0 / P, tmp[:], ALU.mult, ALU.add))
            then(dve.tensor_scalar(var[:], var[:], EPS, None, ALU.add))
            dve.sem_inc(fin, 1)
            dve.wait_ge(sq_done, ONE + 2)
            then(dve.reciprocal(var[:], var[:]))
            with dve.Fori(0, TILES) as t:
                one = bass.ds(t, 1)
                dve.tensor_scalar(outs[:, one, :], outs[:, one, :], mean[:, one], var[:, one], ALU.subtract,
                                  ALU.mult).then_inc(h_step, 1)
            dve.wait_ge(h_step, ONE + 3 * TILES)
            row = lambda v: v.unsqueeze(1).broadcast_to([P, TILES, P])
            then(dve.tensor_tensor(outs[:], outs[:], row(m.lng[:]), ALU.mult))
            then(dve.tensor_tensor(outs[:], outs[:], row(m.lnb[:]), ALU.add))
            for b in range(NBATCH):
                ob = outs[:, b * BT:(b + 1) * BT, :]
                then(dve.tensor_tensor(ob, ob, m.gate[:, 1, 0, b, :].unsqueeze(1).broadcast_to([P, BT, P]), ALU.mult))
            then(dve.tensor_tensor(m.X[:], m.X[:], outs[:], ALU.add))


def build(nc, a, out, phases=99):
    with ExitStack() as ctx:
        sb = lambda name, shape, dt=F32: ctx.enter_context(nc.sbuf_tensor(name, shape, dt))
        m = Memory()
        m.X = sb("X", [P, TILES, P])
        m.hT = sb("hT", [P, NBATCH, PAD + SEQ])
        m.ident = sb("ident", [P, P])
        m.tri = sb("tri", [P, P])
        m.ones = sb("ones", [P, 1])
        m.expert_no = sb("expert_no", [P, NE])
        m.onesrow = sb("onesrow", [1, P])
        m.shift = sb("shift", [P, 2, 2, NBATCH])
        m.scale = sb("scale", [P, 2, 2, NBATCH])
        m.gate = sb("gate", [P, 2, 2, NBATCH, P])
        m.wc1 = sb("wc1", [P, TAPS, COL])
        m.wz1 = sb("wz1", [P, D_IN])
        m.wdt1 = sb("wdt1", [P, HEADS])
        m.cb1 = sb("cb1", [P, COL // P])
        m.dtb1 = sb("dtb1", [HEADS, 1])
        m.negA1 = sb("negA1", [P, HEADS])
        m.d1 = sb("d1", [P, HALVES])
        m.wout1 = sb("wout1", [P, HALVES, P])
        m.lng = sb("lng", [P, P])
        m.lnb = sb("lnb", [P, P])
        m.gate1 = sb("gate1", [P, NE])
        m.gb1 = sb("gb1", [P, 2, NE])
        m.b1 = sb("b1", [P, NE, F1 // P])
        m.b2 = sb("b2", [1, NE * P])
        m.out = out
        m.kept = ctx
        m.stored = ctx.enter_context(nc.semaphore("stored"))
        m.passed = ctx.enter_context(nc.semaphore("passed"))
        layer0 = ctx.enter_context(ExitStack())
        sb0 = lambda name, shape, dt=F32: layer0.enter_context(nc.sbuf_tensor(name, shape, dt))
        m.pick = sb0("pick", [3 * 2 * N0, 2 * N0 * P], BF16)
        m.wc0 = sb0("wc0", [P, TAPS, D_IN])
        m.wz0 = sb0("wz0", [P, D_IN])
        m.cb0 = sb0("cb0", [P, HALVES])
        m.wx = sb0("wx", [P, HALVES, RANK + 6 * N0])
        m.wdt0 = sb0("wdt0", [RANK, D_IN])
        m.bdt0 = sb0("bdt0", [P, HALVES])
        m.negA0 = sb0("negA0", [P, HALVES, N0])
        m.diagD0 = sb0("diagD0", [P, HALVES, P])
        m.wo0 = sb0("wo0", [P, HALVES, P])
        m.router = sb0("router", [P, NE])
        m.wgate = sb0("wgate", [P, NE, F0])
        m.wup = sb0("wup", [P, NE, F0])
        m.wdown = sb0("wdown", [P, NE, F0 // P, P])
        m.sems = {}
        for tag, names in (("n00_", NORM_SEMS), ("n01_", NORM_SEMS), ("n10_", NORM_SEMS), ("n11_", NORM_SEMS),
                           ("ma_", MAMBA_SEMS), ("e0_", EXPERT_SEMS), ("e1_", EXPERT_SEMS), ("ss_", SSD_SEMS)):
            for name in names.split():
                m.sems[tag + name] = ctx.enter_context(nc.semaphore(tag + name))
        setup(nc, a, m)
        steps = [lambda: norm(nc, m, 0, 0), lambda: mamba(nc, m), lambda: norm(nc, m, 0, 1),
                 lambda: experts(nc, a, m, 0), lambda: norm(nc, m, 1, 0), lambda: ssd(nc, m),
                 lambda: norm(nc, m, 1, 1), lambda: experts(nc, a, m, 1)]
        for i, step in enumerate(steps[:phases]):
            if i == 2:
                m.w1 = ctx.enter_context(nc.sbuf_tensor("w1", [P, NE, F1], F32, side="right"))
                m.w2 = ctx.enter_context(nc.sbuf_tensor("w2", [P, NE, F1 // P, P], F32, side="right"))
            if i == 4:
                layer0.close()
            step()
        if phases < len(steps):
            with nc.Block() as block:
                @block.sync
                def _(sp):
                    sp.dma_start(out.rearrange("b (j p) d -> p (b j) d", p=P), m.X[:]).then_inc(m.stored, 16)
                    sp.wait_ge(m.stored, 16)


def kernel(**inputs):
    import numpy as np
    import concourse.bacc as bacc
    from concourse.bass_utils import run_bass_kernel_spmd

    def laid(name, f=lambda v: v):
        return np.ascontiguousarray(f(np.asarray(inputs[name])))

    T = lambda v: v.T
    last2 = lambda v: v.transpose(0, 2, 1)
    three = lambda v: np.concatenate([v.T[:, :RANK]] + 3 * [v.T[:, RANK:]], axis=1)
    arrays = {
        "L0_cT": laid("L0_c", T), "L1_cT": laid("L1_c", T), "L0_wmod": laid("L0_wmod"), "L1_wmod": laid("L1_wmod"),
        "L0_attn_x": laid("L0_attn_x"), "L0_WiT": laid("L0_attn_Wi", T),
        "L0_conv_row": laid("L0_attn_conv_w", lambda v: v[:, 0, :].T), "L0_WxT": laid("L0_attn_Wx", three),
        "L0_WdtT": laid("L0_attn_Wdt", T), "L0_WoT": laid("L0_attn_Wo", T),
        "L1_conv_row": laid("L1_attn_conv_w", T),
        "router_T": laid("L0_ffn_router_w", T), "w_gate_T": laid("L0_ffn_w_gate", last2),
        "w_up_T": laid("L0_ffn_w_up", last2), "w_down_T": laid("L0_ffn_w_down", last2),
        "gate_T": laid("L1_ffn_gate_w", T),
    }
    for short, name in (("cb0", "L0_attn_conv_b"), ("bdt0", "L0_attn_bdt"), ("dp0", "L0_attn_Dp"),
                        ("cb1", "L1_attn_conv_b"), ("rms", "L1_attn_rms_w")):
        arrays[short] = laid(name, lambda v: v.reshape(-1, P).T)
    arrays["b1"] = laid("L1_ffn_b1", lambda v: v.reshape(NE, -1, P).transpose(2, 0, 1))
    for name in ("L0_attn_A_log L1_attn_W_in L1_attn_dt_bias L1_attn_A_log L1_attn_D L1_attn_W_out L1_attn_ln_g "
                 "L1_attn_ln_b L1_ffn_gate_b L1_ffn_expert_bias L1_ffn_w1 L1_ffn_w2").split():
        arrays[name] = laid(name)
    arrays["L1_ffn_b2"] = laid("L1_ffn_b2", lambda v: v.reshape(1, -1))
    arrays["ident"] = np.eye(P, dtype=np.float32)
    arrays["tri"] = np.triu(np.ones((P, P), np.float32))
    arrays["expert_no"] = np.arange(NE, dtype=np.float32).reshape(1, NE)
    arrays["onesrow"] = np.ones((1, P), np.float32)
    pick = np.zeros((3, 2 * N0, 2 * N0, P), mybir.dt.np(BF16))
    for n in range(2 * N0):
        pick[:, n, n, :] = 1.0
    arrays["pick"] = pick.reshape(3 * 2 * N0, 2 * N0 * P)

    nc = bacc.Bacc("TRN2", target_bir_lowering=False, num_devices=1)
    aps = {}
    for name, v in arrays.items():
        aps[name] = nc.dram_tensor("in_" + name, v.shape, mybir.dt.from_np(v.dtype), kind="ExternalInput").ap()
    out = nc.dram_tensor("out", (NBATCH, SEQ, P), F32, kind="ExternalOutput").ap()
    build(nc, aps, out)
    r = run_bass_kernel_spmd(nc, [{"in_" + k: v for k, v in arrays.items()}], core_ids=[0])
    return r.results[0]["out"]
```

```python
from contextlib import ExitStack

import concourse.bass as bass
from concourse import mybir

ALU = mybir.AluOpType
ACT = mybir.ActivationFunctionType
F32 = mybir.dt.float32
BF16 = mybir.dt.bfloat16
AX = mybir.AxisListType.X

P = 128
NBATCH = 4
SEQ = 1024
TOKENS = NBATCH * SEQ
TILES = TOKENS // P
BT = SEQ // P
COL = 512
NCOL = SEQ // COL
TAPS = 4
PAD = TAPS - 1
EPS = 1e-5

D_IN = 256
HALVES = D_IN // P
N0 = 16
RANK = 64
F0 = 256
NE = 8
D_STATE = 128
HEADS = 4
HD = D_IN // HEADS
F1 = 512
CHOICES = (2, 1)
SLOTS = tuple(c * TILES + NE for c in CHOICES)
ROW_NORMS = ((0, 1), (1, 0), (1, 1))
LATE = (48, 80)
CLEARS = sum(SLOTS) // 8


class Memory:
    pass


ONE = 1
NORM_SEMS = "s_stats s_chain s_std s_xn s_tr s_h s_scaled s_rows"
SORTED_SEMS = ("xt_done xt_read up_done act_done wide_done ht_done ht_read out_done out_read "
               "loaded0 loaded1 stored0 stored1")
MAMBA_SEMS = ("pre_done pre_read low_done low_read split_done split_step parts_done dmm_done sp_step ln_done "
              "relu_done delta_done u0_done u1_done bc_done bc_read bu_done decay_done scan_done ch_done acc_done "
              "yg_done out_done gated x_done")
SSD_SEMS = ("proj_done proj_read dt_done dt_step dt_ready dtt_done dtt_read dA_done cs_done tr_done "
            "csc_done seg_done dec_done cdec_done lastx_done gm_done m_done cts_done xdt_done xdd_done "
            "bt_done y_done st_done s_done s_step yd_done yg_done yq_done o_done "
            "dtl_done last_done oc_done fin sq_done tail_step h_step norm_done added")



def setup(nc, a, m):
    with ExitStack() as ctx:
        sb = lambda name, shape, dt=F32: ctx.enter_context(nc.sbuf_tensor("su_" + name, shape, dt))
        sem = lambda name: m.kept.enter_context(nc.semaphore("su_" + name))
        ps = ctx.enter_context(nc.psum_tensor("ps_setup", [P, 8, COL], F32))
        cw0 = sb("cw0", [P, TAPS, D_IN])
        cw1 = sb("cw1", [P, TAPS, COL])
        wmod = sb("wmod", [P, 2, 6 * P])
        win0 = sb("win0", [P, D_IN])
        win1 = sb("win1", [P, COL])
        wout_raw = sb("wout_raw", [P, HALVES, P])
        cT = sb("cT", [P, 2, NBATCH])
        scT = sb("scT", [P, 2, NBATCH])
        sig = sb("sig", [P, 2, NBATCH])
        alog0 = sb("alog0", [P, HALVES, N0])
        alog1 = sb("alog1", [P, HEADS])
        dp0 = sb("dp0", [P, HALVES])
        rms = sb("rms", [P, HALVES])
        gsign = sb("gsign", [P, 2, 2, NBATCH, P])
        gate_raw = sb("gate_raw", [P, 2, 2, NBATCH, P])
        small, big, s_silu, s_modT, s_modB, s_v, s_exp = (
            sem(n) for n in ("small", "big", "s_silu", "s_modT", "s_modB", "s_v", "s_exp"))
        s_abs = sem("s_abs")
        s_bank_read = sem("s_bank_read")
        s_zeros = sem("s_zeros")
        GATE_BANK = ((0, 2), (4, 6))
        ROW_BANK = ((3, 5), (7, 1), (0, 2))
        zeros = sb("zeros", [P, 1024])
        lng = sb("lng", [P, P])
        lnb = sb("lnb", [P, P])
        block = ctx.enter_context(nc.Block())
        n_small, n_big = [0], [0]

        @block.sync
        def _(sp):
            def load(dst, src, s=small, n=n_small):
                sp.dma_start(dst, src).then_inc(s, 16)
                n[0] += 1
            for l, name in ((0, "L0"), (1, "L1")):
                load(cT[:, l, :], a[name + "_cT"])
                load(wmod[:, l, :], a[name + "_wmod"])
            load(m.ident[:], a["ident"])
            load(m.tri[:], a["tri"])
            load(m.pick[:], a["pick"])
            load(m.before[:], a["before"])
            load(m.count[:], a["count"].partition_broadcast(P))
            load(cw0[:], a["L0_conv_row"].partition_broadcast(P))
            load(cw1[:], a["L1_conv_row"].partition_broadcast(P))
            load(win0[:], a["L0_WiT"][:, 0:D_IN])
            load(m.wz0[:], a["L0_WiT"][:, D_IN:2 * D_IN])
            load(win1[:], a["L1_attn_W_in"][:, D_IN:D_IN + COL])
            load(m.wz1[:], a["L1_attn_W_in"][:, 0:D_IN])
            load(m.wdt1[:], a["L1_attn_W_in"][:, D_IN + COL:D_IN + COL + HEADS])
            load(m.wx[:], a["L0_WxT"].rearrange("(j p) n -> p j n", p=P))
            load(m.wdt0[:], a["L0_WdtT"])
            load(m.wo0[:], a["L0_WoT"].rearrange("(j p) n -> p j n", p=P))
            load(wout_raw[:], a["L1_attn_W_out"].rearrange("(j p) n -> p j n", p=P))
            load(m.cb0[:], a["cb0"])
            load(m.cb1[:], a["cb1"])
            load(m.bdt0[:], a["bdt0"])
            load(dp0[:], a["dp0"])
            load(rms[:], a["rms"])
            load(alog0[:], a["L0_attn_A_log"].rearrange("(j p) n -> p j n", p=P))
            load(alog1[:], a["L1_attn_A_log"].partition_broadcast(P))
            load(m.dtb1[:], a["L1_attn_dt_bias"].rearrange("(h o) -> h o", o=1))
            for j in range(HALVES):
                for q in range(P // HD):
                    load(m.d1[q * HD:(q + 1) * HD, j:j + 1],
                         a["L1_attn_D"][2 * j + q:2 * j + q + 1].partition_broadcast(HD))
            load(lng[:], a["L1_attn_ln_g"].partition_broadcast(P))
            load(lnb[:], a["L1_attn_ln_b"].partition_broadcast(P))
            load(m.gb1[:, 0, :], a["L1_ffn_gate_b"].partition_broadcast(P))
            load(m.gb1[:, 1, :], a["L1_ffn_expert_bias"].partition_broadcast(P))
            load(m.X[:], a["L0_attn_x"].rearrange("b (j p) d -> p (b j) d", p=P), big, n_big)
            load(m.router[:], a["router_T"], big, n_big)
            load(m.gate1[:], a["gate_T"], big, n_big)
            for name, semaphore in m.sems.items():
                if not name.startswith("so_"):
                    sp.sem_inc(semaphore, ONE)
            sp.wait_ge(s_zeros, 1)
            for layer in range(2):
                rows = SLOTS[layer] * P
                for r in range(0, rows, 1024):
                    sp.dma_start(m.xs[layer][r:r + 1024, :].rearrange("(p q) d -> p (q d)", p=P), zeros[:]
                                 ).then_inc(m.cleared, 16)
            sp.wait_ge(m.cleared, 16 * CLEARS)
            sp.wait_ge(big, 16 * n_big[0])

        @block.gpsimd
        def _(pool):
            pool.memset(zeros[:], 0.0).then_inc(s_zeros, 1)

        @block.scalar
        def _(act):
            act.wait_ge(small, 16 * n_small[0])
            act.activation(scT[:], cT[:], ACT.Silu).then_inc(s_silu, 1)
            act.activation(m.negA0[:], alog0[:], ACT.Exp).then_inc(s_exp, 1)
            act.activation(m.negA1[:], alog1[:], ACT.Exp).then_inc(s_exp, 1)
            act.wait_ge(s_modB, 16)
            for l in range(2):
                for g in range(2):
                    src = ps[:, GATE_BANK[l][g], 0:NBATCH * P].rearrange("p (b d) -> p b d", b=NBATCH)
                    act.activation(gate_raw[:, l, g], src, ACT.Abs).then_inc(s_abs, 1)

        @block.tensor
        def _(pe):
            pe.wait_ge(s_silu, 1)
            for l in range(2):
                for j in range(6):
                    mm = pe.matmul(ps[:, 1, (6 * l + j) * NBATCH:(6 * l + j + 1) * NBATCH],
                                   wmod[:, l, j * P:(j + 1) * P], scT[:, l, :], start=True, stop=True)
            mm.then_inc(s_modT, 1)
            def spread_rows(bank, l, block):
                for b in range(NBATCH):
                    pe.matmul(ps[:, bank, b * P:(b + 1) * P], scT[:, l, b:b + 1].broadcast_to([P, P]),
                              wmod[:, l, block * P:(block + 1) * P], start=True, stop=True).then_inc(s_modB, 1)
            for l in range(2):
                for g in range(2):
                    spread_rows(GATE_BANK[l][g], l, 3 * g + 2)
            for n, (l, sub) in enumerate(ROW_NORMS):
                for j in range(2):
                    if ROW_BANK[n][j] == 1:
                        pe.wait_ge(s_bank_read, 1)
                    if ROW_BANK[n][j] == 0:
                        pe.wait_ge(s_bank_read, 2)
                    spread_rows(ROW_BANK[n][j], l, 3 * sub + j)

        @block.vector
        def _(dve):
            steps = [0]

            def step(ins):
                steps[0] += 1
                ins.then_inc(s_v, 1)

            dve.wait_ge(small, 16 * n_small[0])
            for k in range(TAPS):
                step(dve.tensor_tensor(m.wc0[:, k, :], win0[:], cw0[:, k, :], ALU.mult))
                step(dve.tensor_tensor(m.wc1[:, k, :], win1[:], cw1[:, k, :], ALU.mult))
            for j in range(HALVES):
                step(dve.tensor_scalar(m.wout1[:, j, :], wout_raw[:, j, :], rms[:, j:j + 1], None, ALU.mult))
                step(dve.tensor_scalar(m.diagD0[:, j, :], m.ident[:], dp0[:, j:j + 1], None, ALU.mult))
            step(dve.memset(m.hT[:, :, 0:PAD], 0.0))
            step(dve.memset(m.ones[:], 1.0))
            step(dve.tensor_scalar(m.count128[:], m.count[:, 0:TILES], float(P), None, ALU.mult))
            step(dve.tensor_tensor(m.gb1[:, 0, :], m.gb1[:, 0, :], m.gb1[:, 1, :], ALU.add))
            dve.wait_ge(s_exp, 2)
            step(dve.tensor_scalar(m.negA0[:], m.negA0[:], -1.0, None, ALU.mult))
            step(dve.tensor_scalar(m.negA1[:], m.negA1[:], -1.0, None, ALU.mult))
            dve.wait_ge(s_modT, 1)
            modT = ps[:, 1, 0:12 * NBATCH].rearrange("p (l j b) -> p l j b", l=2, j=6)
            for l in range(2):
                for g in range(2):
                    step(dve.tensor_copy(m.shift[:, l, g, :], modT[:, l, 3 * g, :]))
                    step(dve.tensor_scalar(m.scale[:, l, g, :], modT[:, l, 3 * g + 1, :], 1.0, None, ALU.add))
            dve.wait_ge(s_v, steps[0])
            dve.sem_inc(s_bank_read, 1)
            dve.wait_ge(s_modB, 16)
            dve.wait_ge(s_abs, 4)
            for l in range(2):
                for g in range(2):
                    src = ps[:, GATE_BANK[l][g], 0:NBATCH * P].rearrange("p (b d) -> p b d", b=NBATCH)
                    step(dve.tensor_scalar(gsign[:, l, g], src, 0.0, 2.0, ALU.is_ge, ALU.mult))
            for l in range(2):
                for g in range(2):
                    step(dve.tensor_scalar(gate_raw[:, l, g], gate_raw[:, l, g], 0.25, None, ALU.max))
            dve.wait_ge(s_v, steps[0])
            step(dve.scalar_tensor_tensor(m.gate[:], gsign[:], -1.0, gate_raw[:], ALU.add, ALU.mult))
            dve.sem_inc(s_bank_read, 1)
            dve.wait_ge(s_v, steps[0])
            for dst, src in ((m.lng_gate, lng), (m.lnb_gate, lnb)):
                step(dve.tensor_tensor(dst[:], m.gate[:, 1, 0], src[:].unsqueeze(1).broadcast_to([P, NBATCH, P]),
                                       ALU.mult))
            dve.wait_ge(s_modB, 16 + 2 * len(ROW_NORMS) * NBATCH)
            for n in range(len(ROW_NORMS)):
                for j, dst in ((0, m.shift_row), (1, m.scale_row)):
                    src = ps[:, ROW_BANK[n][j], 0:NBATCH * P].rearrange("p (b d) -> p b d", b=NBATCH)
                    step(dve.tensor_scalar(dst[:, n], src, float(j), None, ALU.add))
            dve.wait_ge(s_v, steps[0])


def norm(nc, a, m, layer, sub):
    GROUP = 4
    GROUPS = TILES // GROUP
    with ExitStack() as ctx:
        sb = lambda name, shape, dt=F32: ctx.enter_context(nc.sbuf_tensor(f"n{layer}{sub}_" + name, shape, dt))
        sem = lambda name: m.sems[f"n{layer}{sub}_" + name]
        banks = [ctx.enter_context(nc.psum_tensor(f"n{layer}{sub}_ps{i}", [P, COL], F32)) for i in range(2)]
        stats = sb("stats", [P, TILES, 6])
        mean = sb("mean", [P, TILES])
        var = sb("var", [P, TILES])
        rstd = sb("rstd", [P, TILES])
        tmp = sb("tmp", [P, TILES])
        xn = [sb(f"xn{i}", [P, GROUP, P]) for i in range(2)]
        keep_rows = (layer, sub) in ROW_NORMS
        s_stats, s_chain, s_std, s_xn, s_tr, s_h, s_scaled, s_rows = (
            sem(n) for n in NORM_SEMS.split())
        block = ctx.enter_context(nc.Block())

        @block.sync
        def _(sp):
            if (layer, sub) == (0, 1):
                sp.dma_start(m.wgu[:, :, 0:F0], a["w_gate_T"].rearrange("e k f -> k e f")).then_inc(m.late, 16)
                sp.dma_start(m.wgu[:, :, F0:2 * F0], a["w_up_T"].rearrange("e k f -> k e f")).then_inc(m.late, 16)
                sp.dma_start(m.wdown[:], a["w_down_T"].rearrange("e (j p) d -> p e j d", p=P)).then_inc(m.late, 16)
            if (layer, sub) == (1, 1):
                sp.dma_start(m.w1[:], a["L1_ffn_w1"].rearrange("e k f -> k e f")).then_inc(m.late, 16)
                sp.dma_start(m.w2[:], a["L1_ffn_w2"].rearrange("e (j p) d -> p e j d", p=P)).then_inc(m.late, 16)

        @block.vector
        def _(dve):
            with dve.Fori(0, NBATCH) as b:
                for i in range(BT):
                    t = bass.ds(b * BT + i, 1)
                    dve.bn_stats(stats[:, t, :], m.X[:, t, :]).then_inc(s_stats, 1)
            dve.wait_ge(s_stats, ONE + TILES)
            half_e, half_o = stats[:, :, 1], stats[:, :, 4]
            dve.tensor_tensor(tmp[:], half_e, half_o, ALU.subtract).then_inc(s_chain, 1)
            dve.tensor_tensor(mean[:], half_e, half_o, ALU.add).then_inc(s_chain, 1)
            dve.tensor_tensor(var[:], stats[:, :, 2], stats[:, :, 5], ALU.add).then_inc(s_chain, 1)
            dve.wait_ge(s_chain, ONE + 3)
            dve.tensor_scalar(mean[:], mean[:], 0.5, None, ALU.mult).then_inc(s_chain, 1)
            dve.scalar_tensor_tensor(tmp[:], tmp[:], 0.25, tmp[:], ALU.mult, ALU.mult).then_inc(s_chain, 1)
            dve.wait_ge(s_chain, ONE + 5)
            dve.scalar_tensor_tensor(var[:], var[:], 1.0 / P, tmp[:], ALU.mult, ALU.add).then_inc(s_chain, 1)
            dve.wait_ge(s_chain, ONE + 6)
            dve.tensor_scalar(var[:], var[:], EPS, None, ALU.add).then_inc(s_chain, 1)
            dve.wait_ge(s_std, ONE + 1)
            dve.reciprocal(rstd[:], rstd[:]).then_inc(s_chain, 1)
            dve.wait_ge(s_chain, ONE + 8)
            with dve.Fori(0, GROUPS // 2) as i:
                for r in range(2):
                    dve.wait_ge(s_tr, ONE + i * 2 + r + 1)
                    if keep_rows:
                        dve.wait_ge(s_scaled, ONE + i * 2 + r + 1)
                    for j in range(GROUP):
                        t = (i * 2 + r) * GROUP + j
                        dve.tensor_scalar(xn[r][:, j, :], m.X[:, bass.ds(t, 1), :], mean[:, bass.ds(t, 1)],
                                          rstd[:, bass.ds(t, 1)], ALU.subtract, ALU.mult).then_inc(s_xn, 1)

        @block.gpsimd
        def _(pool):
            if keep_rows:
                pool.sem_inc(s_scaled, 2)
                with pool.Fori(0, NBATCH) as b:
                    for r in range(2):
                        g = b * 2 + r
                        dst = m.rows[:, bass.ds(g * GROUP, GROUP), :]
                        row = lambda t: t[:, ROW_NORMS.index((layer, sub)), bass.ds(b, 1), :].broadcast_to([P, GROUP, P])
                        pool.wait_ge(s_xn, ONE + (g + 1) * GROUP)
                        pool.sem_inc(m.passed, 1)
                        pool.tensor_tensor(dst, xn[r][:], row(m.scale_row), ALU.mult).then_inc(s_scaled, 1)
                        pool.wait_ge(s_scaled, ONE + g + 1 + 2)
                        pool.sem_inc(m.passed, 1)
                        pool.tensor_tensor(dst, dst, row(m.shift_row), ALU.add).then_inc(s_rows, 1)

        @block.tensor
        def _(pe):
            pe.sem_inc(s_tr, 2)
            pe.wait_ge(s_h, ONE + 2)
            with pe.Fori(0, GROUPS // 2) as i:
                for r in range(2):
                    pe.wait_ge(s_xn, ONE + (i * 2 + r + 1) * GROUP)
                    pe.wait_ge(s_h, ONE + i * 2 + r + 1)
                    for j in range(GROUP):
                        tr = pe.transpose(banks[r][:, j * P:(j + 1) * P], xn[r][:, j, :], m.ident[:])
                    tr.then_inc(s_tr, 1)

        @block.scalar
        def _(act):
            act.sem_inc(s_h, 2)
            act.wait_ge(s_chain, ONE + 7)
            act.activation(rstd[:], var[:], ACT.Sqrt).then_inc(s_std, 1)
            with act.Fori(0, NBATCH) as b:
                for r in range(2):
                    act.wait_ge(s_tr, ONE + 2 + b * 2 + r + 1)
                    act.sem_inc(m.passed, 1)
                    act.activation(m.hT[:, bass.ds(b, 1), PAD + r * COL:PAD + (r + 1) * COL],
                                   banks[r][:].rearrange("p (o c) -> p o c", o=1), ACT.Identity,
                                   bias=m.shift[:, layer, sub, bass.ds(b, 1)],
                                   scale=m.scale[:, layer, sub, bass.ds(b, 1)]).then_inc(s_h, 1)
            act.wait_ge(s_h, ONE + 2 + GROUPS)


def mamba(nc, m):
    with ExitStack() as ctx:
        sb = lambda name, shape, dt=F32: ctx.enter_context(nc.sbuf_tensor("ma_" + name, shape, dt))
        sem = lambda name: m.sems["ma_" + name]
        bank = [ctx.enter_context(nc.psum_tensor(f"mps{i}", [P, COL], F32)) for i in range(2)]
        bc_ps = ctx.enter_context(nc.psum_tensor("bc_ps", [P, SEQ], F32))
        y_ps = [ctx.enter_context(nc.psum_tensor(f"y_ps{i}", [P, SEQ], F32)) for i in range(HALVES)]
        xp = [sb(f"xp{i}", [P, SEQ]) for i in range(HALVES)]
        sz = [sb(f"sz{i}", [P, SEQ]) for i in range(HALVES)]
        delta = [sb(f"delta{i}", [P, SEQ]) for i in range(HALVES)]
        u = [sb(f"u{i}", [P, SEQ]) for i in range(HALVES)]
        low = sb("low", [RANK, SEQ])
        G = 2 * N0
        parts = sb("parts", [3 * G, SEQ], BF16)
        hi = sb("hi", [3 * G, COL], BF16)
        mid = sb("mid", [3 * G, COL], BF16)
        rest = sb("rest", [3 * G, COL])
        bsb = [sb(f"bsb{i}", [P, SEQ]) for i in range(2)]
        csb = [sb(f"csb{i}", [P, SEQ]) for i in range(2)]
        SLOTS = 4
        bu = [sb(f"bu{i}", [P, SEQ]) for i in range(SLOTS)]
        DECAYS = 4
        decay = [sb(f"decay{i}", [P, SEQ]) for i in range(DECAYS)]
        h = [sb(f"h{i}", [P, SEQ]) for i in range(SLOTS)]
        yg, ab, lt = bu, h, decay
        (pre_done, pre_read, low_done, low_read, split_done, split_step, parts_done, dmm_done, sp_step, ln_done,
         relu_done, delta_done, u0_done, u1_done, bc_done, bc_read, bu_done, decay_done, scan_done, ch_done, acc_done,
         yg_done, out_done, gated, x_done) = (sem(n) for n in MAMBA_SEMS.split())
        RING = 2
        block = ctx.enter_context(nc.Block())
        NPRE = 2 * HALVES * NCOL
        XPRE = HALVES * NCOL
        UNITS = N0 * HALVES
        col = lambda c: slice(c * COL, (c + 1) * COL)

        def row_place(n, w):
            if isinstance(n, int) and (n, w) in ((0, 0), (N0 - 1, 1)):
                return 0 if n == 0 else 2 * N0 - 1
            return 2 * n - 1 if w == 0 else 2 * n + 2

        def all_batches(engine, start, body, finish):
            start(0)
            with engine.Fori(0, NBATCH - 1) as b:
                body(b, lambda: start(b + 1))
                finish(b)
            body(NBATCH - 1, lambda: None)
            finish(NBATCH - 1)

        @block.tensor
        def _(pe):
            def project(b, i):
                what, j, c = i // XPRE, i // NCOL % HALVES, i % NCOL
                pe.wait_ge(pre_read, ONE + b * NPRE + i + 1)
                if i == XPRE:
                    pe.wait_ge(low_read, ONE + b * NCOL + NCOL)
                if not isinstance(b, int):
                    pe.sem_inc(m.passed, 1)
                if what == 0:
                    for k in range(TAPS):
                        mm = pe.matmul(bank[i % 2][:], m.wc0[:, k, j * P:(j + 1) * P],
                                       m.hT[:, bass.ds(b, 1), c * COL + k:c * COL + k + COL],
                                       start=(k == 0), stop=(k == TAPS - 1))
                else:
                    mm = pe.matmul(bank[i % 2][:], m.wz0[:, j * P:(j + 1) * P],
                                   m.hT[:, bass.ds(b, 1), c * COL + PAD:c * COL + PAD + COL],
                                   start=True, stop=True)
                mm.then_inc(pre_done, 1)

            def start(b):
                for i in range(XPRE):
                    project(b, i)
                pe.wait_ge(pre_read, ONE + b * NPRE + XPRE + RING)
                for c in range(NCOL):
                    for j in range(HALVES):
                        mm = pe.matmul(bank[c][0:RANK, :], m.wx[:, j, 0:RANK], xp[j][:, col(c)],
                                       start=(j == 0), stop=(j == 1))
                    mm.then_inc(low_done, 1)

            def body(b, start_next):
                pe.wait_ge(low_read, ONE + b * NCOL + NCOL)
                pe.wait_ge(yg_done, ONE + b * 2)
                for j in range(HALVES):
                    for c in range(NCOL):
                        mm = pe.matmul(y_ps[j][:, col(c)], m.wdt0[:, j * P:(j + 1) * P], low[:, col(c)],
                                       start=True, stop=True)
                    mm.then_inc(dmm_done, 1)
                pe.wait_ge(gated, ONE + b * 2)
                for c in range(NCOL):
                    for j in range(HALVES):
                        mm = pe.matmul(bc_ps[0:3 * G, col(c)], m.wx[:, j, RANK:RANK + 3 * G], xp[j][:, col(c)],
                                       start=(j == 0), stop=(j == 1))
                    mm.then_inc(split_done, 1)
                for i in range(XPRE, XPRE + RING):
                    project(b, i)
                for j in range(HALVES):
                    pe.wait_ge(sp_step, ONE + b * 4 + j + 1)
                    pe.wait_ge(relu_done, ONE + b * 2 + j + 1)
                    for c in range(NCOL):
                        pe.matmul(y_ps[j][:, col(c)], m.diagD0[:, j, :], xp[j][:, col(c)], start=True, stop=True)
                pe.wait_ge(parts_done, ONE + b * 6 + 6)

                def row(n, w):
                    for c in range(NCOL):
                        pe.wait_ge(bc_read, ONE + b * (4 * N0) + row_place(n, w) * NCOL + c - 1 + RING)
                        pe.matmul(bc_ps[:, col(c)], m.pick[:, bass.ds((n + w * N0) * P, P)], parts[:, col(c)],
                                  start=True, stop=True).then_inc(bc_done, 1)

                def add_state(n, r, j):
                    pe.wait_ge(ch_done, ONE + (b * N0 + n) * 2 + j + 1 + SLOTS)
                    for c in range(NCOL):
                        mm = pe.matmul(y_ps[j][:, col(c)], m.ident[:], h[2 * r + j][:, col(c)], start=False,
                                       stop=True, skip_group_check=True)
                    mm.then_inc(acc_done, 1)

                row(0, 0)
                for n in range(2):
                    row(n + 1, 0)
                    row(n, 1)
                def step(n, r):
                    row(n + 1, 0)
                    add_state(n - 2, r, 0)
                    row(n, 1)
                    add_state(n - 2, r, 1)

                with pe.Fori(1, N0 // 2 - 1) as i:
                    for r in range(2):
                        step(i * 2 + r, r)
                step(N0 - 2, 0)
                row(N0 - 1, 1)
                for n in range(N0 - 3, N0):
                    for j in range(HALVES):
                        add_state(n, n % 2, j)
                    if n == N0 - 2:
                        for i in range(XPRE + RING, NPRE):
                            project(b, i)
                start_next()

            def finish(b):
                pe.wait_ge(yg_done, ONE + b * 2 + 2)
                for q in range(NCOL):
                    for t in range(COL // P):
                        tok = slice(q * COL + t * P, q * COL + (t + 1) * P)
                        for j in range(HALVES):
                            mm = pe.matmul(bc_ps[:, tok], yg[j][:, tok], m.wo0[:, j, :], start=(j == 0), stop=(j == 1))
                    mm.then_inc(out_done, 1)

            pe.sem_inc(acc_done, SLOTS)
            all_batches(pe, start, body, finish)

        @block.scalar
        def _(act):
            def projected(b, i):
                what, j, c = i // XPRE, i // NCOL % HALVES, i % NCOL
                act.wait_ge(pre_done, ONE + b * NPRE + i + 1)
                act.activation((xp, sz)[what][j][:, col(c)], bank[i % 2][:], ACT.Silu,
                               bias=m.cb0[:, j:j + 1] if what == 0 else 0.0).then_inc(pre_read, 1)

            def start(b):
                act.wait_ge(u0_done, ONE + b)
                act.wait_ge(u1_done, ONE + b)
                for i in range(XPRE):
                    projected(b, i)

            def body(b, start_next):
                act.wait_ge(out_done, ONE + b * 2)
                for j in range(HALVES):
                    act.wait_ge(dmm_done, ONE + b * 2 + j + 1)
                    act.activation(ab[j][:], y_ps[j][:], ACT.Abs, bias=m.bdt0[:, j:j + 1]).then_inc(sp_step, 1)
                act.wait_ge(ch_done, ONE + b * UNITS + SLOTS)
                for j in range(HALVES):
                    act.wait_ge(sp_step, ONE + b * 4 + j + 1)
                    act.activation(lt[j][:], ab[j][:], ACT.Exp, scale=-1.0).then_inc(sp_step, 1)
                for j in range(HALVES):
                    act.wait_ge(sp_step, ONE + b * 4 + j + 3)
                    act.activation(lt[j][:], lt[j][:], ACT.Ln, bias=1.0).then_inc(ln_done, 1)
                act.wait_ge(delta_done, ONE + b * 2 + 2)

                def read_row(n, r, w):
                    act.wait_ge((bu_done, ch_done)[w], ONE + (b * N0 + n) * 2 + 2)
                    for c in range(NCOL):
                        act.wait_ge(bc_done, ONE + b * (4 * N0) + row_place(n, w) * NCOL + c + 1)
                        act.activation((bsb, csb)[w][r][:, col(c)], bc_ps[:, col(c)], ACT.Copy
                                       ).then_inc(bc_read, 1)

                def decays(n, r, j):
                    act.wait_ge(scan_done, ONE + (b * N0 + n) * 2 + j + 1)
                    act.sem_inc(m.passed, 1)
                    act.activation(decay[2 * r + j][:], delta[j][:], ACT.Exp,
                                   scale=m.negA0[:, j, bass.ds(n, 1)]).then_inc(decay_done, 1)

                def step(n, r):
                    read_row(n + 1, 1 - r, 0)
                    decays(n, r, 0)
                    read_row(n, r, 1)
                    decays(n, r, 1)

                read_row(0, 0, 0)
                step(0, 0)
                step(1, 1)
                with act.Fori(1, N0 // 2 - 1) as i:
                    for r in range(2):
                        step(i * 2 + r, r)
                step(N0 - 2, 0)
                decays(N0 - 1, 1, 0)
                read_row(N0 - 1, 1, 1)
                decays(N0 - 1, 1, 1)
                for i in range(XPRE, NPRE):
                    projected(b, i)
                start_next()

            act.sem_inc(pre_read, RING)
            act.sem_inc(bc_read, RING)
            all_batches(act, start, body, lambda b: None)

        @block.gpsimd
        def _(pool):
            pool.sem_inc(bu_done, SLOTS)
            with pool.Fori(0, NBATCH) as b:
                pool.wait_ge(delta_done, ONE + b * 2 + 2)
                pool.tensor_tensor(u[1][:], delta[1][:], xp[1][:], ALU.mult).then_inc(u1_done, 1)
                def products(n, r):
                    q = (b * N0 + n) * 2
                    pool.wait_ge(bc_read, ONE + b * (4 * N0) + row_place(n, 0) * NCOL + NCOL + RING)
                    for j in range(HALVES):
                        pool.wait_ge(scan_done, ONE + q + j - 3 + DECAYS)
                        pool.tensor_tensor(bu[2 * r + j][:], u[j][:], bsb[r][:], ALU.mult).then_inc(bu_done, 1)

                pool.wait_ge(u0_done, ONE + b + 1)
                pool.wait_ge(u1_done, ONE + b + 1)
                products(0, 0)
                products(1, 1)
                with pool.Fori(1, N0 // 2) as i:
                    for r in range(2):
                        products(i * 2 + r, r)

        @block.vector
        def _(dve):
            def start(b):
                for c in range(NCOL):
                    dve.wait_ge(low_done, ONE + b * 2 + c + 1)
                    dve.tensor_copy(low[:, col(c)], bank[c][0:RANK, :]).then_inc(low_read, 1)

            def body(b, start_next):
                for j in range(HALVES):
                    dve.wait_ge(sp_step, ONE + b * 4 + j + 1)
                    dve.tensor_scalar(delta[j][:], y_ps[j][:], m.bdt0[:, j:j + 1], 0.0, ALU.add,
                                      ALU.max).then_inc(relu_done, 1)
                for c in range(NCOL):
                    k = b * 6 + 3 * c
                    dve.wait_ge(split_done, ONE + b * 2 + c + 1)
                    dve.tensor_copy(hi[:], bc_ps[0:3 * G, col(c)]).then_inc(split_step, 1)
                    dve.wait_ge(split_step, ONE + k + 1)
                    dve.tensor_tensor(rest[:], bc_ps[0:3 * G, col(c)], hi[:], ALU.subtract).then_inc(split_step, 1)
                    dve.tensor_copy(parts[0:G, col(c)], hi[0:G, :]).then_inc(parts_done, 1)
                    dve.wait_ge(split_step, ONE + k + 2)
                    dve.tensor_copy(mid[:], rest[:]).then_inc(split_step, 1)
                    dve.wait_ge(split_step, ONE + k + 3)
                    dve.tensor_copy(parts[G:2 * G, col(c)], mid[G:2 * G, :]).then_inc(parts_done, 1)
                    dve.tensor_tensor(parts[2 * G:3 * G, col(c)], rest[2 * G:3 * G, :], mid[2 * G:3 * G, :],
                                      ALU.subtract).then_inc(parts_done, 1)
                for j in range(HALVES):
                    dve.wait_ge(ln_done, ONE + b * 2 + j + 1)
                    dve.wait_ge(relu_done, ONE + b * 2 + j + 1)
                    dve.tensor_tensor(delta[j][:], delta[j][:], lt[j][:], ALU.add).then_inc(delta_done, 1)
                dve.wait_ge(delta_done, ONE + b * 2 + 1)
                dve.tensor_tensor(u[0][:], delta[0][:], xp[0][:], ALU.mult).then_inc(u0_done, 1)

                def scan(n, r, j):
                    q = (b * N0 + n) * 2 + j
                    dve.wait_ge(bu_done, ONE + q + 1 + SLOTS)
                    dve.wait_ge(decay_done, ONE + q + 1)
                    dve.wait_ge(acc_done, ONE + q - 3 + SLOTS)
                    dve.tensor_tensor_scan(h[2 * r + j][:], decay[2 * r + j][:], bu[2 * r + j][:], 0.0, ALU.mult, ALU.add
                                           ).then_inc(scan_done, 1)

                def times_c(n, r, j):
                    q = (b * N0 + n) * 2 + j
                    dve.wait_ge(scan_done, ONE + q + 1 + DECAYS)
                    dve.wait_ge(bc_read, ONE + b * (4 * N0) + row_place(n, 1) * NCOL + NCOL + RING)
                    hs = h[2 * r + j]
                    dve.tensor_tensor(hs[:], hs[:], csb[r][:], ALU.mult).then_inc(ch_done, 1)

                scan(0, 0, 0)
                with dve.Fori(0, N0 // 2 - 1) as i:
                    for r in range(2):
                        n = i * 2 + r
                        scan(n, r, 1)
                        times_c(n, r, 0)
                        scan(n + 1, 1 - r, 0)
                        times_c(n, r, 1)
                for n in (N0 - 2, N0 - 1):
                    scan(n, n % 2, 1)
                    times_c(n, n % 2, 0)
                    if n + 1 < N0:
                        scan(n + 1, 1, 0)
                    times_c(n, n % 2, 1)
                dve.wait_ge(acc_done, ONE + b * UNITS + UNITS + SLOTS)
                for j in range(HALVES):
                    dve.wait_ge(pre_read, ONE + b * NPRE + XPRE + (j + 1) * NCOL + RING)
                    dve.tensor_tensor(yg[j][:], y_ps[j][:], sz[j][:], ALU.mult).then_inc(yg_done, 1)
                start_next()

            def finish(b):
                for q in range(NCOL):
                    dve.wait_ge(out_done, ONE + b * 2 + q + 1)
                    src = bc_ps[:, col(q)].rearrange("p (t d) -> p t d", t=4)
                    tmp = h[2][:, col(q)].rearrange("p (t d) -> p t d", t=4)
                    dve.tensor_tensor(tmp, src, m.gate[:, 0, 0, bass.ds(b, 1), :].broadcast_to([P, 4, P]),
                                      ALU.mult).then_inc(gated, 1)
                    dve.wait_ge(gated, ONE + b * 2 + q + 1)
                    xs = m.X[:, bass.ds(b * BT + 4 * q, 4), :]
                    dve.tensor_tensor(xs, xs, tmp, ALU.add).then_inc(x_done, 1)

            dve.sem_inc(scan_done, DECAYS)
            dve.sem_inc(ch_done, SLOTS)
            all_batches(dve, start, body, finish)
            dve.wait_ge(x_done, ONE + 2 * NBATCH)


def route(nc, a, m, layer):
    choices = CHOICES[layer]
    slots = SLOTS[layer]
    tag = f"r{layer}_"
    with ExitStack() as ctx:
        sb = lambda name, shape, dt=F32: ctx.enter_context(nc.sbuf_tensor(tag + name, shape, dt))
        sem = lambda name: m.kept.enter_context(nc.semaphore(tag + name))
        lg_ps = ctx.enter_context(nc.psum_tensor(tag + "lg_ps", [P, TILES * NE], F32))
        ahead_ps = ctx.enter_context(nc.psum_tensor(tag + "ahead_ps", [P, TILES * NE], F32))
        total_ps = ctx.enter_context(nc.psum_tensor(tag + "total_ps", [P, TILES * NE], F32))
        R = [P, TILES, NE]
        lg, chosen, keep, val, ex, upto, place = (
            sb(n, R) for n in ("lg", "chosen", "keep", "val", "ex", "upto", "place"))
        onehot = [sb(f"onehot{k}", R) for k in range(choices)]
        mx, first = (sb(n, [P, TILES]) for n in ("mx", "first"))
        past = sb("past", [P, NE, TILES])
        used, upto_e, start = (sb(n, [P, NE]) for n in ("used", "upto_e", "start"))
        past_tile = sb("past_tile", [1, slots, NE])
        owner = sb("owner", [1, slots])
        logits_done, step, near_done, exp_done, chosen_done, counted, placed, sent, loaded = (
            sem(n) for n in "logits_done step near_done exp_done chosen_done counted placed sent loaded".split())
        block = ctx.enter_context(nc.Block())
        router = m.router if layer == 0 else m.gate1
        over = lambda t: t[:].unsqueeze(2).broadcast_to(R)
        numbers = m.count[:, 0:NE].unsqueeze(1).broadcast_to(R)

        @block.tensor
        def _(pe):
            for t in range(TILES):
                c0 = PAD + t % BT * P
                mm = pe.matmul(lg_ps[:, t * NE:(t + 1) * NE], m.hT[:, t // BT, c0:c0 + P], router[:],
                               start=True, stop=True)
            mm.then_inc(logits_done, 1)
            pe.wait_ge(chosen_done, 1)
            flat = chosen[:].rearrange("p t e -> p (t e)")
            pe.matmul(ahead_ps[:], m.before[:], flat, start=True, stop=True)
            pe.matmul(total_ps[:], m.ones[:], flat, start=True, stop=True).then_inc(counted, 1)

        @block.scalar
        def _(act):
            if layer == 0:
                for k in range(choices):
                    act.wait_ge(near_done, k + 1)
                    act.activation(ex[:], val[:], ACT.Exp).then_inc(exp_done, 1)

        @block.vector
        def _(dve):
            steps = [0]

            def then(ins):
                steps[0] += 1
                ins.then_inc(step, 1)
                dve.wait_ge(step, steps[0])

            def first_of_max(scores, hot):
                then(dve.tensor_reduce(mx[:], scores[:], AX, ALU.max))
                then(dve.tensor_tensor(val[:], scores[:], over(mx), ALU.is_lt))
                then(dve.scalar_tensor_tensor(val[:], val[:], float(NE), numbers, ALU.mult, ALU.add))
                then(dve.tensor_reduce(first[:], val[:], AX, ALU.min))
                then(dve.tensor_tensor(hot[:], numbers, over(first), ALU.is_equal))

            dve.wait_ge(logits_done, 1)
            lgv = lg_ps[:].rearrange("p (t e) -> p t e", t=TILES)
            if layer == 1:
                then(dve.tensor_tensor(lg[:], lgv, m.gb1[:, 0, :].unsqueeze(1).broadcast_to(R), ALU.add))
                first_of_max(lg, onehot[0])
                dve.tensor_copy(chosen[:], onehot[0][:]).then_inc(chosen_done, 1)
            else:
                then(dve.tensor_copy(lg[:], lgv))
                first_of_max(lg, onehot[0])
                for k in range(choices):
                    if k == 1:
                        then(dve.scalar_tensor_tensor(ex[:], onehot[0][:], -3.0e38, lg[:], ALU.mult, ALU.add))
                        first_of_max(ex, onehot[1])
                    then(dve.scalar_tensor_tensor(keep[:], lg[:], -1.0, lg[:], ALU.mult, ALU.max))
                    then(dve.tensor_tensor(keep[:], keep[:], over(mx), ALU.max))
                    then(dve.tensor_tensor(val[:], over(mx), lg[:], ALU.subtract))
                    then(dve.scalar_tensor_tensor(keep[:], keep[:], 0.02, val[:], ALU.mult, ALU.is_ge))
                    if k == 1:
                        then(dve.scalar_tensor_tensor(keep[:], onehot[0][:], 0.0, keep[:], ALU.is_equal, ALU.mult))
                    dve.tensor_scalar(val[:], val[:], -1.0, 0.0, ALU.mult, ALU.min).then_inc(near_done, 1)
                    dve.wait_ge(exp_done, k + 1)
                    then(dve.tensor_tensor(ex[:], ex[:], keep[:], ALU.mult))
                    then(dve.tensor_reduce(first[:], ex[:], AX, ALU.add))
                    then(dve.reciprocal(m.weight[:, k, :], first[:]))
                dve.tensor_tensor(chosen[:], onehot[0][:], onehot[1][:], ALU.add).then_inc(chosen_done, 1)
            dve.wait_ge(counted, 1)
            total = total_ps[:].rearrange("p (t e) -> p t e", t=TILES)
            for e in range(NE):
                ins = dve.tensor_tensor_scan(upto[:, :, e], m.ones[:, 0:TILES], total[:, :, e], 0.0, ALU.mult, ALU.add)
            then(ins)
            then(dve.tensor_tensor(past[:], upto[:, TILES - 1, :].unsqueeze(2).broadcast_to([P, NE, TILES]),
                                   m.count128[:].unsqueeze(1).broadcast_to([P, NE, TILES]), ALU.is_gt))
            then(dve.tensor_reduce(used[:], past[:], AX, ALU.add))
            then(dve.tensor_tensor_scan(upto_e[:], m.ones[:, 0:NE], used[:], 0.0, ALU.mult, ALU.add))
            then(dve.tensor_tensor(start[:], upto_e[:], used[:], ALU.subtract))
            then(dve.tensor_scalar(start[:], start[:], float(P), None, ALU.mult))
            then(dve.tensor_tensor(place[:], upto[:], total, ALU.subtract))
            then(dve.tensor_tensor(place[:], place[:], ahead_ps[:].rearrange("p (t e) -> p t e", t=TILES), ALU.add))
            then(dve.tensor_tensor(place[:], place[:], start[:].unsqueeze(1).broadcast_to(R), ALU.add))
            for k in range(choices):
                then(dve.tensor_tensor(val[:], onehot[k][:], place[:], ALU.mult))
                then(dve.tensor_reduce(first[:], val[:], AX, ALU.add))
                dve.tensor_copy(m.where[:, k, :], first[:]).then_inc(placed, 1)
            S = [1, slots, NE]
            then(dve.tensor_tensor(past_tile[:], m.count[0:1, 0:slots].unsqueeze(2).broadcast_to(S),
                                   upto_e[0:1, :].unsqueeze(1).broadcast_to(S), ALU.is_ge))
            then(dve.tensor_reduce(owner[:], past_tile[:], AX, ALU.add))
            then(dve.tensor_scalar(owner[:], owner[:], float(NE - 1), None, ALU.min))
            then(dve.tensor_copy(m.owner[:, 0:slots], owner[:]))

        @block.gpsimd
        def _(pool):
            for k in range(choices):
                pool.wait_ge(placed, k + 1)
                for t in range(TILES):
                    pool.indirect_dma_start(m.xs[layer], bass.IndirectOffsetOnAxis(ap=m.where[:, k, t:t + 1], axis=0),
                                            m.rows[:, t, :], None).then_inc(sent, 16)
            pool.wait_ge(sent, 16 * choices * TILES)

        @block.sync
        def _(sp):
            if layer == 0:
                sp.wait_ge(m.late, LATE[0])
            else:
                sp.dma_start(m.b1[:], a["L1_ffn_b1"].partition_broadcast(P)).then_inc(loaded, 16)
                sp.dma_start(m.b2[:], a["L1_ffn_b2"].partition_broadcast(P)).then_inc(loaded, 16)
                sp.wait_ge(loaded, 32)
                sp.wait_ge(m.late, LATE[1])


def sorted_experts(nc, m, layer):
    slots = SLOTS[layer]
    FB = (F0 if layer == 0 else F1) // P
    FW = FB * P
    GROUP = 4
    BODY = 2 * GROUP
    turns = slots // BODY
    tag = f"s{layer}_"
    with ExitStack() as ctx:
        sb = lambda name, shape, dt=F32: ctx.enter_context(nc.sbuf_tensor(tag + name, shape, dt))
        ps = lambda name: [ctx.enter_context(nc.psum_tensor(f"{tag}{name}{i}", [P, COL], F32)) for i in range(2)]
        xt_ps, up_ps, ht_ps, out_ps = ps("xt_ps"), ps("up_ps"), ps("ht_ps"), ps("out_ps")
        rows = [sb(f"rows{i}", [P, GROUP, P]) for i in range(2)]
        outs = [sb(f"outs{i}", [P, GROUP, P]) for i in range(2)]
        xt = [sb(f"xt{i}", [P, P]) for i in range(2)]
        act_g = [sb(f"act_g{i}", [P, FW]) for i in range(2)]
        wide = [sb(f"wide{i}", [P, FW]) for i in range(2)]
        ht = [sb(f"ht{i}", [P, FW]) for i in range(2)]
        (xt_done, xt_read, up_done, act_done, wide_done, ht_done, ht_read, out_done, out_read, loaded0, loaded1,
         stored0, stored1) = (m.sems["so_" + n] for n in SORTED_SEMS.split())
        loaded, stored = (loaded0, loaded1), (stored0, stored1)
        before = layer * SLOTS[0]
        before_dma = 16 * (before // BODY)
        block = ctx.enter_context(nc.Block())
        w_up = m.wgu if layer == 0 else m.w1
        w_down = m.wdown if layer == 0 else m.w2

        def wait(engine, semaphore, count, j):
            if not (isinstance(j, int) and j + count < 1):
                engine.wait_ge(semaphore, before + j + count)

        @block.sync
        def _(sp):
            def load(g, s, slot_used):
                if slot_used:
                    sp.wait_ge(xt_done, before + g * GROUP - GROUP)
                sp.dma_start(rows[s][:], m.xs[layer][bass.ds(g * (GROUP * P), GROUP * P), :].rearrange(
                    "(q p) d -> p q d", p=P)).then_inc(loaded[s], 16)
            load(0, 0, False)
            load(1, 1, False)
            with sp.Fori(1, turns) as i:
                for s in range(2):
                    load(i * 2 + s, s, True)

        @block.gpsimd
        def _(pool):
            with pool.Fori(0, turns) as i:
                for s in range(2):
                    g = i * 2 + s
                    pool.wait_ge(out_read, before + g * GROUP + GROUP)
                    pool.dma_start(m.ys[layer][bass.ds(g * (GROUP * P), GROUP * P), :].rearrange(
                        "(q p) d -> p q d", p=P), outs[s][:]).then_inc(stored[s], 16)
            for s in range(2):
                pool.wait_ge(stored[s], before_dma + 16 * turns)

        @block.tensor
        def _(pe):
            def turn_rows(j, k):
                if k % GROUP == 0:
                    pe.wait_ge(loaded[k // GROUP], before_dma + (j - k + BODY) * (16 // BODY))
                wait(pe, xt_read, -1, j)
                pe.transpose(xt_ps[k % 2][:, 0:P], rows[k // GROUP][:, k % GROUP, :], m.ident[:]).then_inc(xt_done, 1)

            def widen(j, k):
                e = pe.value_load(m.owner[0:1, bass.ds(j, 1)], min_val=0, max_val=NE - 1)
                wait(pe, wide_done, -1, j)
                wait(pe, xt_read, 1, j)
                pe.matmul(up_ps[k % 2][:], xt[k % 2][:], w_up[:, bass.ds(e, 1), :].rearrange("p o f -> p (o f)"),
                          start=True, stop=True).then_inc(up_done, 1)

            def turn_wide(j, k):
                wait(pe, ht_read, -1, j)
                wait(pe, wide_done, 1, j)
                for f in range(FB):
                    tr = pe.transpose(ht_ps[k % 2][:, f * P:(f + 1) * P], wide[k % 2][:, f * P:(f + 1) * P], m.ident[:])
                tr.then_inc(ht_done, 1)

            def narrow(j, k):
                e = pe.value_load(m.owner[0:1, bass.ds(j, 1)], min_val=0, max_val=NE - 1)
                wait(pe, out_read, -1, j)
                wait(pe, ht_read, 1, j)
                for f in range(FB):
                    mm = pe.matmul(out_ps[k % 2][:, 0:P], ht[k % 2][:, f * P:(f + 1) * P],
                                   w_down[:, bass.ds(e, 1), f, :].rearrange("p o d -> p (o d)"),
                                   start=(f == 0), stop=(f == FB - 1))
                mm.then_inc(out_done, 1)

            stages = (turn_rows, widen, turn_wide, narrow)

            def step(base, k, first=0, last=len(stages) - 1):
                for n in range(first, last + 1):
                    stages[n](base + k - n, (k - n) % BODY)

            for k in range(BODY):
                step(0, k, last=min(k, len(stages) - 1))
            with pe.Fori(1, turns) as i:
                for k in range(BODY):
                    step(i * BODY, k)
            for k in range(len(stages) - 1):
                step(slots, k, first=k + 1)

        @block.scalar
        def _(act):
            def evacuate_rows(j, k):
                wait(act, up_done, -1, j)
                wait(act, xt_done, 1, j)
                act.activation(xt[k % 2][:], xt_ps[k % 2][:, 0:P], ACT.Copy).then_inc(xt_read, 1)

            def silu(j, k):
                if layer == 0:
                    wait(act, wide_done, -1, j)
                    wait(act, up_done, 1, j)
                    act.activation(act_g[k % 2][:], up_ps[k % 2][:, 0:FW], ACT.Silu).then_inc(act_done, 1)

            def evacuate_wide(j, k):
                wait(act, out_done, -1, j)
                wait(act, ht_done, 1, j)
                act.activation(ht[k % 2][:], ht_ps[k % 2][:, 0:FW], ACT.Copy if layer == 0 else ACT.Relu
                               ).then_inc(ht_read, 1)

            stages = (evacuate_rows, silu, evacuate_wide)

            def step(base, k, first=0, last=len(stages) - 1):
                for n in range(first, last + 1):
                    stages[n](base + k - n, (k - n) % BODY)

            for k in range(BODY):
                step(0, k, last=min(k, len(stages) - 1))
            with act.Fori(1, turns) as i:
                for k in range(BODY):
                    step(i * BODY, k)
            for k in range(len(stages) - 1):
                step(slots, k, first=k + 1)

        @block.vector
        def _(dve):
            def widened(j, k):
                if layer == 0:
                    wait(dve, ht_done, -1, j)
                    wait(dve, act_done, 1, j)
                    dve.tensor_tensor(wide[k % 2][:], up_ps[k % 2][:, FW:2 * FW], act_g[k % 2][:],
                                      ALU.mult).then_inc(wide_done, 1)
                else:
                    e = dve.value_load(m.owner[0:1, bass.ds(j, 1)], min_val=0, max_val=NE - 1)
                    wait(dve, ht_done, -1, j)
                    wait(dve, up_done, 1, j)
                    dve.tensor_tensor(wide[k % 2][:], up_ps[k % 2][:], m.b1[:, bass.ds(e * F1, F1)],
                                      ALU.add).then_inc(wide_done, 1)

            def none(j, k):
                pass

            def narrowed(j, k):
                dst = outs[k // GROUP][:, k % GROUP, :]
                if layer == 1:
                    e = dve.value_load(m.owner[0:1, bass.ds(j, 1)], min_val=0, max_val=NE - 1)
                if k % GROUP == 0 and not (isinstance(j, int) and j < BODY):
                    dve.wait_ge(stored[k // GROUP], before_dma + (j - k) * (16 // BODY))
                wait(dve, out_done, 1, j)
                if layer == 0:
                    dve.tensor_copy(dst, out_ps[k % 2][:, 0:P]).then_inc(out_read, 1)
                else:
                    dve.tensor_tensor(dst, out_ps[k % 2][:, 0:P], m.b2[:, bass.ds(e * P, P)], ALU.add
                                      ).then_inc(out_read, 1)

            stages = (widened, none, narrowed)

            def step(base, k, first=0, last=len(stages) - 1):
                for n in range(first, last + 1):
                    stages[n](base + k - n, (k - n) % BODY)

            for k in range(BODY):
                step(0, k, last=min(k, len(stages) - 1))
            with dve.Fori(1, turns) as i:
                for k in range(BODY):
                    step(i * BODY, k)
            for k in range(len(stages) - 1):
                step(slots, k, first=k + 1)


def combine(nc, m, layer):
    choices = CHOICES[layer]
    GROUP = 4
    GROUPS = TILES // GROUP
    tag = f"c{layer}_"
    with ExitStack() as ctx:
        sb = lambda name, shape, dt=F32: ctx.enter_context(nc.sbuf_tensor(tag + name, shape, dt))
        sem = lambda name: m.kept.enter_context(nc.semaphore(tag + name))
        BUFFERS = 3
        y = [[sb(f"y{i}_{k}", [P, GROUP, P]) for k in range(choices)] for i in range(BUFFERS)]
        fetched = [sem(f"fetched{i}") for i in range(BUFFERS)]
        summed, x_done, stored = sem("summed"), sem("x_done"), sem("stored")
        block = ctx.enter_context(nc.Block())
        PER = 3 if choices == 2 else 1

        @block.gpsimd
        def _(pool):
            for g in range(GROUPS):
                if g >= BUFFERS:
                    pool.wait_ge(x_done, g - BUFFERS + 1)
                for k in range(choices):
                    for t in range(GROUP):
                        pool.indirect_dma_start(y[g % BUFFERS][k][:, t, :], None, m.ys[layer], bass.IndirectOffsetOnAxis(
                            ap=m.where[:, k, g * GROUP + t:g * GROUP + t + 1], axis=0)).then_inc(fetched[g % BUFFERS], 16)

        @block.vector
        def _(dve):
            n = [0]

            def then(ins):
                n[0] += 1
                ins.then_inc(summed, 1)
                dve.wait_ge(summed, n[0])

            for g in range(GROUPS):
                dve.wait_ge(fetched[g % BUFFERS], 16 * GROUP * choices * (g // BUFFERS + 1))
                ys = y[g % BUFFERS]
                tiles = slice(g * GROUP, (g + 1) * GROUP)
                over = lambda k: m.weight[:, k, tiles].unsqueeze(2).broadcast_to([P, GROUP, P])
                if choices == 2:
                    for k in range(2):
                        then(dve.tensor_tensor(ys[k][:], ys[k][:], over(k), ALU.mult))
                    then(dve.tensor_tensor(ys[0][:], ys[0][:], ys[1][:], ALU.add))
                then(dve.tensor_tensor(ys[0][:], ys[0][:], m.gate[:, layer, 1, g // 2, :].unsqueeze(1).broadcast_to(
                    [P, GROUP, P]), ALU.mult))
                dve.tensor_tensor(m.X[:, tiles, :], m.X[:, tiles, :], ys[0][:], ALU.add).then_inc(x_done, 1)

        @block.sync
        def _(sp):
            if layer == 1:
                for g in range(GROUPS):
                    sp.wait_ge(x_done, g + 1)
                    sp.dma_start(m.out[g // 2, g % 2 * COL:(g % 2 + 1) * COL, :].rearrange("(t p) d -> p t d", p=P),
                                 m.X[:, g * GROUP:(g + 1) * GROUP, :]).then_inc(stored, 16)
                sp.wait_ge(stored, 16 * GROUPS)


def ssd(nc, m):
    with ExitStack() as ctx:
        sb = lambda name, shape, dt=F32: ctx.enter_context(nc.sbuf_tensor("ss_" + name, shape, dt))
        two = lambda name, shape: [sb(f"{name}{i}", shape) for i in range(2)]
        sem = lambda name: m.sems["ss_" + name]
        psum = lambda name: ctx.enter_context(nc.psum_tensor("ss_" + name, [P, COL], F32))
        pre = [psum("spre0"), psum("spre1")]
        cs_ps, tr_ps, st_ps, y_ps, o_ps, g_ps = (psum(n) for n in "cs_ps tr_ps st_ps y_ps o_ps g_ps".split())
        NB = COL // P
        xbc = [sb(f"xbc{i}", [P, SEQ]) for i in range(NB)]
        sz = [sb(f"ssz{i}", [P, SEQ]) for i in range(HALVES)]
        dtT, dte, dtl = (sb(n, [HEADS, SEQ]) for n in ("dtT", "dte", "dtl"))
        dt = sb("dt", [P, BT, HEADS])
        dA = sb("dA", [P, BT, HEADS])
        outs = sb("outs", [P, TILES, P + 1])
        ss = sb("ss", [P, TILES])
        H4 = [P, HEADS, P]
        csc = sb("csc", [P, HEADS])
        seg = sb("seg", H4)
        dec, cdec, mm_sb, cts = (two(n, H4) for n in ("dec", "cdec", "mm_sb", "cts"))
        last, lastx = sb("last", [P, HEADS]), sb("lastx", [P, HEADS])
        gm, bt = two("gm", [P, P]), two("bt", [P, P])
        xdt, xdd, S = (two(n, [P, HEADS, HD]) for n in ("xdt", "xdd", "S"))
        stats = sb("stats", [P, TILES, 6])
        mean, var, tmp = (sb(n, [P, TILES]) for n in ("mean", "var", "tmp"))
        yv, yq = two("yv", [P, HALVES, P]), two("yq", [P, HALVES, P])
        (proj_done, proj_read, dt_done, dt_step, dt_ready, dtt_done, dtt_read, dA_done, cs_done, tr_done,
         csc_done, seg_done, dec_done, cdec_done, lastx_done, gm_done, m_done, cts_done, xdt_done, xdd_done,
         bt_done, y_done, st_done, s_done, s_step, yd_done, yg_done, yq_done, o_done,
         dtl_done, last_done, oc_done, fin, sq_done, tail_step, h_step, norm_done, added) = (sem(n) for n in SSD_SEMS.split())
        block = ctx.enter_context(nc.Block())
        PIECES = NB + HALVES
        NPRE = PIECES * NCOL
        UPDATES = BT - 1
        assert NCOL == 2
        col = lambda c: slice(c * COL, (c + 1) * COL)
        tok = lambda t: slice(t * P, (t + 1) * P)
        four = lambda t: t.unsqueeze(1).broadcast_to(H4)
        spread = lambda v: v.unsqueeze(2).broadcast_to([P, HEADS, HD])
        flat = lambda t: t[:].rearrange("p h d -> p (h d)")
        tiles = lambda b, t: ONE + b * BT + t
        freed = lambda b, t: ONE + b * BT + max(t - 1, 0)
        updates = lambda b, t: ONE + b * UPDATES + t
        upfreed = lambda b, t: ONE + b * UPDATES + max(t - 1, 0)
        states = lambda b, t: ONE + b * UPDATES + max(t - 1, 0)

        def pipeline(b, front, middle, back, now=None, ahead=None):
            for t in range(BT):
                front(b, t)
                if t == 0:
                    now(b)
                if t >= 1:
                    middle(b, t - 1)
                if t >= 2:
                    back(b, t - 2)
            ahead(0)
            middle(b, BT - 1)
            back(b, BT - 2)
            ahead(1)
            back(b, BT - 1)
            ahead(2)

        def all_batches(engine, front, middle, back, now, ahead):
            for part in range(3):
                ahead(0, part)
            with engine.Fori(0, NBATCH - 1) as b:
                pipeline(b, front, middle, back, now, lambda part: ahead(b + 1, part))
            pipeline(NBATCH - 1, front, middle, back, now, lambda part: None)

        @block.tensor
        def _(pe):
            def project(b, c, j):
                i = c * PIECES + j
                if i == 0 or i == 1:
                    pe.wait_ge(dt_step, ONE + b * 4 + i + 1)
                if i == PIECES:
                    pe.wait_ge(dtt_read, ONE + b + 1)
                pe.wait_ge(proj_read, ONE + b * NPRE + i + 1)
                if not isinstance(b, int):
                    pe.sem_inc(m.passed, 1)
                if j < NB:
                    for k in range(TAPS):
                        mm = pe.matmul(pre[i % 2][:], m.wc1[:, k, j * P:(j + 1) * P],
                                       m.hT[:, bass.ds(b, 1), c * COL + k:c * COL + k + COL],
                                       start=(k == 0), stop=(k == TAPS - 1))
                else:
                    mm = pe.matmul(pre[i % 2][:], m.wz1[:, (j - NB) * P:(j - NB + 1) * P],
                                   m.hT[:, bass.ds(b, 1), c * COL + PAD:c * COL + PAD + COL],
                                   start=True, stop=True)
                mm.then_inc(proj_done, 1)

            def now(b):
                for j in range(PIECES):
                    project(b, 1, j)

            def ahead(b, part):
                if part == 0:
                    pe.wait_ge(proj_read, ONE + b * NPRE + 2)
                    if not isinstance(b, int):
                        pe.sem_inc(m.passed, 1)
                    for c in range(NCOL):
                        mm = pe.matmul(pre[c][0:HEADS, :], m.wdt1[:],
                                       m.hT[:, bass.ds(b, 1), c * COL + PAD:c * COL + PAD + COL],
                                       start=True, stop=True)
                    mm.then_inc(dt_done, 1)
                if part < 2:
                    for j in range(PIECES // 2):
                        project(b, 0, part * (PIECES // 2) + j)
                else:
                    pe.wait_ge(dt_ready, ONE + b + 1)
                    pe.wait_ge(proj_read, ONE + b * NPRE + 2 + PIECES - 1)
                    pe.sem_inc(m.passed, 1)
                    for t in range(BT):
                        tr = pe.transpose(pre[0][:, t * HEADS:(t + 1) * HEADS], dtT[:, tok(t)],
                                          m.ident[0:HEADS, 0:HEADS])
                    tr.then_inc(dtt_done, 1)

            def front(b, t):
                if t == 0:
                    pe.wait_ge(dA_done, ONE + b + 1)
                pe.wait_ge(gm_done, tiles(b, t))
                if t % (BT // 2) == 0:
                    pe.wait_ge(proj_read, ONE + b * NPRE + 2 + (1 + t // (BT // 2)) * PIECES)
                pe.matmul(g_ps[:, 0:P], xbc[2][:, tok(t)], xbc[3][:, tok(t)], start=True, stop=True)
                pe.matmul(g_ps[:, P:P + HEADS], m.tri[:], dA[:, t, :], start=True, stop=True)
                pe.wait_ge(cdec_done, states(b, t))
                pe.wait_ge(seg_done, tiles(b, t))
                for h in range(HEADS):
                    mm = pe.matmul(cs_ps[:, h * P:(h + 1) * P], dA[:, t, h:h + 1].broadcast_to([P, P]), m.tri[:],
                                   start=True, stop=True)
                mm.then_inc(cs_done, 1)
                pe.wait_ge(xdt_done, tiles(b, t))
                pe.wait_ge(bt_done, updates(b, t))
                for j in range(3 if t < UPDATES else 2):
                    tr = pe.transpose(tr_ps[:, j * P:(j + 1) * P], xbc[j][:, tok(t)], m.ident[:])
                tr.then_inc(tr_done, 1)

            def middle(b, t):
                if t < UPDATES:
                    pe.wait_ge(bt_done, updates(b, t) + 1)
                    pe.wait_ge(xdd_done, updates(b, t) + 1)
                    pe.wait_ge(s_done, updates(b, t))
                    pe.matmul(st_ps[:, 0:D_IN], bt[t % 2][:], flat(xdd[t % 2]), start=True, stop=True
                              ).then_inc(st_done, 1)
                pe.wait_ge(xdt_done, tiles(b, t) + 1)
                pe.wait_ge(m_done, tiles(b, t) + 1)
                if t > 0:
                    pe.wait_ge(cts_done, states(b, t) + 1)
                    pe.wait_ge(s_done, updates(b, t))
                pe.wait_ge(yd_done, ONE + (b * BT + t) * 2)
                for h in range(HEADS):
                    dst = y_ps[h % 2 * HD:(h % 2 + 1) * HD, h // 2 * P:(h // 2 + 1) * P]
                    mm = pe.matmul(dst, xdt[t % 2][:, h, :], mm_sb[t % 2][:, h, :], start=True, stop=(t == 0))
                    if t > 0:
                        mm = pe.matmul(dst, S[t % 2][:, h, :], cts[t % 2][:, h, :], start=False, stop=True)
                mm.then_inc(y_done, 1)

            def back(b, t):
                pe.wait_ge(yg_done, ONE + (b * BT + t) * 2 + 2)
                pe.wait_ge(oc_done, tiles(b, t))
                for j in range(HALVES):
                    pe.matmul(o_ps[:, 0:P], yv[t % 2][:, j, :], m.wout1[:, j, :], start=(j == 0), stop=(j == 1))
                pe.wait_ge(yq_done, tiles(b, t) + 1)
                for j in range(HALVES):
                    mm = pe.matmul(o_ps[:, P:P + 1], yq[t % 2][:, j, :], m.ones[:, 0:1], start=(j == 0), stop=(j == 1))
                mm.then_inc(o_done, 1)

            all_batches(pe, front, middle, back, now, ahead)

        @block.scalar
        def _(act):
            def projected(b, c, j):
                i = c * PIECES + j
                act.wait_ge(proj_done, ONE + b * NPRE + i + 1)
                act.activation((xbc + sz)[j][:, col(c)], pre[i % 2][:], ACT.Silu,
                               bias=m.cb1[:, j:j + 1] if j < NB else 0.0).then_inc(proj_read, 1)

            def now(b):
                act.wait_ge(yg_done, ONE + b * BT * 2)
                act.wait_ge(cts_done, updates(b, 0))
                for j in range(PIECES):
                    projected(b, 1, j)

            def ahead(b, part):
                if part == 0:
                    act.wait_ge(dt_done, ONE + b + 1)
                    act.wait_ge(dtt_done, ONE + b)
                    for c in range(NCOL):
                        act.activation(dtT[:, col(c)], pre[c][0:HEADS, :], ACT.Identity, bias=m.dtb1[:]
                                       ).then_inc(dt_step, 1)
                    act.wait_ge(dt_step, ONE + b * 4 + 2)
                    act.activation(dte[:], dtT[:], ACT.Abs).then_inc(dt_step, 1)
                    act.wait_ge(dt_step, ONE + b * 4 + 3)
                    act.activation(dte[:], dte[:], ACT.Exp, scale=-1.0).then_inc(dt_step, 1)
                    act.wait_ge(dt_step, ONE + b * 4 + 4)
                    act.activation(dtl[:], dte[:], ACT.Ln, bias=1.0).then_inc(dtl_done, 1)
                    if not (isinstance(b, int) and b == 0):
                        act.wait_ge(yg_done, ONE + ((b - 1) * BT + BT // 2) * 2)
                        act.wait_ge(cts_done, ONE + (b - 1) * UPDATES + BT // 2 - 1)
                if part < 2:
                    for j in range(PIECES // 2):
                        projected(b, 0, part * (PIECES // 2) + j)

            def front(b, t):
                if t > 0:
                    act.wait_ge(seg_done, tiles(b, t) + 1)
                    act.wait_ge(cts_done, ONE + b * UPDATES + max(t - 2, 0))
                    act.wait_ge(s_done, upfreed(b, t))
                    act.activation(cdec[t % 2][:].rearrange("p h l -> p (h l)"), cs_ps[:], ACT.Exp
                                   ).then_inc(cdec_done, 1)
                if t < UPDATES:
                    act.wait_ge(last_done, updates(b, t) + 1)
                    act.wait_ge(xdd_done, updates(b, t))
                    act.activation(lastx[:], last[:], ACT.Exp).then_inc(lastx_done, 1)
                act.wait_ge(seg_done, tiles(b, t) + 1)
                act.wait_ge(m_done, freed(b, t))
                act.activation(dec[t % 2][:], seg[:], ACT.Exp).then_inc(dec_done, 1)
                if t < UPDATES:
                    act.wait_ge(xdt_done, tiles(b, t) + 1)
                    act.wait_ge(st_done, upfreed(b, t))
                    act.activation(bt[t % 2][:], tr_ps[:, 2 * P:3 * P], ACT.Copy).then_inc(bt_done, 1)

            def middle(b, t):
                act.wait_ge(yg_done, ONE + (b * BT + t) * 2 + 2)
                act.wait_ge(o_done, freed(b, t))
                act.activation(yq[t % 2][:], yv[t % 2][:], ACT.Square).then_inc(yq_done, 1)

            def back(b, t):
                act.wait_ge(o_done, tiles(b, t) + 1)
                if not isinstance(b, int):
                    act.sem_inc(m.passed, 1)
                act.activation(outs[:, bass.ds(b * BT + t, 1), :], o_ps[:, 0:P + 1].rearrange("p (o c) -> p o c", o=1),
                               ACT.Copy).then_inc(oc_done, 1)

            act.sem_inc(proj_read, 2)
            all_batches(act, front, middle, back, now, ahead)
            act.wait_ge(fin, ONE + 1)
            act.activation(ss[:], ss[:], ACT.Sqrt).then_inc(sq_done, 1)
            act.wait_ge(fin, ONE + 2)
            act.activation(var[:], var[:], ACT.Sqrt).then_inc(sq_done, 1)
            act.wait_ge(fin, ONE + 3)
            act.sem_inc(m.passed, 1)
            with act.Fori(0, NBATCH) as b:
                for i in range(BT):
                    one = bass.ds(b * BT + i, 1)
                    act.activation(outs[:, one, 0:P], outs[:, one, 0:P], ACT.Identity, bias=mean[:, one],
                                   scale=var[:, one]).then_inc(norm_done, 1)

        @block.gpsimd
        def _(pool):
            for b in range(NBATCH):
                x = m.X[:, b * BT:(b + 1) * BT, :]
                pool.tensor_tensor(x, x, m.lnb_gate[:, b, :].unsqueeze(1).broadcast_to([P, BT, P]), ALU.add
                                   ).then_inc(added, 1)
            with pool.Fori(0, NBATCH) as b:
                for t in range(BT):
                    if t > 0:
                        pool.wait_ge(cdec_done, states(b, t) + 1)
                        pool.wait_ge(y_done, freed(b, t))
                        pool.tensor_tensor(cts[t % 2][:], cdec[t % 2][:], four(xbc[3][:, tok(t)]), ALU.mult
                                           ).then_inc(cts_done, 1)
                    pool.wait_ge(gm_done, tiles(b, t) + 1)
                    pool.wait_ge(dec_done, tiles(b, t) + 1)
                    pool.wait_ge(y_done, freed(b, t))
                    pool.tensor_tensor(mm_sb[t % 2][:], dec[t % 2][:], four(gm[t % 2][:]), ALU.mult
                                       ).then_inc(m_done, 1)

        @block.vector
        def _(dve):
            def now(b):
                pass

            def ahead(b, part):
                if part == 0:
                    dve.wait_ge(dt_step, ONE + b * 4 + 4)
                    dve.wait_ge(dtl_done, ONE + b + 1)
                    dve.scalar_tensor_tensor(dtT[:], dtT[:], 0.0, dtl[:], ALU.max, ALU.add).then_inc(dt_ready, 1)
                if part == 2:
                    dve.wait_ge(dtt_done, ONE + b + 1)
                    dve.tensor_copy(dt[:], pre[0][:, 0:BT * HEADS].rearrange("p (t h) -> p t h", h=HEADS)
                                    ).then_inc(dtt_read, 1)
                    dve.wait_ge(dtt_read, ONE + b + 1)
                    dve.tensor_tensor(dA[:], dt[:], m.negA1[:].unsqueeze(1).broadcast_to([P, BT, HEADS]),
                                      ALU.mult).then_inc(dA_done, 1)

            def front(b, t):
                cs = cs_ps[:].rearrange("p (h l) -> p h l", h=HEADS)
                dve.wait_ge(cs_done, tiles(b, t) + 1)
                dve.tensor_copy(csc[:], g_ps[:, P:P + HEADS]).then_inc(csc_done, 1)
                dve.wait_ge(csc_done, tiles(b, t) + 1)
                if t < UPDATES:
                    dve.wait_ge(lastx_done, updates(b, t))
                    dve.tensor_tensor(last[:], cs[:, :, P - 1], csc[:], ALU.subtract).then_inc(last_done, 1)
                dve.wait_ge(dec_done, tiles(b, t))
                for h in range(HEADS):
                    ins = dve.tensor_scalar(seg[:, h, :], cs[:, h, :], csc[:, h:h + 1], 0.0, ALU.subtract, ALU.min)
                ins.then_inc(seg_done, 1)
                dve.wait_ge(m_done, freed(b, t))
                dve.tensor_tensor(gm[t % 2][:], g_ps[:, 0:P], m.tri[:], ALU.mult).then_inc(gm_done, 1)
                dve.wait_ge(tr_done, tiles(b, t) + 1)
                dve.wait_ge(y_done, freed(b, t))
                xv = tr_ps[:, 0:D_IN].rearrange("p (h d) -> p h d", h=HEADS)
                dve.tensor_tensor(xdt[t % 2][:], xv, spread(dt[:, t, :]), ALU.mult).then_inc(xdt_done, 1)
                if t < UPDATES:
                    dve.wait_ge(xdt_done, tiles(b, t) + 1)
                    dve.wait_ge(lastx_done, updates(b, t) + 1)
                    dve.wait_ge(st_done, upfreed(b, t))
                    dve.tensor_tensor(xdd[t % 2][:], xdt[t % 2][:], spread(lastx[:]), ALU.mult).then_inc(xdd_done, 1)

            def middle(b, t):
                old, new = S[t % 2], S[1 - t % 2]
                if t < UPDATES:
                    added = st_ps[:, 0:D_IN].rearrange("p (h d) -> p h d", h=HEADS)
                    dve.wait_ge(y_done, tiles(b, t))
                    if t == 0:
                        dve.wait_ge(st_done, updates(b, t) + 1)
                        dve.tensor_copy(new[:], added).then_inc(s_done, 1)
                    else:
                        dve.wait_ge(cdec_done, states(b, t) + 1)
                        dve.wait_ge(s_done, updates(b, t))
                        dve.tensor_tensor(new[:], old[:], spread(cdec[t % 2][:, :, P - 1]), ALU.mult
                                          ).then_inc(s_step, 1)
                        dve.wait_ge(s_step, ONE + b * (UPDATES - 1) + t)
                        dve.wait_ge(st_done, updates(b, t) + 1)
                        dve.tensor_tensor(new[:], new[:], added, ALU.add).then_inc(s_done, 1)
                T = b * BT + t
                dve.wait_ge(y_done, tiles(b, t) + 1)
                dve.wait_ge(o_done, freed(b, t))
                dve.wait_ge(yq_done, freed(b, t))
                y = yv[t % 2]
                for j in range(HALVES):
                    dve.scalar_tensor_tensor(y[:, j, :], xbc[j][:, tok(t)], m.d1[:, j:j + 1],
                                             y_ps[:, j * P:(j + 1) * P], ALU.mult, ALU.add).then_inc(yd_done, 1)
                for j in range(HALVES):
                    dve.wait_ge(yd_done, ONE + T * 2 + j + 1)
                    dve.tensor_tensor(y[:, j, :], y[:, j, :], sz[j][:, tok(t)], ALU.mult).then_inc(yg_done, 1)

            def back(b, t):
                pass

            all_batches(dve, front, middle, back, now, ahead)
            chain = [0]

            def then(ins):
                chain[0] += 1
                ins.then_inc(tail_step, 1)
                dve.wait_ge(tail_step, ONE + chain[0])

            dve.wait_ge(oc_done, ONE + TILES)
            dve.wait_ge(added, ONE + NBATCH)
            then(dve.tensor_scalar(ss[:], outs[:, :, P], 1.0 / D_IN, EPS, ALU.mult, ALU.add))
            dve.sem_inc(fin, 1)
            dve.wait_ge(sq_done, ONE + 1)
            then(dve.reciprocal(ss[:], ss[:]))
            with dve.Fori(0, NBATCH) as b:
                for i in range(BT):
                    one = bass.ds(b * BT + i, 1)
                    dve.scalar_tensor_tensor(outs[:, one, 0:P], outs[:, one, 0:P], ss[:, one], m.rows[:, one, :],
                                             ALU.mult, ALU.add).then_inc(h_step, 1)
                for i in range(BT):
                    one = bass.ds(b * BT + i, 1)
                    dve.wait_ge(h_step, ONE + b * 2 * BT + BT + i)
                    dve.sem_inc(m.passed, 1)
                    dve.bn_stats(stats[:, one, :], outs[:, one, 0:P]).then_inc(h_step, 1)
            dve.wait_ge(h_step, ONE + 2 * TILES)
            then(dve.tensor_tensor(tmp[:], stats[:, :, 1], stats[:, :, 4], ALU.subtract))
            then(dve.tensor_tensor(mean[:], stats[:, :, 1], stats[:, :, 4], ALU.add))
            then(dve.tensor_scalar(mean[:], mean[:], -0.5, None, ALU.mult))
            then(dve.tensor_tensor(var[:], stats[:, :, 2], stats[:, :, 5], ALU.add))
            then(dve.scalar_tensor_tensor(tmp[:], tmp[:], 0.25, tmp[:], ALU.mult, ALU.mult))
            then(dve.scalar_tensor_tensor(var[:], var[:], 1.0 / P, tmp[:], ALU.mult, ALU.add))
            then(dve.tensor_scalar(var[:], var[:], EPS, None, ALU.add))
            dve.sem_inc(fin, 1)
            dve.wait_ge(sq_done, ONE + 2)
            then(dve.reciprocal(var[:], var[:]))
            then(dve.tensor_tensor(mean[:], mean[:], var[:], ALU.mult))
            dve.sem_inc(fin, 1)
            with dve.Fori(0, NBATCH) as b:
                here = bass.ds(b * BT, BT)
                o = outs[:, here, 0:P]
                dve.wait_ge(norm_done, ONE + b * BT + BT)
                dve.sem_inc(m.passed, 1)
                dve.tensor_tensor(o, o, m.lng_gate[:, bass.ds(b, 1), :].broadcast_to([P, BT, P]), ALU.mult
                                  ).then_inc(h_step, 1)
                dve.wait_ge(h_step, ONE + 2 * TILES + b * 2 + 1)
                dve.sem_inc(m.passed, 1)
                dve.tensor_tensor(m.X[:, here, :], m.X[:, here, :], o, ALU.add).then_inc(h_step, 1)


def build(nc, a, out, phases=99):
    with ExitStack() as ctx:
        sb = lambda name, shape, dt=F32: ctx.enter_context(nc.sbuf_tensor(name, shape, dt))
        m = Memory()
        m.X = sb("X", [P, TILES, P])
        m.hT = sb("hT", [P, NBATCH, PAD + SEQ])
        m.ident = sb("ident", [P, P])
        m.tri = sb("tri", [P, P])
        m.ones = sb("ones", [P, P])
        m.before = sb("before", [P, P])
        m.count = sb("count", [P, max(SLOTS)])
        m.count128 = sb("count128", [P, TILES])
        m.where = sb("where", [P, 2, TILES], mybir.dt.uint32)
        m.weight = sb("weight", [P, 2, TILES])
        m.owner = sb("owner", [1, max(SLOTS)], mybir.dt.int32)
        m.scale_row = sb("scale_row", [P, len(ROW_NORMS), NBATCH, P])
        m.shift_row = sb("shift_row", [P, len(ROW_NORMS), NBATCH, P])
        m.shift = sb("shift", [P, 2, 2, NBATCH])
        m.scale = sb("scale", [P, 2, 2, NBATCH])
        m.gate = sb("gate", [P, 2, 2, NBATCH, P])
        m.wc1 = sb("wc1", [P, TAPS, COL])
        m.wz1 = sb("wz1", [P, D_IN])
        m.wdt1 = sb("wdt1", [P, HEADS])
        m.cb1 = sb("cb1", [P, COL // P])
        m.dtb1 = sb("dtb1", [HEADS, 1])
        m.negA1 = sb("negA1", [P, HEADS])
        m.d1 = sb("d1", [P, HALVES])
        m.wout1 = sb("wout1", [P, HALVES, P])
        m.lng_gate = sb("lng_gate", [P, NBATCH, P])
        m.lnb_gate = sb("lnb_gate", [P, NBATCH, P])
        m.gate1 = sb("gate1", [P, NE])
        m.gb1 = sb("gb1", [P, 2, NE])
        m.xs = [nc.dram_tensor(f"xs{layer}", (SLOTS[layer] * P, P), F32).ap() for layer in range(2)]
        m.ys = [nc.dram_tensor(f"ys{layer}", (SLOTS[layer] * P, P), F32).ap() for layer in range(2)]
        m.out = out
        m.kept = ctx
        m.stored = ctx.enter_context(nc.semaphore("stored"))
        m.passed = ctx.enter_context(nc.semaphore("passed"))
        m.late = ctx.enter_context(nc.semaphore("late"))
        m.cleared = ctx.enter_context(nc.semaphore("cleared"))
        layer0 = ctx.enter_context(ExitStack())
        sb0 = lambda name, shape, dt=F32: layer0.enter_context(nc.sbuf_tensor(name, shape, dt))
        m.pick = sb0("pick", [3 * 2 * N0, 2 * N0 * P], BF16)
        m.wc0 = sb0("wc0", [P, TAPS, D_IN])
        m.wz0 = sb0("wz0", [P, D_IN])
        m.cb0 = sb0("cb0", [P, HALVES])
        m.wx = sb0("wx", [P, HALVES, RANK + 6 * N0])
        m.wdt0 = sb0("wdt0", [RANK, D_IN])
        m.bdt0 = sb0("bdt0", [P, HALVES])
        m.negA0 = sb0("negA0", [P, HALVES, N0])
        m.diagD0 = sb0("diagD0", [P, HALVES, P])
        m.wo0 = sb0("wo0", [P, HALVES, P])
        m.router = sb0("router", [P, NE])
        m.sems = {}
        for tag, names in (("n00_", NORM_SEMS), ("n01_", NORM_SEMS), ("n10_", NORM_SEMS), ("n11_", NORM_SEMS),
                           ("ma_", MAMBA_SEMS), ("ss_", SSD_SEMS), ("so_", SORTED_SEMS)):
            for name in names.split():
                m.sems[tag + name] = ctx.enter_context(nc.semaphore(tag + name))
        setup(nc, a, m)
        steps = [lambda: norm(nc, a, m, 0, 0), lambda: mamba(nc, m), lambda: norm(nc, a, m, 0, 1),
                 lambda: route(nc, a, m, 0), lambda: sorted_experts(nc, m, 0), lambda: combine(nc, m, 0), lambda: norm(nc, a, m, 1, 0), lambda: ssd(nc, m),
                 lambda: norm(nc, a, m, 1, 1), 
                 lambda: route(nc, a, m, 1), lambda: sorted_experts(nc, m, 1), lambda: combine(nc, m, 1)]
        for i, step in enumerate(steps[:phases]):
            if i == 8:
                m.w1 = ctx.enter_context(nc.sbuf_tensor("w1", [P, NE, F1], F32, side="right"))
                m.w2 = ctx.enter_context(nc.sbuf_tensor("w2", [P, NE, F1 // P, P], F32, side="right"))
            if i == 2:
                m.wgu = sb0("wgu", [P, NE, 2 * F0])
                m.wdown = sb0("wdown", [P, NE, F0 // P, P])
                m.rows = ctx.enter_context(nc.sbuf_tensor("rows", [P, TILES, P], F32, side="right"))
            if i == 9:
                m.b1 = ctx.enter_context(nc.sbuf_tensor("b1", [P, NE * F1], F32, side="right"))
                m.b2 = ctx.enter_context(nc.sbuf_tensor("b2", [P, NE * P], F32, side="right"))
            if i == 6:
                layer0.close()
            step()
        if phases < len(steps):
            with nc.Block() as block:
                @block.sync
                def _(sp):
                    sp.dma_start(out.rearrange("b (j p) d -> p (b j) d", p=P), m.X[:]).then_inc(m.stored, 16)
                    sp.wait_ge(m.stored, 16)


def kernel(**inputs):
    import numpy as np
    import concourse.bacc as bacc
    from concourse.bass_utils import run_bass_kernel_spmd

    def laid(name, f=lambda v: v):
        return np.ascontiguousarray(f(np.asarray(inputs[name])))

    T = lambda v: v.T
    last2 = lambda v: v.transpose(0, 2, 1)
    three = lambda v: np.concatenate([v.T[:, :RANK]] + 3 * [v.T[:, RANK:]], axis=1)
    arrays = {
        "L0_cT": laid("L0_c", T), "L1_cT": laid("L1_c", T), "L0_wmod": laid("L0_wmod"), "L1_wmod": laid("L1_wmod"),
        "L0_attn_x": laid("L0_attn_x"), "L0_WiT": laid("L0_attn_Wi", T),
        "L0_conv_row": laid("L0_attn_conv_w", lambda v: v[:, 0, :].T), "L0_WxT": laid("L0_attn_Wx", three),
        "L0_WdtT": laid("L0_attn_Wdt", T), "L0_WoT": laid("L0_attn_Wo", T),
        "L1_conv_row": laid("L1_attn_conv_w", T),
        "router_T": laid("L0_ffn_router_w", T), "w_gate_T": laid("L0_ffn_w_gate", last2),
        "w_up_T": laid("L0_ffn_w_up", last2), "w_down_T": laid("L0_ffn_w_down", last2),
        "gate_T": laid("L1_ffn_gate_w", T),
    }
    for short, name in (("cb0", "L0_attn_conv_b"), ("bdt0", "L0_attn_bdt"), ("dp0", "L0_attn_Dp"),
                        ("cb1", "L1_attn_conv_b"), ("rms", "L1_attn_rms_w")):
        arrays[short] = laid(name, lambda v: v.reshape(-1, P).T)
    arrays["L1_ffn_b1"] = laid("L1_ffn_b1", lambda v: v.reshape(-1))
    for name in ("L0_attn_A_log L1_attn_W_in L1_attn_dt_bias L1_attn_A_log L1_attn_D L1_attn_W_out L1_attn_ln_g "
                 "L1_attn_ln_b L1_ffn_gate_b L1_ffn_expert_bias L1_ffn_w1 L1_ffn_w2").split():
        arrays[name] = laid(name)
    arrays["L1_ffn_b2"] = laid("L1_ffn_b2", lambda v: v.reshape(-1))
    arrays["ident"] = np.eye(P, dtype=np.float32)
    arrays["tri"] = np.triu(np.ones((P, P), np.float32))
    arrays["before"] = np.triu(np.ones((P, P), np.float32), 1)
    arrays["count"] = np.arange(max(SLOTS), dtype=np.float32)
    pick = np.zeros((3, 2 * N0, 2 * N0, P), mybir.dt.np(BF16))
    for n in range(2 * N0):
        pick[:, n, n, :] = 1.0
    arrays["pick"] = pick.reshape(3 * 2 * N0, 2 * N0 * P)

    nc = bacc.Bacc("TRN2", target_bir_lowering=False, num_devices=1)
    aps = {}
    for name, v in arrays.items():
        aps[name] = nc.dram_tensor("in_" + name, v.shape, mybir.dt.from_np(v.dtype), kind="ExternalInput").ap()
    out = nc.dram_tensor("out", (NBATCH, SEQ, P), F32, kind="ExternalOutput").ap()
    build(nc, aps, out)
    r = run_bass_kernel_spmd(nc, [{"in_" + k: v for k, v in arrays.items()}], core_ids=[0])
    return r.results[0]["out"]
```

```python
from contextlib import ExitStack

import concourse.bass as bass
from concourse import mybir

ALU = mybir.AluOpType
ACT = mybir.ActivationFunctionType
F32 = mybir.dt.float32
BF16 = mybir.dt.bfloat16
AX = mybir.AxisListType.X

P = 128
NBATCH = 4
SEQ = 1024
TOKENS = NBATCH * SEQ
TILES = TOKENS // P
BT = SEQ // P
COL = 512
NCOL = SEQ // COL
TAPS = 4
PAD = TAPS - 1
EPS = 1e-5

D_IN = 256
HALVES = D_IN // P
N0 = 16
RANK = 64
F0 = 256
NE = 8
HEADS = 4
HD = D_IN // HEADS
F1 = 512
CHOICES = (2, 1)
SLOTS = tuple(c * TILES + NE for c in CHOICES)
ROW_NORMS = ((0, 1), (1, 0), (1, 1))
LATE = (48, 80)


class Memory:
    pass


ONE = 1
SORTED_SEMS = ("xt_done xt_read up_done act_done wide_done ht_done ht_read out_done out_read "
               "loaded0 loaded1 stored0 stored1")
MAMBA_SEMS = ("pre_done pre_read low_done low_read split_done split_step parts_done dmm_done sp_step ln_done "
              "relu_done delta_done u0_done u1_done bc_done bc_read bu_done decay_done scan_done ch_done acc_done "
              "yg_done out_done gated x_done")
SSD_SEMS = ("proj_done proj_read dt_done dt_step dt_ready dtt_done dtt_read dA_done cs_done tr_done "
            "csc_done seg_done dec_done cdec_done lastx_done gm_done m_done cts_done xdt_done xdd_done "
            "bt_done y_done st_done s_done s_step yd_done yg_done yq_done o_done "
            "dtl_done last_done oc_done fin sq_done tail_step h_step norm_done added conv_step conv_read")


def setup(nc, a, m):
    with ExitStack() as ctx:
        sb = lambda name, shape, dt=F32: ctx.enter_context(nc.sbuf_tensor("su_" + name, shape, dt))
        sem = lambda name: m.kept.enter_context(nc.semaphore("su_" + name))
        ps = ctx.enter_context(nc.psum_tensor("ps_setup", [P, 8, COL], F32))
        cw0 = sb("cw0", [P, TAPS, D_IN])
        cw1 = sb("cw1", [P, TAPS, D_IN])
        wmod = sb("wmod", [P, 2, 6 * P])
        win0 = sb("win0", [P, D_IN])
        wout_raw = sb("wout_raw", [P, HALVES, P])
        cT = sb("cT", [P, 2, NBATCH])
        scT = sb("scT", [P, 2, NBATCH])
        sig = sb("sig", [P, 2, NBATCH])
        alog0 = sb("alog0", [P, HALVES, N0])
        alog1 = sb("alog1", [P, HEADS])
        dp0 = sb("dp0", [P, HALVES])
        rms = sb("rms", [P, HALVES])
        gsign = sb("gsign", [P, 2, 2, NBATCH, P])
        gate_raw = sb("gate_raw", [P, 2, 2, NBATCH, P])
        small, big, s_silu, s_modT, s_modB, s_v, s_exp = (
            sem(n) for n in ("small", "big", "s_silu", "s_modT", "s_modB", "s_v", "s_exp"))
        s_abs = sem("s_abs")
        s_bank_read = sem("s_bank_read")
        s_zeros = sem("s_zeros")
        s_x = sem("s_x")
        GATE_BANK = ((0, 2), (4, 6))
        ROW_BANK = ((3, 5), (7, 1), (0, 2))
        lng = sb("lng", [P, P])
        lnb = sb("lnb", [P, P])
        s_early, s_counted = sem("s_early"), sem("s_counted")
        norm = make_norm(nc, ctx, m, 0, 0, [ps[:, 3, :], ps[:, 5, :]])
        block = ctx.enter_context(nc.Block())
        n_small, n_big, n_early = [0], [0], [0]

        @block.sync
        def _(sp):
            def load(dst, src, s=small, n=n_small):
                sp.dma_start(dst, src).then_inc(s, 16)
                n[0] += 1
            sp.dma_start(m.X[:], a["L0_attn_x"].rearrange("b (j p) d -> p (b j) d", p=P)).then_inc(s_x, 16)
            for l, name in ((0, "L0"), (1, "L1")):
                load(cT[:, l, :], a[name + "_cT"], s_early, n_early)
                load(wmod[:, l, :], a[name + "_wmod"], s_early, n_early)
            load(m.ident[:], a["ident"], s_early, n_early)
            load(m.tri[:], a["tri"])
            load(m.pick[:], a["pick"])
            load(m.before[:], a["before"])
            load(m.count[:], a["count"].partition_broadcast(P))
            load(cw0[:], a["L0_conv_row"].partition_broadcast(P))
            load(cw1[:], a["L1_conv_row"][:, 0:D_IN].partition_broadcast(P))
            load(win0[:], a["L0_WiT"][:, 0:D_IN])
            load(m.wz0[:], a["L0_WiT"][:, D_IN:2 * D_IN])
            load(m.tap1[:], a["tap1"])
            load(m.win1[:], a["L1_attn_W_in"][:, D_IN:D_IN + COL])
            load(m.wz1[:], a["L1_attn_W_in"][:, 0:D_IN])
            load(m.wdt1[:], a["L1_attn_W_in"][:, D_IN + COL:D_IN + COL + HEADS])
            load(m.wx[:], a["L0_WxT"].rearrange("(j p) n -> p j n", p=P))
            load(m.wdt0[:], a["L0_WdtT"])
            load(m.wo0[:], a["L0_WoT"].rearrange("(j p) n -> p j n", p=P))
            load(wout_raw[:], a["L1_attn_W_out"].rearrange("(j p) n -> p j n", p=P))
            load(m.cb0[:], a["cb0"])
            load(m.cb1[:], a["cb1"])
            load(m.bdt0[:], a["bdt0"])
            load(dp0[:], a["dp0"])
            load(rms[:], a["rms"])
            load(alog0[:], a["L0_attn_A_log"].rearrange("(j p) n -> p j n", p=P))
            load(alog1[:], a["L1_attn_A_log"].partition_broadcast(P))
            load(m.dtb1[:], a["L1_attn_dt_bias"].rearrange("(h o) -> h o", o=1))
            for j in range(HALVES):
                for q in range(P // HD):
                    load(m.d1[q * HD:(q + 1) * HD, j:j + 1],
                         a["L1_attn_D"][2 * j + q:2 * j + q + 1].partition_broadcast(HD))
            load(lng[:], a["L1_attn_ln_g"].partition_broadcast(P))
            load(lnb[:], a["L1_attn_ln_b"].partition_broadcast(P))
            load(m.gb1[:, 0, :], a["L1_ffn_gate_b"].partition_broadcast(P))
            load(m.gb1[:, 1, :], a["L1_ffn_expert_bias"].partition_broadcast(P))
            load(m.router[:], a["router_T"], big, n_big)
            load(m.gate1[:], a["gate_T"], big, n_big)
            for name, semaphore in m.sems.items():
                if not name.startswith("so_"):
                    sp.sem_inc(semaphore, ONE)
            sp.wait_ge(s_zeros, 1)
            for layer in range(2):
                sp.dma_start(m.xs[layer].rearrange("(p q) d -> p q d", p=P),
                             m.zeros[:].unsqueeze(1).broadcast_to([P, SLOTS[layer], P])).then_inc(m.cleared, 16)
            sp.wait_ge(big, 16 * n_big[0])

        @block.gpsimd
        def _(pool):
            pool.memset(m.zeros[:], 0.0).then_inc(s_zeros, 1)

        @block.scalar
        def _(act):
            act.wait_ge(s_early, 16 * n_early[0])
            act.activation(scT[:], cT[:], ACT.Silu).then_inc(s_silu, 1)
            for b in range(NBATCH):
                norm.root(act, b)
            act.wait_ge(small, 16 * n_small[0])
            act.activation(m.negA0[:], alog0[:], ACT.Exp).then_inc(s_exp, 1)
            act.activation(m.negA1[:], alog1[:], ACT.Exp).then_inc(s_exp, 1)
            act.wait_ge(s_modB, 16)
            for l in range(2):
                for g in range(2):
                    src = ps[:, GATE_BANK[l][g], 0:NBATCH * P].rearrange("p (b d) -> p b d", b=NBATCH)
                    act.activation(gate_raw[:, l, g], src, ACT.Abs).then_inc(s_abs, 1)
            act.wait_ge(s_bank_read, 1)
            for b in range(NBATCH):
                norm.write(act, b)

        @block.tensor
        def _(pe):
            pe.wait_ge(s_silu, 1)
            for l in range(2):
                for j in range(6):
                    mm = pe.matmul(ps[:, 1, (6 * l + j) * NBATCH:(6 * l + j + 1) * NBATCH],
                                   wmod[:, l, j * P:(j + 1) * P], scT[:, l, :], start=True, stop=True)
            mm.then_inc(s_modT, 1)
            def spread_rows(bank, l, block):
                for b in range(NBATCH):
                    pe.matmul(ps[:, bank, b * P:(b + 1) * P], scT[:, l, b:b + 1].broadcast_to([P, P]),
                              wmod[:, l, block * P:(block + 1) * P], start=True, stop=True).then_inc(s_modB, 1)
            for l in range(2):
                for g in range(2):
                    spread_rows(GATE_BANK[l][g], l, 3 * g + 2)
            for b in range(NBATCH):
                norm.turn(pe, b)
            pe.wait_ge(norm.written, 2 * NBATCH)
            for n, (l, sub) in enumerate(ROW_NORMS):
                for j in range(2):
                    if ROW_BANK[n][j] == 1:
                        pe.wait_ge(s_bank_read, 1)
                    if ROW_BANK[n][j] == 0:
                        pe.wait_ge(s_bank_read, 2)
                    spread_rows(ROW_BANK[n][j], l, 3 * sub + j)

        @block.vector
        def _(dve):
            steps = [0]

            def step(ins):
                steps[0] += 1
                ins.then_inc(s_v, 1)

            dve.wait_ge(s_x, 16)
            for t in range(TILES):
                dve.bn_stats(m.stats[:, t, :], m.X[:, t, :]).then_inc(s_counted, 1)
            dve.wait_ge(s_counted, TILES)
            for b in range(NBATCH):
                norm.moments(dve, b)
            for b in range(NBATCH):
                norm.normalize(dve, b)
            dve.wait_ge(s_modT, 1)
            modT = ps[:, 1, 0:12 * NBATCH].rearrange("p (l j b) -> p l j b", l=2, j=6)
            for l in range(2):
                for g in range(2):
                    step(dve.tensor_copy(m.shift[:, l, g, :], modT[:, l, 3 * g, :]))
                    step(dve.tensor_scalar(m.scale[:, l, g, :], modT[:, l, 3 * g + 1, :], 1.0, None, ALU.add))
            dve.wait_ge(s_v, steps[0])
            dve.sem_inc(s_bank_read, 1)
            dve.wait_ge(small, 16 * n_small[0])
            for k in range(TAPS):
                step(dve.tensor_tensor(m.wc0[:, k, :], win0[:], cw0[:, k, :], ALU.mult))
                step(dve.tensor_tensor(m.wc1[:, k, :], m.win1[:, 0:D_IN], cw1[:, k, :], ALU.mult))
            for j in range(HALVES):
                step(dve.tensor_scalar(m.wout1[:, j, :], wout_raw[:, j, :], rms[:, j:j + 1], None, ALU.mult))
                step(dve.tensor_scalar(m.diagD0[:, j, :], m.ident[:], dp0[:, j:j + 1], None, ALU.mult))
            step(dve.memset(m.hT[:, :, 0:PAD], 0.0))
            step(dve.memset(m.ones[:], 1.0))
            step(dve.tensor_scalar(m.count128[:], m.count[:, 0:TILES], float(P), None, ALU.mult))
            step(dve.tensor_tensor(m.gb1[:, 0, :], m.gb1[:, 0, :], m.gb1[:, 1, :], ALU.add))
            dve.wait_ge(s_exp, 2)
            step(dve.tensor_scalar(m.negA0[:], m.negA0[:], -1.0, None, ALU.mult))
            step(dve.tensor_scalar(m.negA1[:], m.negA1[:], -1.0, None, ALU.mult))
            dve.wait_ge(s_modB, 16)
            dve.wait_ge(s_abs, 4)
            for l in range(2):
                for g in range(2):
                    src = ps[:, GATE_BANK[l][g], 0:NBATCH * P].rearrange("p (b d) -> p b d", b=NBATCH)
                    step(dve.tensor_scalar(gsign[:, l, g], src, 0.0, 2.0, ALU.is_ge, ALU.mult))
            for l in range(2):
                for g in range(2):
                    step(dve.tensor_scalar(gate_raw[:, l, g], gate_raw[:, l, g], 0.25, None, ALU.max))
            dve.wait_ge(s_v, steps[0])
            step(dve.scalar_tensor_tensor(m.gate[:], gsign[:], -1.0, gate_raw[:], ALU.add, ALU.mult))
            dve.sem_inc(s_bank_read, 1)
            dve.wait_ge(s_v, steps[0])
            for dst, src in ((m.lng_gate, lng), (m.lnb_gate, lnb)):
                step(dve.tensor_tensor(dst[:], m.gate[:, 1, 0], src[:].unsqueeze(1).broadcast_to([P, NBATCH, P]),
                                       ALU.mult))
            dve.wait_ge(s_modB, 16 + 2 * len(ROW_NORMS) * NBATCH)
            for n in range(len(ROW_NORMS)):
                for j, dst in ((0, m.shift_row), (1, m.scale_row)):
                    src = ps[:, ROW_BANK[n][j], 0:NBATCH * P].rearrange("p (b d) -> p b d", b=NBATCH)
                    step(dve.tensor_scalar(dst[:, n], src, float(j), None, ALU.add))
            dve.wait_ge(s_v, steps[0])


class Norm:
    GROUP = COL // P

    def moments(self, dve, b):
        T = slice(b * BT, (b + 1) * BT)
        mean, var, tmp = self.mean[:, T], self.var[:, T], self.tmp[:, T]
        stats, chain, before = self.m.stats[:, T], self.chain, 7 * b
        half_e, half_o = stats[:, :, 1], stats[:, :, 4]
        dve.tensor_tensor(tmp, half_e, half_o, ALU.subtract).then_inc(chain, 1)
        dve.tensor_tensor(mean, half_e, half_o, ALU.add).then_inc(chain, 1)
        dve.tensor_tensor(var, stats[:, :, 2], stats[:, :, 5], ALU.add).then_inc(chain, 1)
        dve.wait_ge(chain, before + 3)
        dve.tensor_scalar(mean, mean, 0.5, None, ALU.mult).then_inc(chain, 1)
        dve.scalar_tensor_tensor(tmp, tmp, 0.25, tmp, ALU.mult, ALU.mult).then_inc(chain, 1)
        dve.wait_ge(chain, before + 5)
        dve.scalar_tensor_tensor(var, var, 1.0 / P, tmp, ALU.mult, ALU.add).then_inc(chain, 1)
        dve.wait_ge(chain, before + 6)
        dve.tensor_scalar(var, var, EPS, None, ALU.add).then_inc(chain, 1)

    def root(self, act, b):
        T = slice(b * BT, (b + 1) * BT)
        act.wait_ge(self.chain, 7 * b + 7)
        act.activation(self.rstd[:, T], self.var[:, T], ACT.Sqrt).then_inc(self.root_done, 1)

    def normalize(self, dve, b):
        T = slice(b * BT, (b + 1) * BT)
        dve.wait_ge(self.root_done, b + 1)
        dve.reciprocal(self.rstd[:, T], self.rstd[:, T]).then_inc(self.inverted, 1)
        dve.wait_ge(self.inverted, b + 1)
        for t in range(b * BT, (b + 1) * BT):
            dve.tensor_scalar(self.xn[:, t, :], self.m.X[:, t, :], self.mean[:, t:t + 1], self.rstd[:, t:t + 1],
                              ALU.subtract, ALU.mult).then_inc(self.xn_done, 1)

    def turn(self, pe, b):
        for g in range(2 * b, 2 * b + 2):
            pe.wait_ge(self.xn_done, (g + 1) * self.GROUP)
            if g >= 2:
                pe.wait_ge(self.written, g - 1)
            for j in range(self.GROUP):
                tr = pe.transpose(self.banks[g % 2][:, j * P:(j + 1) * P], self.xn[:, g * self.GROUP + j, :],
                                  self.m.ident[:])
            tr.then_inc(self.turned, 1)

    def write(self, act, b):
        scale = self.m.scale[:, self.layer, self.sub, b:b + 1]
        shift = self.m.shift[:, self.layer, self.sub, b:b + 1]
        for r in range(2):
            act.wait_ge(self.turned, 2 * b + r + 1)
            act.activation(self.m.hT[:, b, PAD + r * COL:PAD + (r + 1) * COL], self.banks[r], ACT.Identity,
                           bias=shift, scale=scale).then_inc(self.written, 1)


def make_norm(nc, ctx, m, layer, sub, banks):
    norm = Norm()
    sb = lambda name, shape: ctx.enter_context(nc.sbuf_tensor(f"n{layer}{sub}_" + name, shape, F32))
    norm.m, norm.layer, norm.sub, norm.banks = m, layer, sub, banks
    norm.mean, norm.var, norm.rstd, norm.tmp = (sb(n, [P, TILES]) for n in ("mean", "var", "rstd", "tmp"))
    norm.xn = m.rows if (layer, sub) in ROW_NORMS else sb("xn", [P, TILES, P])
    norm.chain, norm.root_done, norm.inverted, norm.xn_done, norm.turned, norm.written = (
        m.kept.enter_context(nc.semaphore(f"n{layer}{sub}_" + n))
        for n in ("chain", "root_done", "inverted", "xn_done", "turned", "written"))
    return norm


def norm_for_experts(nc, a, m, layer):
    with ExitStack() as ctx:
        banks = [ctx.enter_context(nc.psum_tensor(f"n{layer}1_ps{i}", [P, COL], F32))[:] for i in range(2)]
        norm = make_norm(nc, ctx, m, layer, 1, banks)
        modulated = m.kept.enter_context(nc.semaphore(f"n{layer}1_modulated"))
        block = ctx.enter_context(nc.Block())

        @block.sync
        def _(sp):
            if layer == 0:
                sp.dma_start(m.wgu[:, :, 0:F0], a["w_gate_T"].rearrange("e k f -> k e f")).then_inc(m.late, 16)
                sp.dma_start(m.wgu[:, :, F0:2 * F0], a["w_up_T"].rearrange("e k f -> k e f")).then_inc(m.late, 16)
                sp.dma_start(m.wdown[:], a["w_down_T"].rearrange("e (j p) d -> p e j d", p=P)).then_inc(m.late, 16)
            else:
                sp.dma_start(m.w1[:], a["L1_ffn_w1"].rearrange("e k f -> k e f")).then_inc(m.late, 16)
                sp.dma_start(m.w2[:], a["L1_ffn_w2"].rearrange("e (j p) d -> p e j d", p=P)).then_inc(m.late, 16)

        @block.vector
        def _(dve):
            for b in range(NBATCH):
                norm.moments(dve, b)
            for b in range(NBATCH):
                norm.normalize(dve, b)

        @block.tensor
        def _(pe):
            def logits(b):
                pe.wait_ge(norm.written, 2 * b + 2)
                for t in range(b * BT, (b + 1) * BT):
                    c0 = PAD + t % BT * P
                    pe.matmul(m.logits[:, t * NE:(t + 1) * NE], m.hT[:, b, c0:c0 + P],
                              (m.router, m.gate1)[layer][:], start=True, stop=True)

            for b in range(NBATCH):
                norm.turn(pe, b)
                if b > 0:
                    logits(b - 1)
            logits(NBATCH - 1)

        @block.scalar
        def _(act):
            for b in range(NBATCH):
                norm.root(act, b)
            for b in range(NBATCH):
                norm.write(act, b)

        @block.gpsimd
        def _(pool):
            modulate(pool, m, layer, 1, modulated, norm.turned)


def modulate(pool, m, layer, sub, done, turned=None):
    n = ROW_NORMS.index((layer, sub))
    for b in range(NBATCH):
        if turned:
            pool.wait_ge(turned, 2 * b + 2)
        rows = m.rows[:, b * BT:(b + 1) * BT, :]
        for i, (row, op) in enumerate(((m.scale_row, ALU.mult), (m.shift_row, ALU.add))):
            pool.tensor_tensor(rows, rows, row[:, n, b, :].unsqueeze(1).broadcast_to([P, BT, P]), op
                               ).then_inc(done, 1)
            pool.wait_ge(done, 2 * b + i + 1)


def mamba(nc, m):
    with ExitStack() as ctx:
        sb = lambda name, shape, dt=F32: ctx.enter_context(nc.sbuf_tensor("ma_" + name, shape, dt))
        sem = lambda name: m.sems["ma_" + name]
        bank = [ctx.enter_context(nc.psum_tensor(f"mps{i}", [P, COL], F32)) for i in range(2)]
        bc_ps = ctx.enter_context(nc.psum_tensor("bc_ps", [P, SEQ], F32))
        y_ps = [ctx.enter_context(nc.psum_tensor(f"y_ps{i}", [P, SEQ], F32)) for i in range(HALVES)]
        xp = [sb(f"xp{i}", [P, SEQ]) for i in range(HALVES)]
        sz = [sb(f"sz{i}", [P, SEQ]) for i in range(HALVES)]
        delta = [sb(f"delta{i}", [P, SEQ]) for i in range(HALVES)]
        u = [sb(f"u{i}", [P, SEQ]) for i in range(HALVES)]
        low = sb("low", [RANK, SEQ])
        G = 2 * N0
        parts = sb("parts", [3 * G, SEQ], BF16)
        hi = sb("hi", [3 * G, COL], BF16)
        mid = sb("mid", [3 * G, COL], BF16)
        rest = sb("rest", [3 * G, COL])
        bsb = [sb(f"bsb{i}", [P, SEQ]) for i in range(2)]
        csb = [sb(f"csb{i}", [P, SEQ]) for i in range(2)]
        SLOTS = 4
        bu = [sb(f"bu{i}", [P, SEQ]) for i in range(SLOTS)]
        DECAYS = 4
        decay = [sb(f"decay{i}", [P, SEQ]) for i in range(DECAYS)]
        h = [sb(f"h{i}", [P, SEQ]) for i in range(SLOTS)]
        yg, ab, lt = bu, h, decay
        (pre_done, pre_read, low_done, low_read, split_done, split_step, parts_done, dmm_done, sp_step, ln_done,
         relu_done, delta_done, u0_done, u1_done, bc_done, bc_read, bu_done, decay_done, scan_done, ch_done, acc_done,
         yg_done, out_done, gated, x_done) = (sem(n) for n in MAMBA_SEMS.split())
        RING = 2
        block = ctx.enter_context(nc.Block())
        NPRE = 2 * HALVES * NCOL
        XPRE = HALVES * NCOL
        UNITS = N0 * HALVES
        col = lambda c: slice(c * COL, (c + 1) * COL)

        def row_place(n, w):
            if isinstance(n, int) and (n, w) in ((0, 0), (N0 - 1, 1)):
                return 0 if n == 0 else 2 * N0 - 1
            return 2 * n - 1 if w == 0 else 2 * n + 2

        x_bank = [bank[i % 2][:] for i in range(XPRE)]
        z_bank = [bc_ps[:, col(0)], bc_ps[:, col(1)], bank[0][:], bank[1][:]]

        def place(b, what, i, last=False):
            if what == "x":
                return i if isinstance(b, int) and b == 0 else b * NPRE - XPRE + i + (XPRE if i >= RING else 0)
            return b * NPRE + XPRE + i + (0 if last else RING)

        def all_batches(engine, first, start, body, finish):
            first(0, 0)
            first(0, 1)
            start(0)
            with engine.Fori(0, NBATCH - 1) as b:
                body(b, lambda i: first(b + 1, i), False)
                start(b + 1)
                finish(b, False)
            body(NBATCH - 1, lambda i: None, True)
            finish(NBATCH - 1, True)

        @block.tensor
        def _(pe):
            def project(b, what, i, last=False):
                j, c, at = i // NCOL, i % NCOL, place(b, what, i, last)
                if what == "x":
                    pe.wait_ge(pre_read, ONE + at + 1)
                elif i < RING:
                    pe.wait_ge(bc_read, ONE + (b + 1) * (4 * N0) + RING)
                else:
                    pe.wait_ge(pre_read, ONE + at - 1)
                if not isinstance(b, int):
                    pe.sem_inc(m.passed, 1)
                if what == "x":
                    for k in range(TAPS):
                        mm = pe.matmul(x_bank[i], m.wc0[:, k, j * P:(j + 1) * P],
                                       m.hT[:, bass.ds(b, 1), c * COL + k:c * COL + k + COL],
                                       start=(k == 0), stop=(k == TAPS - 1))
                else:
                    mm = pe.matmul(z_bank[i], m.wz0[:, j * P:(j + 1) * P],
                                   m.hT[:, bass.ds(b, 1), c * COL + PAD:c * COL + PAD + COL],
                                   start=True, stop=True)
                mm.then_inc(pre_done, 1)

            def first(b, i):
                project(b, "x", i)

            def start(b):
                for i in range(RING, XPRE):
                    project(b, "x", i)
                pe.wait_ge(pre_read, ONE + place(b, "x", XPRE - 1) + 1 + RING)
                for c in range(NCOL):
                    for j in range(HALVES):
                        mm = pe.matmul(bank[c][0:RANK, :], m.wx[:, j, 0:RANK], xp[j][:, col(c)],
                                       start=(j == 0), stop=(j == 1))
                    mm.then_inc(low_done, 1)
                pe.wait_ge(bc_read, ONE + b * (4 * N0) + RING)
                for c in range(NCOL):
                    for j in range(HALVES):
                        mm = pe.matmul(bc_ps[0:3 * G, col(c)], m.wx[:, j, RANK:RANK + 3 * G], xp[j][:, col(c)],
                                       start=(j == 0), stop=(j == 1))
                    mm.then_inc(split_done, 1)
                pe.wait_ge(low_read, ONE + b * NCOL + NCOL)
                pe.wait_ge(yg_done, ONE + b * 2)
                for j in range(HALVES):
                    for c in range(NCOL):
                        mm = pe.matmul(y_ps[j][:, col(c)], m.wdt0[:, j * P:(j + 1) * P], low[:, col(c)],
                                       start=True, stop=True)
                    mm.then_inc(dmm_done, 1)

            def body(b, first_of_next, last):
                for j in range(HALVES):
                    pe.wait_ge(sp_step, ONE + b * 4 + j + 1)
                    pe.wait_ge(relu_done, ONE + b * 2 + j + 1)
                    for c in range(NCOL):
                        pe.matmul(y_ps[j][:, col(c)], m.diagD0[:, j, :], xp[j][:, col(c)], start=True, stop=True)
                pe.wait_ge(parts_done, ONE + b * 6 + 6)

                def row(n, w):
                    for c in range(NCOL):
                        pe.wait_ge(bc_read, ONE + b * (4 * N0) + row_place(n, w) * NCOL + c - 1 + RING)
                        pe.matmul(bc_ps[:, col(c)], m.pick[:, bass.ds((n + w * N0) * P, P)], parts[:, col(c)],
                                  start=True, stop=True).then_inc(bc_done, 1)

                def add_state(n, r, j):
                    pe.wait_ge(ch_done, ONE + (b * N0 + n) * 2 + j + 1 + SLOTS)
                    for c in range(NCOL):
                        mm = pe.matmul(y_ps[j][:, col(c)], m.ident[:], h[2 * r + j][:, col(c)], start=False,
                                       stop=True, skip_group_check=True)
                    mm.then_inc(acc_done, 1)

                row(0, 0)
                row(1, 0)
                pe.wait_ge(gated, ONE + b * 2)
                pe.wait_ge(low_read, ONE + b * NCOL + NCOL)
                first_of_next(0)
                row(0, 1)
                row(2, 0)
                first_of_next(1)
                row(1, 1)

                def step(n, r):
                    row(n + 1, 0)
                    add_state(n - 2, r, 0)
                    row(n, 1)
                    add_state(n - 2, r, 1)

                with pe.Fori(1, N0 // 2 - 1) as i:
                    for r in range(2):
                        step(i * 2 + r, r)
                step(N0 - 2, 0)
                row(N0 - 1, 1)
                for n in range(N0 - 3, N0):
                    for j in range(HALVES):
                        add_state(n, n % 2, j)
                    if n < N0 - 1:
                        for i in range(RING):
                            project(b, "z", (n - (N0 - 3)) * RING + i, last)

            def finish(b, last):
                pe.wait_ge(yg_done, ONE + b * 2 + 2)
                if not last:
                    pe.wait_ge(low_read, ONE + b * NCOL + 2 * NCOL)
                for q in range(NCOL):
                    for t in range(COL // P):
                        tok = slice(q * COL + t * P, q * COL + (t + 1) * P)
                        for j in range(HALVES):
                            mm = pe.matmul(bank[q][:, t * P:(t + 1) * P], yg[j][:, tok], m.wo0[:, j, :], start=(j == 0), stop=(j == 1))
                    mm.then_inc(out_done, 1)

            pe.sem_inc(acc_done, SLOTS)
            all_batches(pe, first, start, body, finish)

        @block.scalar
        def _(act):
            def projected(b, what, i, last=False):
                act.wait_ge(pre_done, ONE + place(b, what, i, last) + 1)
                j = i // NCOL
                act.activation((xp if what == "x" else sz)[j][:, col(i % NCOL)], (x_bank if what == "x" else z_bank)[i], ACT.Silu,
                               bias=m.cb0[:, j:j + 1] if what == "x" else 0.0).then_inc(pre_read, 1)

            def first(b, i):
                act.wait_ge(u0_done, ONE + b)
                act.wait_ge(u1_done, ONE + b)
                projected(b, "x", i)

            def start(b):
                for i in range(RING, XPRE):
                    projected(b, "x", i)
                for j in range(HALVES):
                    act.wait_ge(dmm_done, ONE + b * 2 + j + 1)
                    act.activation(ab[j][:], y_ps[j][:], ACT.Abs, bias=m.bdt0[:, j:j + 1]).then_inc(sp_step, 1)
                act.wait_ge(ch_done, ONE + b * UNITS + SLOTS)
                for j in range(HALVES):
                    act.wait_ge(sp_step, ONE + b * 4 + j + 1)
                    act.activation(lt[j][:], ab[j][:], ACT.Exp, scale=-1.0).then_inc(sp_step, 1)
                for j in range(HALVES):
                    act.wait_ge(sp_step, ONE + b * 4 + j + 3)
                    act.activation(lt[j][:], lt[j][:], ACT.Ln, bias=1.0).then_inc(ln_done, 1)

            def body(b, first_of_next, last):

                def read_row(n, r, w):
                    act.wait_ge((bu_done, ch_done)[w], ONE + (b * N0 + n) * 2 + 2)
                    for c in range(NCOL):
                        act.wait_ge(bc_done, ONE + b * (4 * N0) + row_place(n, w) * NCOL + c + 1)
                        act.activation((bsb, csb)[w][r][:, col(c)], bc_ps[:, col(c)], ACT.Copy
                                       ).then_inc(bc_read, 1)

                def decays(n, r, j):
                    act.wait_ge(scan_done, ONE + (b * N0 + n) * 2 + j + 1)
                    act.sem_inc(m.passed, 1)
                    act.activation(decay[2 * r + j][:], delta[j][:], ACT.Exp,
                                   scale=m.negA0[:, j, bass.ds(n, 1)]).then_inc(decay_done, 1)

                def step(n, r):
                    read_row(n + 1, 1 - r, 0)
                    decays(n, r, 0)
                    read_row(n, r, 1)
                    decays(n, r, 1)

                read_row(0, 0, 0)
                act.wait_ge(delta_done, ONE + b * 2 + 1)
                decays(0, 0, 0)
                read_row(1, 1, 0)
                read_row(0, 0, 1)
                act.wait_ge(delta_done, ONE + b * 2 + 2)
                decays(0, 0, 1)
                step(1, 1)
                with act.Fori(1, N0 // 2 - 1) as i:
                    for r in range(2):
                        step(i * 2 + r, r)
                step(N0 - 2, 0)
                decays(N0 - 1, 1, 0)
                read_row(N0 - 1, 1, 1)
                decays(N0 - 1, 1, 1)
                for i in range(RING):
                    first_of_next(i)
                for i in range(XPRE):
                    projected(b, "z", i, last)

            act.sem_inc(pre_read, RING)
            act.sem_inc(bc_read, RING)
            all_batches(act, first, start, body, lambda b, last: None)

        @block.gpsimd
        def _(pool):
            pool.sem_inc(bu_done, SLOTS)
            with pool.Fori(0, NBATCH) as b:
                def products(n, r):
                    q = (b * N0 + n) * 2
                    pool.wait_ge(bc_read, ONE + b * (4 * N0) + row_place(n, 0) * NCOL + NCOL + RING)
                    for j in range(HALVES):
                        if isinstance(n, int) and n == 0:
                            pool.wait_ge((u0_done, u1_done)[j], ONE + b + 1)
                        pool.wait_ge(scan_done, ONE + q + j - 3 + DECAYS)
                        pool.tensor_tensor(bu[2 * r + j][:], u[j][:], bsb[r][:], ALU.mult).then_inc(bu_done, 1)

                products(0, 0)
                products(1, 1)
                with pool.Fori(1, N0 // 2) as i:
                    for r in range(2):
                        products(i * 2 + r, r)

        @block.vector
        def _(dve):
            def start(b):
                for c in range(NCOL):
                    dve.wait_ge(low_done, ONE + b * 2 + c + 1)
                    dve.tensor_copy(low[:, col(c)], bank[c][0:RANK, :]).then_inc(low_read, 1)

                for c in range(NCOL):
                    k = b * 6 + 3 * c
                    dve.wait_ge(split_done, ONE + b * 2 + c + 1)
                    dve.tensor_copy(hi[:], bc_ps[0:3 * G, col(c)]).then_inc(split_step, 1)
                    dve.wait_ge(split_step, ONE + k + 1)
                    dve.tensor_tensor(rest[:], bc_ps[0:3 * G, col(c)], hi[:], ALU.subtract).then_inc(split_step, 1)
                    dve.tensor_copy(parts[0:G, col(c)], hi[0:G, :]).then_inc(parts_done, 1)
                    dve.wait_ge(split_step, ONE + k + 2)
                    dve.tensor_copy(mid[:], rest[:]).then_inc(split_step, 1)
                    dve.wait_ge(split_step, ONE + k + 3)
                    dve.tensor_copy(parts[G:2 * G, col(c)], mid[G:2 * G, :]).then_inc(parts_done, 1)
                    dve.tensor_tensor(parts[2 * G:3 * G, col(c)], rest[2 * G:3 * G, :], mid[2 * G:3 * G, :],
                                      ALU.subtract).then_inc(parts_done, 1)
                for j in range(HALVES):
                    dve.wait_ge(sp_step, ONE + b * 4 + j + 1)
                    dve.tensor_scalar(delta[j][:], y_ps[j][:], m.bdt0[:, j:j + 1], 0.0, ALU.add,
                                      ALU.max).then_inc(relu_done, 1)

            def body(b, first_of_next, last):
                for j in range(HALVES):
                    dve.wait_ge(ln_done, ONE + b * 2 + j + 1)
                    dve.wait_ge(relu_done, ONE + b * 2 + j + 1)
                    dve.tensor_tensor(delta[j][:], delta[j][:], lt[j][:], ALU.add).then_inc(delta_done, 1)
                    dve.wait_ge(delta_done, ONE + b * 2 + j + 1)
                    dve.tensor_tensor(u[j][:], delta[j][:], xp[j][:], ALU.mult).then_inc((u0_done, u1_done)[j], 1)

                def scan(n, r, j):
                    q = (b * N0 + n) * 2 + j
                    dve.wait_ge(bu_done, ONE + q + 1 + SLOTS)
                    dve.wait_ge(decay_done, ONE + q + 1)
                    dve.wait_ge(acc_done, ONE + q - 3 + SLOTS)
                    dve.tensor_tensor_scan(h[2 * r + j][:], decay[2 * r + j][:], bu[2 * r + j][:], 0.0, ALU.mult, ALU.add
                                           ).then_inc(scan_done, 1)

                def times_c(n, r, j):
                    q = (b * N0 + n) * 2 + j
                    dve.wait_ge(scan_done, ONE + q + 1 + DECAYS)
                    dve.wait_ge(bc_read, ONE + b * (4 * N0) + row_place(n, 1) * NCOL + NCOL + RING)
                    hs = h[2 * r + j]
                    dve.tensor_tensor(hs[:], hs[:], csb[r][:], ALU.mult).then_inc(ch_done, 1)

                scan(0, 0, 0)
                with dve.Fori(0, N0 // 2 - 1) as i:
                    for r in range(2):
                        n = i * 2 + r
                        scan(n, r, 1)
                        times_c(n, r, 0)
                        scan(n + 1, 1 - r, 0)
                        times_c(n, r, 1)
                for n in (N0 - 2, N0 - 1):
                    scan(n, n % 2, 1)
                    times_c(n, n % 2, 0)
                    if n + 1 < N0:
                        scan(n + 1, 1, 0)
                    times_c(n, n % 2, 1)
                dve.wait_ge(acc_done, ONE + b * UNITS + UNITS + SLOTS)
                for j in range(HALVES):
                    dve.wait_ge(pre_read, ONE + place(b, "z", (j + 1) * NCOL - 1, last) + 1 + RING)
                    dve.tensor_tensor(yg[j][:], y_ps[j][:], sz[j][:], ALU.mult).then_inc(yg_done, 1)

            def finish(b, last):
                for q in range(NCOL):
                    dve.wait_ge(out_done, ONE + b * 2 + q + 1)
                    src = bank[q][:].rearrange("p (t d) -> p t d", t=4)
                    tmp = h[2][:, col(q)].rearrange("p (t d) -> p t d", t=4)
                    dve.tensor_tensor(tmp, src, m.gate[:, 0, 0, bass.ds(b, 1), :].broadcast_to([P, 4, P]),
                                      ALU.mult).then_inc(gated, 1)
                    dve.wait_ge(gated, ONE + b * 2 + q + 1)
                    xs = m.X[:, bass.ds(b * BT + 4 * q, 4), :]
                    dve.tensor_tensor(xs, xs, tmp, ALU.add).then_inc(x_done, 1)
                here = bass.ds(b * BT, BT)
                xs, stats = m.X[:, here, :], m.stats[:, here, :]
                dve.wait_ge(x_done, ONE + b * 2 + 2)
                if not isinstance(b, int):
                    dve.sem_inc(m.passed, 1)
                for t in range(BT):
                    dve.bn_stats(stats[:, t:t + 1, :], xs[:, t:t + 1, :])

            dve.sem_inc(scan_done, DECAYS)
            dve.sem_inc(ch_done, SLOTS)
            all_batches(dve, lambda b, i: None, start, body, finish)


def route(nc, a, m, layer):
    choices = CHOICES[layer]
    slots = SLOTS[layer]
    tag = f"r{layer}_"
    with ExitStack() as ctx:
        sb = lambda name, shape, dt=F32: ctx.enter_context(nc.sbuf_tensor(tag + name, shape, dt))
        sem = lambda name: m.kept.enter_context(nc.semaphore(tag + name))
        ahead_ps = ctx.enter_context(nc.psum_tensor(tag + "ahead_ps", [P, TILES * NE], F32))
        total_ps = ctx.enter_context(nc.psum_tensor(tag + "total_ps", [P, TILES * NE], F32))
        R = [P, TILES, NE]
        lg, chosen, keep, val, ex, upto, place = (
            sb(n, R) for n in ("lg", "chosen", "keep", "val", "ex", "upto", "place"))
        onehot = [sb(f"onehot{k}", R) for k in range(choices)]
        mx = [sb(f"mx{k}", [P, TILES]) for k in range(choices)]
        first = sb("first", [P, TILES])
        past = sb("past", [P, NE, TILES])
        used, upto_e, start = (sb(n, [P, NE]) for n in ("used", "upto_e", "start"))
        past_tile = sb("past_tile", [1, slots, NE])
        owner = sb("owner", [1, slots])
        step, near_done, exp_done, chosen_done, counted, placed, sent, loaded = (
            sem(n) for n in "step near_done exp_done chosen_done counted placed sent loaded".split())
        block = ctx.enter_context(nc.Block())
        over = lambda t: t[:].unsqueeze(2).broadcast_to(R)
        numbers = m.count[:, 0:NE].unsqueeze(1).broadcast_to(R)

        @block.tensor
        def _(pe):
            pe.wait_ge(chosen_done, 1)
            flat = chosen[:].rearrange("p t e -> p (t e)")
            pe.matmul(ahead_ps[:], m.before[:], flat, start=True, stop=True)
            pe.matmul(total_ps[:], m.ones[:], flat, start=True, stop=True).then_inc(counted, 1)

        @block.scalar
        def _(act):
            if layer == 0:
                for k in range(choices):
                    act.wait_ge(near_done, k + 1)
                    act.activation(ex[:], val[:], ACT.Exp).then_inc(exp_done, 1)

        @block.vector
        def _(dve):
            steps = [0]

            def then(ins):
                steps[0] += 1
                ins.then_inc(step, 1)
                dve.wait_ge(step, steps[0])

            def first_of_max(scores, hot, mx):
                then(dve.tensor_reduce(mx[:], scores[:], AX, ALU.max))
                then(dve.tensor_tensor(val[:], scores[:], over(mx), ALU.is_lt))
                then(dve.scalar_tensor_tensor(val[:], val[:], float(NE), numbers, ALU.mult, ALU.add))
                then(dve.tensor_reduce(first[:], val[:], AX, ALU.min))
                then(dve.tensor_tensor(hot[:], numbers, over(first), ALU.is_equal))

            lgv = m.logits[:, 0:TILES * NE].rearrange("p (t e) -> p t e", t=TILES)
            if layer == 1:
                then(dve.tensor_tensor(lg[:], lgv, m.gb1[:, 0, :].unsqueeze(1).broadcast_to(R), ALU.add))
                first_of_max(lg, onehot[0], mx[0])
                dve.tensor_copy(chosen[:], onehot[0][:]).then_inc(chosen_done, 1)
            else:
                then(dve.tensor_copy(lg[:], lgv))
                first_of_max(lg, onehot[0], mx[0])
                then(dve.scalar_tensor_tensor(ex[:], onehot[0][:], -3.0e38, lg[:], ALU.mult, ALU.add))
                first_of_max(ex, onehot[1], mx[1])
                dve.tensor_tensor(chosen[:], onehot[0][:], onehot[1][:], ALU.add).then_inc(chosen_done, 1)
            dve.wait_ge(counted, 1)
            total = total_ps[:].rearrange("p (t e) -> p t e", t=TILES)
            for e in range(NE):
                ins = dve.tensor_tensor_scan(upto[:, :, e], m.ones[:, 0:TILES], total[:, :, e], 0.0, ALU.mult, ALU.add)
            then(ins)
            then(dve.tensor_tensor(past[:], upto[:, TILES - 1, :].unsqueeze(2).broadcast_to([P, NE, TILES]),
                                   m.count128[:].unsqueeze(1).broadcast_to([P, NE, TILES]), ALU.is_gt))
            then(dve.tensor_reduce(used[:], past[:], AX, ALU.add))
            then(dve.tensor_tensor_scan(upto_e[:], m.ones[:, 0:NE], used[:], 0.0, ALU.mult, ALU.add))
            then(dve.tensor_tensor(start[:], upto_e[:], used[:], ALU.subtract))
            then(dve.tensor_scalar(start[:], start[:], float(P), None, ALU.mult))
            then(dve.tensor_tensor(place[:], upto[:], total, ALU.subtract))
            then(dve.tensor_tensor(place[:], place[:], ahead_ps[:].rearrange("p (t e) -> p t e", t=TILES), ALU.add))
            then(dve.tensor_tensor(place[:], place[:], start[:].unsqueeze(1).broadcast_to(R), ALU.add))
            for k in range(choices):
                then(dve.tensor_tensor(val[:], onehot[k][:], place[:], ALU.mult))
                then(dve.tensor_reduce(first[:], val[:], AX, ALU.add))
                dve.tensor_copy(m.where[:, k, :], first[:]).then_inc(placed, 1)
            S = [1, slots, NE]
            then(dve.tensor_tensor(past_tile[:], m.count[0:1, 0:slots].unsqueeze(2).broadcast_to(S),
                                   upto_e[0:1, :].unsqueeze(1).broadcast_to(S), ALU.is_ge))
            then(dve.tensor_reduce(owner[:], past_tile[:], AX, ALU.add))
            then(dve.tensor_scalar(owner[:], owner[:], float(NE - 1), None, ALU.min))
            then(dve.tensor_copy(m.owner[:, 0:slots], owner[:]))
            if layer == 0:
                for k in range(choices):
                    then(dve.scalar_tensor_tensor(keep[:], lg[:], -1.0, lg[:], ALU.mult, ALU.max))
                    then(dve.tensor_tensor(keep[:], keep[:], over(mx[k]), ALU.max))
                    then(dve.tensor_tensor(val[:], over(mx[k]), lg[:], ALU.subtract))
                    then(dve.scalar_tensor_tensor(keep[:], keep[:], 0.02, val[:], ALU.mult, ALU.is_ge))
                    if k == 1:
                        then(dve.scalar_tensor_tensor(keep[:], onehot[0][:], 0.0, keep[:], ALU.is_equal, ALU.mult))
                    dve.tensor_scalar(val[:], val[:], -1.0, 0.0, ALU.mult, ALU.min).then_inc(near_done, 1)
                    dve.wait_ge(exp_done, k + 1)
                    then(dve.tensor_tensor(ex[:], ex[:], keep[:], ALU.mult))
                    then(dve.tensor_reduce(first[:], ex[:], AX, ALU.add))
                    then(dve.reciprocal(m.weight[:, k, :], first[:]))

        @block.gpsimd
        def _(pool):
            pool.wait_ge(m.cleared, 32)
            for k in range(choices):
                pool.wait_ge(placed, k + 1)
                for t in range(TILES):
                    pool.indirect_dma_start(m.xs[layer], bass.IndirectOffsetOnAxis(ap=m.where[:, k, t:t + 1], axis=0),
                                            m.rows[:, t, :], None).then_inc(sent, 16)
            pool.wait_ge(sent, 16 * choices * TILES)

        @block.sync
        def _(sp):
            if layer == 0:
                sp.wait_ge(m.late, LATE[0])
            else:
                sp.dma_start(m.b1[:], a["L1_ffn_b1"].partition_broadcast(P)).then_inc(loaded, 16)
                sp.dma_start(m.b2[:], a["L1_ffn_b2"].partition_broadcast(P)).then_inc(loaded, 16)
                sp.wait_ge(loaded, 32)
                sp.wait_ge(m.late, LATE[1])


def sorted_experts(nc, m, layer):
    slots = SLOTS[layer]
    FB = (F0 if layer == 0 else F1) // P
    FW = FB * P
    GROUP = 4
    BODY = 2 * GROUP
    turns = slots // BODY
    tag = f"s{layer}_"
    with ExitStack() as ctx:
        sb = lambda name, shape, dt=F32: ctx.enter_context(nc.sbuf_tensor(tag + name, shape, dt))
        ps = lambda name: [ctx.enter_context(nc.psum_tensor(f"{tag}{name}{i}", [P, COL], F32)) for i in range(2)]
        xt_ps, up_ps, ht_ps, out_ps = ps("xt_ps"), ps("up_ps"), ps("ht_ps"), ps("out_ps")
        rows = [sb(f"rows{i}", [P, GROUP, P]) for i in range(2)]
        outs = [sb(f"outs{i}", [P, GROUP, P]) for i in range(2)]
        xt = [sb(f"xt{i}", [P, P]) for i in range(2)]
        act_g = [sb(f"act_g{i}", [P, FW]) for i in range(2)]
        wide = [sb(f"wide{i}", [P, FW]) for i in range(2)]
        ht = [sb(f"ht{i}", [P, FW]) for i in range(2)]
        (xt_done, xt_read, up_done, act_done, wide_done, ht_done, ht_read, out_done, out_read, loaded0, loaded1,
         stored0, stored1) = (m.sems["so_" + n] for n in SORTED_SEMS.split())
        loaded, stored = (loaded0, loaded1), (stored0, stored1)
        before = layer * SLOTS[0]
        before_dma = 16 * (before // BODY)
        block = ctx.enter_context(nc.Block())
        w_up = m.wgu if layer == 0 else m.w1
        w_down = m.wdown if layer == 0 else m.w2

        def wait(engine, semaphore, count, j):
            if not (isinstance(j, int) and j + count < 1):
                engine.wait_ge(semaphore, before + j + count)

        @block.sync
        def _(sp):
            def load(g, s, slot_used):
                if slot_used:
                    sp.wait_ge(xt_done, before + g * GROUP - GROUP)
                sp.dma_start(rows[s][:], m.xs[layer][bass.ds(g * (GROUP * P), GROUP * P), :].rearrange(
                    "(q p) d -> p q d", p=P)).then_inc(loaded[s], 16)
            load(0, 0, False)
            load(1, 1, False)
            with sp.Fori(1, turns) as i:
                for s in range(2):
                    load(i * 2 + s, s, True)

        @block.gpsimd
        def _(pool):
            with pool.Fori(0, turns) as i:
                for s in range(2):
                    g = i * 2 + s
                    pool.wait_ge(out_read, before + g * GROUP + GROUP)
                    pool.dma_start(m.ys[layer][bass.ds(g * (GROUP * P), GROUP * P), :].rearrange(
                        "(q p) d -> p q d", p=P), outs[s][:]).then_inc(stored[s], 16)
            for s in range(2):
                pool.wait_ge(stored[s], before_dma + 16 * turns)

        @block.tensor
        def _(pe):
            def turn_rows(j, k):
                if k % GROUP == 0:
                    pe.wait_ge(loaded[k // GROUP], before_dma + (j - k + BODY) * (16 // BODY))
                wait(pe, xt_read, -1, j)
                pe.transpose(xt_ps[k % 2][:, 0:P], rows[k // GROUP][:, k % GROUP, :], m.ident[:]).then_inc(xt_done, 1)

            def owner(j):
                return pe.value_load(m.owner[0:1, bass.ds(j, 1)], min_val=0, max_val=NE - 1)

            def widen(j, k, e):
                wait(pe, wide_done, -1, j)
                wait(pe, xt_read, 1, j)
                pe.matmul(up_ps[k % 2][:], xt[k % 2][:], w_up[:, bass.ds(e, 1), :].rearrange("p o f -> p (o f)"),
                          start=True, stop=True).then_inc(up_done, 1)

            def turn_wide(j, k):
                wait(pe, ht_read, -1, j)
                wait(pe, wide_done, 1, j)
                for f in range(FB):
                    tr = pe.transpose(ht_ps[k % 2][:, f * P:(f + 1) * P], wide[k % 2][:, f * P:(f + 1) * P], m.ident[:])
                tr.then_inc(ht_done, 1)

            def narrow(j, k, e):
                wait(pe, out_read, -1, j)
                wait(pe, ht_read, 1, j)
                for f in range(FB):
                    mm = pe.matmul(out_ps[k % 2][:, 0:P], ht[k % 2][:, f * P:(f + 1) * P],
                                   w_down[:, bass.ds(e, 1), f, :].rearrange("p o d -> p (o d)"),
                                   start=(f == 0), stop=(f == FB - 1))
                mm.then_inc(out_done, 1)

            def step(base, k, tiles, last_step, wide_owner):
                at = [(base + k - n, (k - n) % BODY) for n in range(4)]
                if 0 in tiles:
                    turn_rows(*at[0])
                if 1 in tiles:
                    widen(*at[1], owner(at[1][0]) if wide_owner is None else wide_owner)
                narrow_owner = owner(at[3][0]) if 3 in tiles else None
                wide_owner = owner(at[0][0]) if 0 in tiles and not last_step else None
                if 2 in tiles:
                    turn_wide(*at[2])
                if 3 in tiles:
                    narrow(*at[3], narrow_owner)
                return wide_owner

            e = None
            for k in range(BODY):
                e = step(0, k, range(min(k, 3) + 1), k == BODY - 1, e)
            with pe.Fori(1, turns) as i:
                e = None
                for k in range(BODY):
                    e = step(i * BODY, k, range(4), k == BODY - 1, e)
            for k in range(3):
                step(slots, k, range(k + 1, 4), True, None)

        @block.scalar
        def _(act):
            def evacuate_rows(j, k):
                wait(act, up_done, -1, j)
                wait(act, xt_done, 1, j)
                act.activation(xt[k % 2][:], xt_ps[k % 2][:, 0:P], ACT.Copy).then_inc(xt_read, 1)

            def silu(j, k):
                if layer == 0:
                    wait(act, wide_done, -1, j)
                    wait(act, up_done, 1, j)
                    act.activation(act_g[k % 2][:], up_ps[k % 2][:, 0:FW], ACT.Silu).then_inc(act_done, 1)

            def evacuate_wide(j, k):
                wait(act, out_done, -1, j)
                wait(act, ht_done, 1, j)
                act.activation(ht[k % 2][:], ht_ps[k % 2][:, 0:FW], ACT.Copy if layer == 0 else ACT.Relu
                               ).then_inc(ht_read, 1)

            stages = (evacuate_rows, silu, evacuate_wide)

            def step(base, k, first=0, last=len(stages) - 1):
                for n in range(first, last + 1):
                    stages[n](base + k - n, (k - n) % BODY)

            for k in range(BODY):
                step(0, k, last=min(k, len(stages) - 1))
            with act.Fori(1, turns) as i:
                for k in range(BODY):
                    step(i * BODY, k)
            for k in range(len(stages) - 1):
                step(slots, k, first=k + 1)

        @block.vector
        def _(dve):
            def widened(j, k):
                if layer == 0:
                    wait(dve, ht_done, -1, j)
                    wait(dve, act_done, 1, j)
                    dve.tensor_tensor(wide[k % 2][:], up_ps[k % 2][:, FW:2 * FW], act_g[k % 2][:],
                                      ALU.mult).then_inc(wide_done, 1)
                else:
                    e = dve.value_load(m.owner[0:1, bass.ds(j, 1)], min_val=0, max_val=NE - 1)
                    wait(dve, ht_done, -1, j)
                    wait(dve, up_done, 1, j)
                    dve.tensor_tensor(wide[k % 2][:], up_ps[k % 2][:], m.b1[:, bass.ds(e * F1, F1)],
                                      ALU.add).then_inc(wide_done, 1)

            def none(j, k):
                pass

            def narrowed(j, k):
                dst = outs[k // GROUP][:, k % GROUP, :]
                if layer == 1:
                    e = dve.value_load(m.owner[0:1, bass.ds(j, 1)], min_val=0, max_val=NE - 1)
                if k % GROUP == 0 and not (isinstance(j, int) and j < BODY):
                    dve.wait_ge(stored[k // GROUP], before_dma + (j - k) * (16 // BODY))
                wait(dve, out_done, 1, j)
                if layer == 0:
                    dve.tensor_copy(dst, out_ps[k % 2][:, 0:P]).then_inc(out_read, 1)
                else:
                    dve.tensor_tensor(dst, out_ps[k % 2][:, 0:P], m.b2[:, bass.ds(e * P, P)], ALU.add
                                      ).then_inc(out_read, 1)

            stages = (widened, none, narrowed)

            def step(base, k, first=0, last=len(stages) - 1):
                for n in range(first, last + 1):
                    stages[n](base + k - n, (k - n) % BODY)

            for k in range(BODY):
                step(0, k, last=min(k, len(stages) - 1))
            with dve.Fori(1, turns) as i:
                for k in range(BODY):
                    step(i * BODY, k)
            for k in range(len(stages) - 1):
                step(slots, k, first=k + 1)


def combine(nc, m, layer):
    choices = CHOICES[layer]
    GROUP = 4
    GROUPS = TILES // GROUP
    tag = f"c{layer}_"
    with ExitStack() as ctx:
        sb = lambda name, shape, dt=F32: ctx.enter_context(nc.sbuf_tensor(tag + name, shape, dt))
        sem = lambda name: m.kept.enter_context(nc.semaphore(tag + name))
        BUFFERS = 3
        y = [[sb(f"y{i}_{k}", [P, GROUP, P]) for k in range(choices)] for i in range(BUFFERS)]
        fetched = [sem(f"fetched{i}") for i in range(BUFFERS)]
        summed, x_done, stored, counted = sem("summed"), sem("x_done"), sem("stored"), sem("counted")
        if layer == 0:
            norm = make_norm(nc, ctx, m, 1, 0, [ctx.enter_context(nc.psum_tensor(f"n10_ps{i}", [P, COL], F32))[:]
                                           for i in range(2)])
        block = ctx.enter_context(nc.Block())

        @block.tensor
        def _(pe):
            if layer == 0:
                for b in range(NBATCH):
                    norm.turn(pe, b)

        @block.scalar
        def _(act):
            if layer == 0:
                for b in range(NBATCH):
                    norm.root(act, b)
                    norm.write(act, b)

        @block.gpsimd
        def _(pool):
            for g in range(GROUPS):
                if g >= BUFFERS:
                    pool.wait_ge(x_done, g - BUFFERS + 1)
                for k in range(choices):
                    for t in range(GROUP):
                        pool.indirect_dma_start(y[g % BUFFERS][k][:, t, :], None, m.ys[layer], bass.IndirectOffsetOnAxis(
                            ap=m.where[:, k, g * GROUP + t:g * GROUP + t + 1], axis=0)).then_inc(fetched[g % BUFFERS], 16)

        @block.vector
        def _(dve):
            n = [0]

            def then(ins):
                n[0] += 1
                ins.then_inc(summed, 1)
                dve.wait_ge(summed, n[0])

            for g in range(GROUPS):
                dve.wait_ge(fetched[g % BUFFERS], 16 * GROUP * choices * (g // BUFFERS + 1))
                ys = y[g % BUFFERS]
                tiles = slice(g * GROUP, (g + 1) * GROUP)
                over = lambda k: m.weight[:, k, tiles].unsqueeze(2).broadcast_to([P, GROUP, P])
                if choices == 2:
                    for k in range(2):
                        then(dve.tensor_tensor(ys[k][:], ys[k][:], over(k), ALU.mult))
                    then(dve.tensor_tensor(ys[0][:], ys[0][:], ys[1][:], ALU.add))
                then(dve.tensor_tensor(ys[0][:], ys[0][:], m.gate[:, layer, 1, g // 2, :].unsqueeze(1).broadcast_to(
                    [P, GROUP, P]), ALU.mult))
                dve.tensor_tensor(m.X[:, tiles, :], m.X[:, tiles, :], ys[0][:], ALU.add).then_inc(x_done, 1)
                if layer == 0:
                    dve.wait_ge(x_done, g + 1)
                    for t in range(g * GROUP, (g + 1) * GROUP):
                        dve.bn_stats(m.stats[:, t, :], m.X[:, t, :]).then_inc(counted, 1)
                    if g % 2 == 1:
                        dve.wait_ge(counted, (g + 1) * GROUP)
                        norm.moments(dve, g // 2)
                        norm.normalize(dve, g // 2)

        @block.sync
        def _(sp):
            if layer == 1:
                for g in range(GROUPS):
                    sp.wait_ge(x_done, g + 1)
                    sp.dma_start(m.out[g // 2, g % 2 * COL:(g % 2 + 1) * COL, :].rearrange("(t p) d -> p t d", p=P),
                                 m.X[:, g * GROUP:(g + 1) * GROUP, :]).then_inc(stored, 16)
                sp.wait_ge(stored, 16 * GROUPS)


def ssd(nc, m):
    with ExitStack() as ctx:
        sb = lambda name, shape, dt=F32: ctx.enter_context(nc.sbuf_tensor("ss_" + name, shape, dt))
        two = lambda name, shape: [sb(f"{name}{i}", shape) for i in range(2)]
        sem = lambda name: m.sems["ss_" + name]
        psum = lambda name: ctx.enter_context(nc.psum_tensor("ss_" + name, [P, COL], F32))
        pre = [psum("spre0"), psum("spre1")]
        cs_ps, tr_ps, st_ps, y_ps, o_ps, g_ps = (psum(n) for n in "cs_ps tr_ps st_ps y_ps o_ps g_ps".split())
        NB = COL // P
        xbc = [sb(f"xbc{i}", [P, SEQ]) for i in range(NB)]
        CONV = (2, 3)
        raw = [sb(f"raw{q}", [P, PAD + SEQ]) for q in range(2)]
        acc = [sb(f"acc{q}", [P, COL]) for q in range(2)]
        sz = [sb(f"ssz{i}", [P, SEQ]) for i in range(HALVES)]
        dtT, dte, dtl = (sb(n, [HEADS, SEQ]) for n in ("dtT", "dte", "dtl"))
        dt = sb("dt", [P, BT, HEADS])
        dA = sb("dA", [P, BT, HEADS])
        outs = sb("outs", [P, TILES, P + 1])
        ss = sb("ss", [P, TILES])
        H4 = [P, HEADS, P]
        csc = sb("csc", [P, HEADS])
        seg = sb("seg", H4)
        dec, cdec, mm_sb, cts = (two(n, H4) for n in ("dec", "cdec", "mm_sb", "cts"))
        last, lastx = sb("last", [P, HEADS]), sb("lastx", [P, HEADS])
        gm, bt = two("gm", [P, P]), two("bt", [P, P])
        xdt, xdd, S = (two(n, [P, HEADS, HD]) for n in ("xdt", "xdd", "S"))
        stats = sb("stats", [P, TILES, 6])
        mean, var, tmp = (sb(n, [P, TILES]) for n in ("mean", "var", "tmp"))
        yv, yq = two("yv", [P, HALVES, P]), two("yq", [P, HALVES, P])
        (proj_done, proj_read, dt_done, dt_step, dt_ready, dtt_done, dtt_read, dA_done, cs_done, tr_done,
         csc_done, seg_done, dec_done, cdec_done, lastx_done, gm_done, m_done, cts_done, xdt_done, xdd_done,
         bt_done, y_done, st_done, s_done, s_step, yd_done, yg_done, yq_done, o_done,
         dtl_done, last_done, oc_done, fin, sq_done, tail_step, h_step, norm_done, added,
         conv_step, conv_read) = (sem(n) for n in SSD_SEMS.split())
        modulated = m.kept.enter_context(nc.semaphore("ss_modulated"))
        block = ctx.enter_context(nc.Block())
        PIECES = NB + HALVES
        NPRE = PIECES * NCOL
        ORDER = CONV + (0, 1, 4, 5)
        CSTEPS = 2 * TAPS
        csteps = lambda b, c: ONE + 2 + (b * NCOL + c) * CSTEPS
        UPDATES = BT - 1
        assert NCOL == 2
        col = lambda c: slice(c * COL, (c + 1) * COL)
        tok = lambda t: slice(t * P, (t + 1) * P)
        four = lambda t: t.unsqueeze(1).broadcast_to(H4)
        spread = lambda v: v.unsqueeze(2).broadcast_to([P, HEADS, HD])
        flat = lambda t: t[:].rearrange("p h d -> p (h d)")
        tiles = lambda b, t: ONE + b * BT + t
        freed = lambda b, t: ONE + b * BT + max(t - 1, 0)
        updates = lambda b, t: ONE + b * UPDATES + t
        upfreed = lambda b, t: ONE + b * UPDATES + max(t - 1, 0)
        states = lambda b, t: ONE + b * UPDATES + max(t - 1, 0)

        def pipeline(b, front, middle, back, now=None, ahead=None):
            for t in range(BT):
                front(b, t)
                if t == 0:
                    now(b)
                if t >= 1:
                    middle(b, t - 1)
                if t >= 2:
                    back(b, t - 2)
            ahead(0)
            middle(b, BT - 1)
            back(b, BT - 2)
            ahead(1)
            back(b, BT - 1)
            ahead(2)

        def all_batches(engine, front, middle, back, now, ahead):
            for part in range(3):
                ahead(0, part)
            with engine.Fori(0, NBATCH - 1) as b:
                pipeline(b, front, middle, back, now, lambda part: ahead(b + 1, part))
            pipeline(NBATCH - 1, front, middle, back, now, lambda part: None)

        @block.tensor
        def _(pe):
            def project(b, c, at):
                i, j = c * PIECES + at, ORDER[at]
                if i == 0 or i == 1:
                    pe.wait_ge(dt_step, ONE + b * 4 + i + 1)
                if i == PIECES:
                    pe.wait_ge(dtt_read, ONE + b + 1)
                pe.wait_ge(proj_read, ONE + b * NPRE + i + 1)
                if not isinstance(b, int):
                    pe.sem_inc(m.passed, 1)
                if j in CONV:
                    mm = pe.matmul(pre[i % 2][:], m.win1[:, j * P:(j + 1) * P],
                                   m.hT[:, bass.ds(b, 1), c * COL + PAD:c * COL + PAD + COL],
                                   start=True, stop=True)
                elif j < NB:
                    for k in range(TAPS):
                        mm = pe.matmul(pre[i % 2][:], m.wc1[:, k, j * P:(j + 1) * P],
                                       m.hT[:, bass.ds(b, 1), c * COL + k:c * COL + k + COL],
                                       start=(k == 0), stop=(k == TAPS - 1))
                else:
                    mm = pe.matmul(pre[i % 2][:], m.wz1[:, (j - NB) * P:(j - NB + 1) * P],
                                   m.hT[:, bass.ds(b, 1), c * COL + PAD:c * COL + PAD + COL],
                                   start=True, stop=True)
                mm.then_inc(proj_done, 1)

            def now(b):
                for j in range(PIECES):
                    project(b, 1, j)

            def ahead(b, part):
                if part == 0:
                    pe.wait_ge(proj_read, ONE + b * NPRE + 2)
                    if not isinstance(b, int):
                        pe.sem_inc(m.passed, 1)
                    for c in range(NCOL):
                        mm = pe.matmul(pre[c][0:HEADS, :], m.wdt1[:],
                                       m.hT[:, bass.ds(b, 1), c * COL + PAD:c * COL + PAD + COL],
                                       start=True, stop=True)
                    mm.then_inc(dt_done, 1)
                if part < 2:
                    for j in range(PIECES // 2):
                        project(b, 0, part * (PIECES // 2) + j)
                else:
                    pe.wait_ge(dt_ready, ONE + b + 1)
                    pe.wait_ge(proj_read, ONE + b * NPRE + 2 + PIECES - 1)
                    pe.sem_inc(m.passed, 1)
                    for t in range(BT):
                        tr = pe.transpose(pre[0][:, t * HEADS:(t + 1) * HEADS], dtT[:, tok(t)],
                                          m.ident[0:HEADS, 0:HEADS])
                    tr.then_inc(dtt_done, 1)

            def front(b, t):
                if t == 0:
                    pe.wait_ge(dA_done, ONE + b + 1)
                pe.wait_ge(gm_done, tiles(b, t))
                if t % (BT // 2) == 0:
                    pe.wait_ge(conv_read, ONE + (b * NCOL + t // (BT // 2) + 1) * len(CONV))
                    pe.wait_ge(proj_read, ONE + b * NPRE + 2 + (1 + t // (BT // 2)) * PIECES)
                pe.matmul(g_ps[:, 0:P], xbc[2][:, tok(t)], xbc[3][:, tok(t)], start=True, stop=True)
                pe.matmul(g_ps[:, P:P + HEADS], m.tri[:], dA[:, t, :], start=True, stop=True)
                pe.wait_ge(cdec_done, states(b, t))
                pe.wait_ge(seg_done, tiles(b, t))
                for h in range(HEADS):
                    mm = pe.matmul(cs_ps[:, h * P:(h + 1) * P], dA[:, t, h:h + 1].broadcast_to([P, P]), m.tri[:],
                                   start=True, stop=True)
                mm.then_inc(cs_done, 1)
                pe.wait_ge(xdt_done, tiles(b, t))
                pe.wait_ge(bt_done, updates(b, t))
                for j in range(3 if t < UPDATES else 2):
                    tr = pe.transpose(tr_ps[:, j * P:(j + 1) * P], xbc[j][:, tok(t)], m.ident[:])
                tr.then_inc(tr_done, 1)

            def middle(b, t):
                if t < UPDATES:
                    pe.wait_ge(bt_done, updates(b, t) + 1)
                    pe.wait_ge(xdd_done, updates(b, t) + 1)
                    pe.wait_ge(s_done, updates(b, t))
                    pe.matmul(st_ps[:, 0:D_IN], bt[t % 2][:], flat(xdd[t % 2]), start=True, stop=True
                              ).then_inc(st_done, 1)
                pe.wait_ge(xdt_done, tiles(b, t) + 1)
                pe.wait_ge(m_done, tiles(b, t) + 1)
                if t > 0:
                    pe.wait_ge(cts_done, states(b, t) + 1)
                    pe.wait_ge(s_done, updates(b, t))
                pe.wait_ge(yd_done, ONE + (b * BT + t) * 2)
                for h in range(HEADS):
                    dst = y_ps[h % 2 * HD:(h % 2 + 1) * HD, h // 2 * P:(h // 2 + 1) * P]
                    mm = pe.matmul(dst, xdt[t % 2][:, h, :], mm_sb[t % 2][:, h, :], start=True, stop=(t == 0))
                    if t > 0:
                        mm = pe.matmul(dst, S[t % 2][:, h, :], cts[t % 2][:, h, :], start=False, stop=True)
                mm.then_inc(y_done, 1)

            def back(b, t):
                pe.wait_ge(yg_done, ONE + (b * BT + t) * 2 + 2)
                pe.wait_ge(oc_done, tiles(b, t))
                for j in range(HALVES):
                    pe.matmul(o_ps[:, 0:P], yv[t % 2][:, j, :], m.wout1[:, j, :], start=(j == 0), stop=(j == 1))
                pe.wait_ge(yq_done, tiles(b, t) + 1)
                for j in range(HALVES):
                    mm = pe.matmul(o_ps[:, P:P + 1], yq[t % 2][:, j, :], m.ones[:, 0:1], start=(j == 0), stop=(j == 1))
                mm.then_inc(o_done, 1)

            all_batches(pe, front, middle, back, now, ahead)

        @block.scalar
        def _(act):
            def projected(b, c, at):
                i, j = c * PIECES + at, ORDER[at]
                if at == 0:
                    act.wait_ge(conv_step, csteps(b, 0))
                act.wait_ge(proj_done, ONE + b * NPRE + i + 1)
                if j in CONV:
                    act.activation(raw[at][:, PAD + c * COL:PAD + (c + 1) * COL], pre[i % 2][:], ACT.Copy
                                   ).then_inc(proj_read, 1)
                else:
                    act.activation((xbc + sz)[j][:, col(c)], pre[i % 2][:], ACT.Silu,
                                   bias=m.cb1[:, j:j + 1] if j < NB else 0.0).then_inc(proj_read, 1)

            def convolved(b, c):
                for q, j in enumerate(CONV):
                    act.wait_ge(conv_step, csteps(b, c) + CSTEPS - 1 + q)
                    act.activation(xbc[j][:, col(c)], acc[q][:], ACT.Silu, bias=m.cb1[:, j:j + 1]
                                   ).then_inc(conv_read, 1)

            def now(b):
                act.wait_ge(yg_done, ONE + b * BT * 2)
                act.wait_ge(cts_done, updates(b, 0))
                for j in range(PIECES):
                    projected(b, 1, j)
                convolved(b, 1)

            def ahead(b, part):
                if part == 0:
                    act.wait_ge(dt_done, ONE + b + 1)
                    act.wait_ge(dtt_done, ONE + b)
                    for c in range(NCOL):
                        act.activation(dtT[:, col(c)], pre[c][0:HEADS, :], ACT.Identity, bias=m.dtb1[:]
                                       ).then_inc(dt_step, 1)
                    for at in range(len(CONV)):
                        projected(b, 0, at)
                    act.wait_ge(dt_step, ONE + b * 4 + 2)
                    act.activation(dte[:], dtT[:], ACT.Abs).then_inc(dt_step, 1)
                    act.wait_ge(dt_step, ONE + b * 4 + 3)
                    act.activation(dte[:], dte[:], ACT.Exp, scale=-1.0).then_inc(dt_step, 1)
                    act.wait_ge(dt_step, ONE + b * 4 + 4)
                    act.activation(dtl[:], dte[:], ACT.Ln, bias=1.0).then_inc(dtl_done, 1)
                    if not (isinstance(b, int) and b == 0):
                        act.wait_ge(yg_done, ONE + ((b - 1) * BT + BT // 2) * 2)
                        act.wait_ge(cts_done, ONE + (b - 1) * UPDATES + BT // 2 - 1)
                if part < 2:
                    for at in range(len(CONV) if part == 0 else PIECES // 2, (part + 1) * (PIECES // 2)):
                        projected(b, 0, at)
                if part == 1:
                    convolved(b, 0)

            def front(b, t):
                if t > 0:
                    act.wait_ge(seg_done, tiles(b, t) + 1)
                    act.wait_ge(cts_done, ONE + b * UPDATES + max(t - 2, 0))
                    act.wait_ge(s_done, upfreed(b, t))
                    act.activation(cdec[t % 2][:].rearrange("p h l -> p (h l)"), cs_ps[:], ACT.Exp
                                   ).then_inc(cdec_done, 1)
                if t < UPDATES:
                    act.wait_ge(last_done, updates(b, t) + 1)
                    act.wait_ge(xdd_done, updates(b, t))
                    act.activation(lastx[:], last[:], ACT.Exp).then_inc(lastx_done, 1)
                act.wait_ge(seg_done, tiles(b, t) + 1)
                act.wait_ge(m_done, freed(b, t))
                act.activation(dec[t % 2][:], seg[:], ACT.Exp).then_inc(dec_done, 1)
                if t < UPDATES:
                    act.wait_ge(xdt_done, tiles(b, t) + 1)
                    act.wait_ge(st_done, upfreed(b, t))
                    act.activation(bt[t % 2][:], tr_ps[:, 2 * P:3 * P], ACT.Copy).then_inc(bt_done, 1)

            def middle(b, t):
                act.wait_ge(yg_done, ONE + (b * BT + t) * 2 + 2)
                act.wait_ge(o_done, freed(b, t))
                act.activation(yq[t % 2][:], yv[t % 2][:], ACT.Square).then_inc(yq_done, 1)

            def back(b, t):
                act.wait_ge(o_done, tiles(b, t) + 1)
                if not isinstance(b, int):
                    act.sem_inc(m.passed, 1)
                act.activation(outs[:, bass.ds(b * BT + t, 1), :], o_ps[:, 0:P + 1].rearrange("p (o c) -> p o c", o=1),
                               ACT.Copy).then_inc(oc_done, 1)

            act.sem_inc(proj_read, 2)
            all_batches(act, front, middle, back, now, ahead)
            act.wait_ge(fin, ONE + 1)
            act.activation(ss[:], ss[:], ACT.Sqrt).then_inc(sq_done, 1)
            act.wait_ge(fin, ONE + 2)
            act.activation(var[:], var[:], ACT.Sqrt).then_inc(sq_done, 1)
            act.wait_ge(fin, ONE + 3)
            act.sem_inc(m.passed, 1)
            with act.Fori(0, NBATCH) as b:
                here = bass.ds(b * BT, BT)
                os, mean_b, var_b = outs[:, here, 0:P], mean[:, here], var[:, here]
                for i in range(BT):
                    one = slice(i, i + 1)
                    act.activation(os[:, one, :], os[:, one, :], ACT.Identity, bias=mean_b[:, one],
                                   scale=var_b[:, one]).then_inc(norm_done, 1)

        @block.gpsimd
        def _(pool):
            modulate(pool, m, 1, 0, modulated)
            for b in range(NBATCH):
                x = m.X[:, b * BT:(b + 1) * BT, :]
                pool.tensor_tensor(x, x, m.lnb_gate[:, b, :].unsqueeze(1).broadcast_to([P, BT, P]), ALU.add
                                   ).then_inc(added, 1)
            with pool.Fori(0, NBATCH) as b:
                for t in range(BT):
                    if t > 0:
                        pool.wait_ge(cdec_done, states(b, t) + 1)
                        pool.wait_ge(y_done, freed(b, t))
                        pool.tensor_tensor(cts[t % 2][:], cdec[t % 2][:], four(xbc[3][:, tok(t)]), ALU.mult
                                           ).then_inc(cts_done, 1)
                    pool.wait_ge(gm_done, tiles(b, t) + 1)
                    pool.wait_ge(dec_done, tiles(b, t) + 1)
                    pool.wait_ge(y_done, freed(b, t))
                    pool.tensor_tensor(mm_sb[t % 2][:], dec[t % 2][:], four(gm[t % 2][:]), ALU.mult
                                       ).then_inc(m_done, 1)

        @block.vector
        def _(dve):
            def convolve(b, c):
                dve.wait_ge(conv_read, ONE + (b * NCOL + c) * len(CONV))
                for k in range(TAPS):
                    for q, j in enumerate(CONV):
                        src, tap = raw[q][:, c * COL + k:c * COL + k + COL], m.tap1[:, j, k:k + 1]
                        if k == 0:
                            dve.wait_ge(proj_read, ONE + b * NPRE + 2 + c * PIECES + q + 1)
                            dve.tensor_scalar(acc[q][:], src, tap, None, ALU.mult).then_inc(conv_step, 1)
                        else:
                            dve.wait_ge(conv_step, csteps(b, c) + (k - 1) * 2 + q + 1)
                            dve.scalar_tensor_tensor(acc[q][:], src, tap, acc[q][:], ALU.mult, ALU.add
                                                     ).then_inc(conv_step, 1)

            def now(b):
                convolve(b, 1)

            def ahead(b, part):
                if part == 0:
                    convolve(b, 0)
                    dve.wait_ge(dt_step, ONE + b * 4 + 4)
                    dve.wait_ge(dtl_done, ONE + b + 1)
                    dve.scalar_tensor_tensor(dtT[:], dtT[:], 0.0, dtl[:], ALU.max, ALU.add).then_inc(dt_ready, 1)
                if part == 2:
                    dve.wait_ge(dtt_done, ONE + b + 1)
                    dve.tensor_copy(dt[:], pre[0][:, 0:BT * HEADS].rearrange("p (t h) -> p t h", h=HEADS)
                                    ).then_inc(dtt_read, 1)
                    dve.wait_ge(dtt_read, ONE + b + 1)
                    dve.tensor_tensor(dA[:], dt[:], m.negA1[:].unsqueeze(1).broadcast_to([P, BT, HEADS]),
                                      ALU.mult).then_inc(dA_done, 1)

            def front(b, t):
                cs = cs_ps[:].rearrange("p (h l) -> p h l", h=HEADS)
                dve.wait_ge(cs_done, tiles(b, t) + 1)
                dve.tensor_copy(csc[:], g_ps[:, P:P + HEADS]).then_inc(csc_done, 1)
                dve.wait_ge(csc_done, tiles(b, t) + 1)
                if t < UPDATES:
                    dve.wait_ge(lastx_done, updates(b, t))
                    dve.tensor_tensor(last[:], cs[:, :, P - 1], csc[:], ALU.subtract).then_inc(last_done, 1)
                dve.wait_ge(dec_done, tiles(b, t))
                for h in range(HEADS):
                    ins = dve.tensor_scalar(seg[:, h, :], cs[:, h, :], csc[:, h:h + 1], 0.0, ALU.subtract, ALU.min)
                ins.then_inc(seg_done, 1)
                dve.wait_ge(m_done, freed(b, t))
                dve.tensor_tensor(gm[t % 2][:], g_ps[:, 0:P], m.tri[:], ALU.mult).then_inc(gm_done, 1)
                dve.wait_ge(tr_done, tiles(b, t) + 1)
                dve.wait_ge(y_done, freed(b, t))
                xv = tr_ps[:, 0:D_IN].rearrange("p (h d) -> p h d", h=HEADS)
                dve.tensor_tensor(xdt[t % 2][:], xv, spread(dt[:, t, :]), ALU.mult).then_inc(xdt_done, 1)
                if t < UPDATES:
                    dve.wait_ge(xdt_done, tiles(b, t) + 1)
                    dve.wait_ge(lastx_done, updates(b, t) + 1)
                    dve.wait_ge(st_done, upfreed(b, t))
                    dve.tensor_tensor(xdd[t % 2][:], xdt[t % 2][:], spread(lastx[:]), ALU.mult).then_inc(xdd_done, 1)

            def middle(b, t):
                old, new = S[t % 2], S[1 - t % 2]
                if t < UPDATES:
                    added = st_ps[:, 0:D_IN].rearrange("p (h d) -> p h d", h=HEADS)
                    dve.wait_ge(y_done, tiles(b, t))
                    if t == 0:
                        dve.wait_ge(st_done, updates(b, t) + 1)
                        dve.tensor_copy(new[:], added).then_inc(s_done, 1)
                    else:
                        dve.wait_ge(cdec_done, states(b, t) + 1)
                        dve.wait_ge(s_done, updates(b, t))
                        dve.tensor_tensor(new[:], old[:], spread(cdec[t % 2][:, :, P - 1]), ALU.mult
                                          ).then_inc(s_step, 1)
                        dve.wait_ge(s_step, ONE + b * (UPDATES - 1) + t)
                        dve.wait_ge(st_done, updates(b, t) + 1)
                        dve.tensor_tensor(new[:], new[:], added, ALU.add).then_inc(s_done, 1)
                T = b * BT + t
                dve.wait_ge(y_done, tiles(b, t) + 1)
                dve.wait_ge(o_done, freed(b, t))
                dve.wait_ge(yq_done, freed(b, t))
                y = yv[t % 2]
                for j in range(HALVES):
                    dve.scalar_tensor_tensor(y[:, j, :], xbc[j][:, tok(t)], m.d1[:, j:j + 1],
                                             y_ps[:, j * P:(j + 1) * P], ALU.mult, ALU.add).then_inc(yd_done, 1)
                for j in range(HALVES):
                    dve.wait_ge(yd_done, ONE + T * 2 + j + 1)
                    dve.tensor_tensor(y[:, j, :], y[:, j, :], sz[j][:, tok(t)], ALU.mult).then_inc(yg_done, 1)

            def back(b, t):
                pass

            for q in range(2):
                dve.memset(raw[q][:, 0:PAD], 0.0).then_inc(conv_step, 1)
            dve.wait_ge(conv_step, ONE + 2)
            all_batches(dve, front, middle, back, now, ahead)
            chain = [0]

            def then(ins):
                chain[0] += 1
                ins.then_inc(tail_step, 1)
                dve.wait_ge(tail_step, ONE + chain[0])

            dve.wait_ge(oc_done, ONE + TILES)
            dve.wait_ge(added, ONE + NBATCH)
            dve.wait_ge(modulated, 2 * NBATCH)
            then(dve.tensor_scalar(ss[:], outs[:, :, P], 1.0 / D_IN, EPS, ALU.mult, ALU.add))
            dve.sem_inc(fin, 1)
            dve.wait_ge(sq_done, ONE + 1)
            then(dve.reciprocal(ss[:], ss[:]))
            with dve.Fori(0, NBATCH) as b:
                here = bass.ds(b * BT, BT)
                os, rs, ss_b, stats_b = outs[:, here, 0:P], m.rows[:, here, :], ss[:, here], stats[:, here, :]
                for i in range(BT):
                    one = slice(i, i + 1)
                    dve.scalar_tensor_tensor(os[:, one, :], os[:, one, :], ss_b[:, one], rs[:, one, :],
                                             ALU.mult, ALU.add).then_inc(h_step, 1)
                dve.wait_ge(h_step, ONE + b * 2 * BT + BT)
                dve.sem_inc(m.passed, 1)
                for i in range(BT):
                    dve.bn_stats(stats_b[:, i:i + 1, :], os[:, i:i + 1, :]).then_inc(h_step, 1)
            dve.wait_ge(h_step, ONE + 2 * TILES)
            then(dve.tensor_tensor(tmp[:], stats[:, :, 1], stats[:, :, 4], ALU.subtract))
            then(dve.tensor_tensor(mean[:], stats[:, :, 1], stats[:, :, 4], ALU.add))
            then(dve.tensor_scalar(mean[:], mean[:], -0.5, None, ALU.mult))
            then(dve.tensor_tensor(var[:], stats[:, :, 2], stats[:, :, 5], ALU.add))
            then(dve.scalar_tensor_tensor(tmp[:], tmp[:], 0.25, tmp[:], ALU.mult, ALU.mult))
            then(dve.scalar_tensor_tensor(var[:], var[:], 1.0 / P, tmp[:], ALU.mult, ALU.add))
            then(dve.tensor_scalar(var[:], var[:], EPS, None, ALU.add))
            dve.sem_inc(fin, 1)
            dve.wait_ge(sq_done, ONE + 2)
            then(dve.reciprocal(var[:], var[:]))
            then(dve.tensor_tensor(mean[:], mean[:], var[:], ALU.mult))
            dve.sem_inc(fin, 1)
            with dve.Fori(0, NBATCH) as b:
                here = bass.ds(b * BT, BT)
                o = outs[:, here, 0:P]
                dve.wait_ge(norm_done, ONE + b * BT + BT)
                dve.sem_inc(m.passed, 1)
                dve.tensor_tensor(o, o, m.lng_gate[:, bass.ds(b, 1), :].broadcast_to([P, BT, P]), ALU.mult
                                  ).then_inc(h_step, 1)
                dve.wait_ge(h_step, ONE + 2 * TILES + b * 2 + 1)
                dve.sem_inc(m.passed, 1)
                xs, stats_b = m.X[:, here, :], m.stats[:, here, :]
                dve.tensor_tensor(xs, xs, o, ALU.add).then_inc(h_step, 1)
                dve.wait_ge(h_step, ONE + 2 * TILES + b * 2 + 2)
                dve.sem_inc(m.passed, 1)
                for t in range(BT):
                    dve.bn_stats(stats_b[:, t:t + 1, :], xs[:, t:t + 1, :])


def build(nc, a, out):
    with ExitStack() as ctx:
        sb = lambda name, shape, dt=F32: ctx.enter_context(nc.sbuf_tensor(name, shape, dt))
        m = Memory()
        m.X = sb("X", [P, TILES, P])
        m.stats = sb("stats", [P, TILES, 6])
        m.hT = sb("hT", [P, NBATCH, PAD + SEQ])
        m.ident = sb("ident", [P, P])
        m.tri = sb("tri", [P, P])
        m.ones = sb("ones", [P, P])
        m.before = sb("before", [P, P])
        m.zeros = sb("zeros", [P, P])
        m.count = sb("count", [P, max(SLOTS)])
        m.count128 = sb("count128", [P, TILES])
        m.where = sb("where", [P, 2, TILES], mybir.dt.uint32)
        m.weight = sb("weight", [P, 2, TILES])
        m.owner = sb("owner", [1, max(SLOTS)], mybir.dt.int32)
        m.scale_row = sb("scale_row", [P, len(ROW_NORMS), NBATCH, P])
        m.shift_row = sb("shift_row", [P, len(ROW_NORMS), NBATCH, P])
        m.shift = sb("shift", [P, 2, 2, NBATCH])
        m.scale = sb("scale", [P, 2, 2, NBATCH])
        m.gate = sb("gate", [P, 2, 2, NBATCH, P])
        m.wc1 = sb("wc1", [P, TAPS, D_IN])
        m.win1 = sb("win1", [P, COL])
        m.tap1 = sb("tap1", [P, COL // P, TAPS])
        m.wz1 = sb("wz1", [P, D_IN])
        m.wdt1 = sb("wdt1", [P, HEADS])
        m.cb1 = sb("cb1", [P, COL // P])
        m.dtb1 = sb("dtb1", [HEADS, 1])
        m.negA1 = sb("negA1", [P, HEADS])
        m.d1 = sb("d1", [P, HALVES])
        m.wout1 = sb("wout1", [P, HALVES, P])
        m.lng_gate = sb("lng_gate", [P, NBATCH, P])
        m.lnb_gate = sb("lnb_gate", [P, NBATCH, P])
        m.gate1 = sb("gate1", [P, NE])
        m.gb1 = sb("gb1", [P, 2, NE])
        m.xs = [nc.dram_tensor(f"xs{layer}", (SLOTS[layer] * P, P), F32).ap() for layer in range(2)]
        m.ys = [nc.dram_tensor(f"ys{layer}", (SLOTS[layer] * P, P), F32).ap() for layer in range(2)]
        m.out = out
        m.kept = ctx
        m.passed = ctx.enter_context(nc.semaphore("passed"))
        m.late = ctx.enter_context(nc.semaphore("late"))
        m.cleared = ctx.enter_context(nc.semaphore("cleared"))
        layer0 = ctx.enter_context(ExitStack())
        sb0 = lambda name, shape, dt=F32: layer0.enter_context(nc.sbuf_tensor(name, shape, dt))
        m.pick = sb0("pick", [3 * 2 * N0, 2 * N0 * P], BF16)
        m.wc0 = sb0("wc0", [P, TAPS, D_IN])
        m.wz0 = sb0("wz0", [P, D_IN])
        m.cb0 = sb0("cb0", [P, HALVES])
        m.wx = sb0("wx", [P, HALVES, RANK + 6 * N0])
        m.wdt0 = sb0("wdt0", [RANK, D_IN])
        m.bdt0 = sb0("bdt0", [P, HALVES])
        m.negA0 = sb0("negA0", [P, HALVES, N0])
        m.diagD0 = sb0("diagD0", [P, HALVES, P])
        m.wo0 = sb0("wo0", [P, HALVES, P])
        m.router = sb0("router", [P, NE])
        m.sems = {}
        for tag, names in (("ma_", MAMBA_SEMS), ("ss_", SSD_SEMS), ("so_", SORTED_SEMS)):
            for name in names.split():
                m.sems[tag + name] = ctx.enter_context(nc.semaphore(tag + name))
        setup(nc, a, m)
        mamba(nc, m)
        m.wgu = sb0("wgu", [P, NE, 2 * F0])
        m.wdown = sb0("wdown", [P, NE, F0 // P, P])
        late = lambda name, shape: ctx.enter_context(nc.sbuf_tensor(name, shape, F32, side="right"))
        m.rows = late("rows", [P, TILES, P])
        for layer in range(2):
            if layer == 1:
                ssd(nc, m)
                m.w1 = late("w1", [P, NE, F1])
                m.w2 = late("w2", [P, NE, F1 // P, P])
            with nc.psum_tensor(f"logits{layer}", [P, COL], F32) as m.logits:
                norm_for_experts(nc, a, m, layer)
                if layer == 1:
                    m.b1 = late("b1", [P, NE * F1])
                    m.b2 = late("b2", [P, NE * P])
                route(nc, a, m, layer)
            sorted_experts(nc, m, layer)
            combine(nc, m, layer)
            if layer == 0:
                layer0.close()


def kernel(**inputs):
    import numpy as np
    import concourse.bacc as bacc
    from concourse.bass_utils import run_bass_kernel_spmd

    def laid(name, f=lambda v: v):
        return np.ascontiguousarray(f(np.asarray(inputs[name])))

    T = lambda v: v.T
    last2 = lambda v: v.transpose(0, 2, 1)
    three = lambda v: np.concatenate([v.T[:, :RANK]] + 3 * [v.T[:, RANK:]], axis=1)
    arrays = {
        "L0_cT": laid("L0_c", T), "L1_cT": laid("L1_c", T), "L0_wmod": laid("L0_wmod"), "L1_wmod": laid("L1_wmod"),
        "L0_attn_x": laid("L0_attn_x"), "L0_WiT": laid("L0_attn_Wi", T),
        "L0_conv_row": laid("L0_attn_conv_w", lambda v: v[:, 0, :].T), "L0_WxT": laid("L0_attn_Wx", three),
        "L0_WdtT": laid("L0_attn_Wdt", T), "L0_WoT": laid("L0_attn_Wo", T),
        "L1_conv_row": laid("L1_attn_conv_w", T),
        "router_T": laid("L0_ffn_router_w", T), "w_gate_T": laid("L0_ffn_w_gate", last2),
        "w_up_T": laid("L0_ffn_w_up", last2), "w_down_T": laid("L0_ffn_w_down", last2),
        "gate_T": laid("L1_ffn_gate_w", T),
    }
    arrays["tap1"] = laid("L1_attn_conv_w", lambda v: v.reshape(-1, P, TAPS).transpose(1, 0, 2))
    for short, name in (("cb0", "L0_attn_conv_b"), ("bdt0", "L0_attn_bdt"), ("dp0", "L0_attn_Dp"),
                        ("cb1", "L1_attn_conv_b"), ("rms", "L1_attn_rms_w")):
        arrays[short] = laid(name, lambda v: v.reshape(-1, P).T)
    arrays["L1_ffn_b1"] = laid("L1_ffn_b1", lambda v: v.reshape(-1))
    for name in ("L0_attn_A_log L1_attn_W_in L1_attn_dt_bias L1_attn_A_log L1_attn_D L1_attn_W_out L1_attn_ln_g "
                 "L1_attn_ln_b L1_ffn_gate_b L1_ffn_expert_bias L1_ffn_w1 L1_ffn_w2").split():
        arrays[name] = laid(name)
    arrays["L1_ffn_b2"] = laid("L1_ffn_b2", lambda v: v.reshape(-1))
    arrays["ident"] = np.eye(P, dtype=np.float32)
    arrays["tri"] = np.triu(np.ones((P, P), np.float32))
    arrays["before"] = np.triu(np.ones((P, P), np.float32), 1)
    arrays["count"] = np.arange(max(SLOTS), dtype=np.float32)
    pick = np.zeros((3, 2 * N0, 2 * N0, P), mybir.dt.np(BF16))
    for n in range(2 * N0):
        pick[:, n, n, :] = 1.0
    arrays["pick"] = pick.reshape(3 * 2 * N0, 2 * N0 * P)

    nc = bacc.Bacc("TRN2", target_bir_lowering=False, num_devices=1)
    aps = {}
    for name, v in arrays.items():
        aps[name] = nc.dram_tensor("in_" + name, v.shape, mybir.dt.from_np(v.dtype), kind="ExternalInput").ap()
    out = nc.dram_tensor("out", (NBATCH, SEQ, P), F32, kind="ExternalOutput").ap()
    build(nc, aps, out)
    r = run_bass_kernel_spmd(nc, [{"in_" + k: v for k, v in arrays.items()}], core_ids=[0])
    return r.results[0]["out"]
```
